# Optimizing a Trainium2 kernel written in Bass

```python
import numpy as np
import jax
import jax.numpy as jnp

def _softmax(x, axis=-1):
    return jax.nn.softmax(x, axis=axis)

def _gelu(x):
    return jax.nn.gelu(x, approximate=True)

def _silu(x):
    return jax.nn.silu(x)

def _sigmoid(x):
    return jax.nn.sigmoid(x)

def _layernorm(x, axis=-1, eps=1e-05):
    m = jnp.mean(x, axis=axis, keepdims=True)
    v = jnp.var(x, axis=axis, keepdims=True)
    return (x - m) / jnp.sqrt(v + eps)

def _scatter_add(tgt, idx, src, axis=0):
    return tgt.at[idx].add(src)

def _segment_sum(src, seg, n):
    return jax.ops.segment_sum(src, seg, n)
kernel_name = 'mk_perceiver_d1_seqx_r2_1553c7'

def setup_inputs(seed: int=0):
    np.random.seed(seed)
    _w = jnp.asarray

    def _rec_inputs():
        import jax
        import jax.numpy as jnp
        _rk = jax.random.key(seed)
        x = -0.0002928 + 1 * jax.random.normal(jax.random.fold_in(_rk, 1), (2, 512, 512), jnp.float32)
        _lenS = 512 - jax.random.randint(jax.random.fold_in(_rk, 7), (2,), 0, max(1, 512 // 4) + 1, jnp.int32)
        _lenS2 = 8192 - jax.random.randint(jax.random.fold_in(_rk, 8), (2,), 0, max(1, 8192 // 4) + 1, jnp.int32)
        _ctx_1024P = jax.random.normal(jax.random.fold_in(_rk, 11), (2, 16, 512), jnp.float32)
        _ctx_1024c = jax.random.dirichlet(jax.random.fold_in(_rk, 511), 0.3 * jnp.ones((16,), jnp.float32), (2, 8192))
        _ctx_1024t = jnp.einsum('bsk,bkd->bsd', _ctx_1024c, _ctx_1024P)
        _ctx_1024t = _ctx_1024t * jax.lax.rsqrt(jnp.mean(jnp.square(_ctx_1024t)) + 1e-12) * 0.953939
        ctx_1024 = 4.13588e-05 + 0.999923 * (_ctx_1024t + 0.3 * jax.random.normal(jax.random.fold_in(_rk, 611), (2, 8192, 512), jnp.float32))
        return (x, ctx_1024)
    x, ctx_1024 = _rec_inputs()

    def _L0_xattn_setup():
        import jax, jax.numpy as jnp
        import numpy as np
        EMBED_DIM = 512
        NUM_HEADS = 16
        HEAD_DIM = EMBED_DIM // NUM_HEADS
        key = jax.random.key(seed)
        ks = jax.random.split(key, 11)
        B, Q, K = (4, 512, 1024)
        s = 1.0 / np.sqrt(EMBED_DIM)
        return {'query': jax.random.normal(ks[0], (B, Q, EMBED_DIM), jnp.float32), 'key': jax.random.normal(ks[1], (B, K, EMBED_DIM), jnp.float32), 'value': jax.random.normal(ks[2], (B, K, EMBED_DIM), jnp.float32), 'Wq': jax.random.normal(ks[3], (EMBED_DIM, EMBED_DIM), jnp.float32) * s, 'bq': jnp.zeros((EMBED_DIM,), jnp.float32), 'Wk': jax.random.normal(ks[4], (EMBED_DIM, EMBED_DIM), jnp.float32) * s, 'bk': jnp.zeros((EMBED_DIM,), jnp.float32), 'Wv': jax.random.normal(ks[5], (EMBED_DIM, EMBED_DIM), jnp.float32) * s, 'bv': jnp.zeros((EMBED_DIM,), jnp.float32), 'Wo': jax.random.normal(ks[6], (EMBED_DIM, EMBED_DIM), jnp.float32) * s, 'bo': jnp.zeros((EMBED_DIM,), jnp.float32)}
    _L0_xattn_all = _L0_xattn_setup()
    _L0_xattn_in = {k: v for k, v in _L0_xattn_all.items() if k in ('Wq', 'bq', 'Wk', 'bk', 'Wv', 'bv', 'Wo', 'bo')}
    del _L0_xattn_all

    def _L0_attn_setup():
        import jax, jax.numpy as jnp
        import numpy as np
        SEQLEN, K, OLDK, HEADS = (1024, 512, 512, 16)
        BASE = 10000.0

        def rope(x):
            t = x.shape[1]
            half = K // 2
            theta = 1.0 / BASE ** (jnp.arange(half, dtype=jnp.float32) / half)
            ang = jnp.arange(t, dtype=jnp.float32)[:, None] * theta[None, :]
            cos, sin = (jnp.cos(ang), jnp.sin(ang))
            xr = x.reshape(x.shape[0], t, half, 2)
            xe, xo = (xr[..., 0], xr[..., 1])
            re = xe * cos - xo * sin
            im = xe * sin + xo * cos
            return jnp.stack([re, im], axis=-1).reshape(x.shape)
        key = jax.random.key(seed)
        ks = jax.random.split(key, 5)
        b = 4
        x = jax.random.normal(ks[0], (b, SEQLEN, OLDK), jnp.float32)
        sc_in = 1.0 / np.sqrt(OLDK).astype(np.float32)
        Wq = jax.random.normal(ks[1], (K, OLDK), jnp.float32) * sc_in
        Wk = jax.random.normal(ks[2], (K, OLDK), jnp.float32) * sc_in
        Wv = jax.random.normal(ks[3], (K, OLDK), jnp.float32) * sc_in
        Wu = jax.random.normal(ks[4], (K, K), jnp.float32) * (1.0 / np.sqrt(K).astype(np.float32))
        bu = jnp.zeros((K,), jnp.float32)
        return {'x': x, 'Wq': Wq, 'Wk': Wk, 'Wv': Wv, 'Wu': Wu, 'bu': bu}
    _L0_attn_all = _L0_attn_setup()
    _L0_attn_in = {k: v for k, v in _L0_attn_all.items() if k in ('Wq', 'Wk', 'Wv', 'Wu', 'bu')}
    del _L0_attn_all

    def _L0_ffn_setup():
        import jax, jax.numpy as jnp
        import numpy as np
        B, S, H, E = (4, 1024, 512, 8)
        key = jax.random.key(seed)
        k1, k2, k3 = jax.random.split(key, 3)
        scale_w = 1.0 / np.sqrt(H)
        return {'x': jax.random.normal(k1, (B, S, H), dtype=jnp.float32), 'router_w': jax.random.normal(k2, (H, E), dtype=jnp.float32) * scale_w, 'router_b': jnp.zeros((E,), dtype=jnp.float32), 'expert_w': jax.random.normal(k3, (E, H, H), dtype=jnp.float32) * scale_w, 'expert_b': jnp.zeros((E, H), dtype=jnp.float32)}
    _L0_ffn_all = _L0_ffn_setup()
    _L0_ffn_in = {k: v for k, v in _L0_ffn_all.items() if k in ('router_w', 'router_b', 'expert_w', 'expert_b')}
    del _L0_ffn_all
    return {'x': x, 'ctx_1024': ctx_1024, 'L0_xattn_Wq': _L0_xattn_in['Wq'], 'L0_xattn_bq': _L0_xattn_in['bq'], 'L0_xattn_Wk': _L0_xattn_in['Wk'], 'L0_xattn_bk': _L0_xattn_in['bk'], 'L0_xattn_Wv': _L0_xattn_in['Wv'], 'L0_xattn_bv': _L0_xattn_in['bv'], 'L0_xattn_Wo': _L0_xattn_in['Wo'], 'L0_xattn_bo': _L0_xattn_in['bo'], 'L0_attn_Wq': _L0_attn_in['Wq'], 'L0_attn_Wk': _L0_attn_in['Wk'], 'L0_attn_Wv': _L0_attn_in['Wv'], 'L0_attn_Wu': _L0_attn_in['Wu'], 'L0_attn_bu': _L0_attn_in['bu'], 'L0_ffn_router_w': _L0_ffn_in['router_w'], 'L0_ffn_router_b': _L0_ffn_in['router_b'], 'L0_ffn_expert_w': _L0_ffn_in['expert_w'], 'L0_ffn_expert_b': _L0_ffn_in['expert_b']}

def reference(x, ctx_1024, L0_xattn_Wq, L0_xattn_bq, L0_xattn_Wk, L0_xattn_bk, L0_xattn_Wv, L0_xattn_bv, L0_xattn_Wo, L0_xattn_bo, L0_attn_Wq, L0_attn_Wk, L0_attn_Wv, L0_attn_Wu, L0_attn_bu, L0_ffn_router_w, L0_ffn_router_b, L0_ffn_expert_w, L0_ffn_expert_b):
    import jax
    import jax.numpy as jnp

    def _L0_xattn_ref(query, key, value, Wq, bq, Wk, bk, Wv, bv, Wo, bo):
        import jax, jax.numpy as jnp
        import numpy as np
        EMBED_DIM = 512
        NUM_HEADS = 16
        HEAD_DIM = EMBED_DIM // NUM_HEADS
        B = query.shape[0]
        q = query @ Wq.T + bq
        k = key @ Wk.T + bk
        v = value @ Wv.T + bv
        q = q.reshape(B, -1, NUM_HEADS, HEAD_DIM)
        k = k.reshape(B, -1, NUM_HEADS, HEAD_DIM)
        v = v.reshape(B, -1, NUM_HEADS, HEAD_DIM)
        scores = jnp.einsum('bqhd,bkhd->bhqk', q, k) / np.sqrt(HEAD_DIM).astype(np.float32)
        probs = jax.nn.softmax(scores, axis=-1)
        out = jnp.einsum('bhqk,bkhd->bqhd', probs, v)
        out = out.reshape(B, -1, EMBED_DIM)
        return out @ Wo.T + bo

    def _L0_attn_ref(x, Wq, Wk, Wv, Wu, bu):
        import jax, jax.numpy as jnp
        import numpy as np
        SEQLEN, K, OLDK, HEADS = (1024, 512, 512, 16)
        BASE = 10000.0

        def rope(x):
            t = x.shape[1]
            half = K // 2
            theta = 1.0 / BASE ** (jnp.arange(half, dtype=jnp.float32) / half)
            ang = jnp.arange(t, dtype=jnp.float32)[:, None] * theta[None, :]
            cos, sin = (jnp.cos(ang), jnp.sin(ang))
            xr = x.reshape(x.shape[0], t, half, 2)
            xe, xo = (xr[..., 0], xr[..., 1])
            re = xe * cos - xo * sin
            im = xe * sin + xo * cos
            return jnp.stack([re, im], axis=-1).reshape(x.shape)
        b, t, _ = x.shape
        h = HEADS
        s = K // h
        q = rope(x @ Wq.T)
        k = rope(x @ Wk.T)
        v = x @ Wv.T
        q = q.reshape(b, t, h, s).transpose(0, 2, 1, 3)
        k = k.reshape(b, t, h, s).transpose(0, 2, 1, 3)
        v = v.reshape(b, t, h, s).transpose(0, 2, 1, 3)
        dot = jnp.einsum('bhqd,bhkd->bhqk', q, k) / jnp.sqrt(jnp.float32(s))
        att = jax.nn.softmax(dot, axis=-1)
        out = jnp.einsum('bhqk,bhkd->bhqd', att, v)
        out = out.transpose(0, 2, 1, 3).reshape(b, t, h * s)
        return out @ Wu.T + bu

    def _L0_ffn_ref(x, router_w, router_b, expert_w, expert_b):
        import jax, jax.numpy as jnp
        import numpy as np
        B, S, H, E = (4, 1024, 512, 8)
        b, s, h = x.shape
        xt = x.reshape(b * s, h)
        logits = xt @ router_w + router_b
        probs = jax.nn.softmax(logits, axis=-1)
        gate = jnp.max(probs, axis=-1)
        idx = jnp.argmax(probs, axis=-1)
        out_all = jnp.einsum('th,ehd->ted', xt, expert_w) + expert_b[None, :, :]
        e_out = jnp.take_along_axis(out_all, idx[:, None, None], axis=1)[:, 0, :]
        y = gate[:, None] * e_out
        return y.reshape(b, s, h)
    x = x + _L0_xattn_ref(_layernorm(x, axis=-1), ctx_1024, ctx_1024, L0_xattn_Wq, L0_xattn_bq, L0_xattn_Wk, L0_xattn_bk, L0_xattn_Wv, L0_xattn_bv, L0_xattn_Wo, L0_xattn_bo)
    x = x + _L0_attn_ref(_layernorm(x, axis=-1), L0_attn_Wq, L0_attn_Wk, L0_attn_Wv, L0_attn_Wu, L0_attn_bu)
    x = x + _L0_ffn_ref(_layernorm(x, axis=-1), L0_ffn_router_w, L0_ffn_router_b, L0_ffn_expert_w, L0_ffn_expert_b)
    return x

_drawn_inputs = setup_inputs


def setup_inputs(seed=0):
    import zlib

    import numpy as np

    out = dict(_drawn_inputs(seed))
    spreads = {'L0_xattn_bq': (0.0, 0.1),
     'L0_xattn_bk': (0.0, 0.8),
     'L0_xattn_bv': (0.0, 0.1),
     'L0_xattn_bo': (0.0, 0.1),
     'L0_attn_bu': (0.0, 0.1),
     'L0_ffn_router_b': (0.0, 0.1),
     'L0_ffn_expert_b': (0.0, 0.287)}
    factors = {}
    for name, (base, spread) in spreads.items():
        noise = np.random.default_rng([zlib.crc32(name.encode()), seed]).standard_normal(out[name].shape)
        drawn = base * np.exp(spread * noise) if base else spread * noise
        out[name] = jnp.asarray(drawn.astype(out[name].dtype))
    for name, factor in factors.items():
        out[name] = (out[name] * factor).astype(out[name].dtype)
    return out
```

```python
from contextlib import ExitStack

import concourse.bass as bass
from concourse import mybir

F32 = mybir.dt.float32
F32R = mybir.dt.float32r
ALU = mybir.AluOpType
ACT = mybir.ActivationFunctionType
AX_X = mybir.AxisListType.X

P = 128
B = 2
T = 512
D = 512
DT = D // P
H = 16
HD = D // H
HG = P // HD
G = H // HG
KC = 512
KT = KC // P
TT = T // P
SCALE = float(HD) ** -0.5
EPS = 1e-5
STACK = 3 * HD
NT = B * TT
E = 8
ROWS = STACK + HG
BIG = 1e30


def fp(ap):
    return ap.bitcast(F32)


class Norm:

    def __init__(self, nc, ctx, tag, x, ident):
        sb = lambda name, shape, dt=F32: ctx.enter_context(nc.sbuf_tensor(f"{tag}_{name}", shape, dt))
        sem = lambda name: ctx.enter_context(nc.semaphore(f"{tag}_{name}"))
        self.x, self.ident = x, ident
        self.ps = ctx.enter_context(nc.psum_tensor(f"{tag}_ps_turn", [P, 2, 512], F32))
        self.xn = sb("xn", [P, NT, D])
        self.hi, self.lo = sb("nh", [P, DT, B * T], F32R), sb("nl", [P, DT, B * T], F32R)
        self.stats, self.mv, self.var = sb("stats", [P, NT, 6]), sb("mv", [P, NT, 2]), sb("var", [P, NT])
        self.std, self.rstd, self.work = sb("std", [P, NT]), sb("rstd", [P, NT]), sb("work", [P, NT])
        self.vector_steps, self.std_done, self.xn_done = sem("vector_steps"), sem("std_done"), sem("xn_done")
        self.turned, self.hi_done, self.lo_done = sem("turned"), sem("hi_done"), sem("lo_done")

    def vector_1_stats(self, dve, i):
        dve.bn_stats(self.stats[:, i, :], self.x[:, i, :]).then_inc(self.vector_steps, 1)

    def vector_2_variance(self, dve):
        for i in range(NT):
            dve.wait_ge(self.vector_steps, NT + i)
            dve.bn_aggr(self.mv[:, i, :], self.stats[:, i, :]).then_inc(self.vector_steps, 1)
        dve.wait_ge(self.vector_steps, 2 * NT)
        dve.tensor_scalar(self.var[:], self.mv[:, :, 1], EPS, None, ALU.add).then_inc(self.vector_steps, 1)

    def scalar_3_root(self, act):
        act.wait_ge(self.vector_steps, 2 * NT + 1)
        act.activation(self.std[:], self.var[:], ACT.Sqrt).then_inc(self.std_done, 1)

    def vector_4_apply(self, dve):
        y, w, step = self.rstd, self.work, self.vector_steps
        dve.wait_ge(self.std_done, 1)
        dve.reciprocal(y[:], self.std[:]).then_inc(step, 1)
        dve.wait_ge(step, 2 * NT + 2)
        dve.tensor_tensor(w[:], y[:], y[:], ALU.mult).then_inc(step, 1)
        dve.wait_ge(step, 2 * NT + 3)
        dve.tensor_tensor(w[:], w[:], self.var[:], ALU.mult).then_inc(step, 1)
        dve.wait_ge(step, 2 * NT + 4)
        dve.tensor_scalar(w[:], w[:], -0.5, 1.5, ALU.mult, ALU.add).then_inc(step, 1)
        dve.wait_ge(step, 2 * NT + 5)
        dve.tensor_tensor(y[:], y[:], w[:], ALU.mult).then_inc(step, 1)
        dve.wait_ge(step, 2 * NT + 6)
        for i in range(NT):
            dve.tensor_scalar(self.xn[:, i, :], self.x[:, i, :], self.mv[:, i, 0:1], y[:, i:i + 1],
                              ALU.subtract, ALU.mult).then_inc(self.xn_done, 1)

    def tensor_5_turn(self, pe):
        for k in range(B * DT):
            b, d = k // DT, k % DT
            pe.wait_ge(self.xn_done, TT * (b + 1))
            if k >= 2:
                pe.wait_ge(self.lo_done, k - 1)
            for t in range(TT):
                mm = pe.transpose(self.ps[:, k % 2, t * P:(t + 1) * P],
                                  self.xn[:, b * TT + t, d * P:(d + 1) * P], self.ident[:])
            mm.then_inc(self.turned, 1)

    def _tokens(self, k):
        return slice((k // DT) * T, (k // DT + 1) * T)

    def scalar_6_hi(self, act):
        for k in range(B * DT):
            act.wait_ge(self.turned, k + 1)
            act.activation(self.hi[:, k % DT, self._tokens(k)], self.ps[:, k % 2, :], ACT.Copy).then_inc(self.hi_done, 1)

    def vector_7_lo(self, dve):
        for k in range(B * DT):
            dve.wait_ge(self.hi_done, k + 1)
            s = self._tokens(k)
            dve.tensor_tensor(self.lo[:, k % DT, s], self.ps[:, k % 2, :], fp(self.hi[:, k % DT, s]),
                              ALU.subtract).then_inc(self.lo_done, 1)


def exact_product(pe, out, left, right):
    for n, (lp, rp) in enumerate(((0, 0), (0, 1), (1, 0))):
        for d in range(DT):
            mm = pe.matmul(out, left(lp, d), right(rp, d), start=(n == 0 and d == 0), stop=(n == 2 and d == DT - 1))
    return mm


def project_queries(nc, x, wq, bq, ident, q_split):
    with ExitStack() as ctx:
        sb = lambda name, shape, dt=F32: ctx.enter_context(nc.sbuf_tensor(name, shape, dt))
        sem = lambda name: ctx.enter_context(nc.semaphore(name))
        ps_q = ctx.enter_context(nc.psum_tensor("a_ps_q", [P, 2, 512], F32))
        xs, idn, bias = sb("a_x", [P, NT, D]), sb("a_id", [P, P]), sb("a_b", [P, DT])
        w, wh, wl = sb("a_w", [P, DT, D]), sb("a_wh", [P, DT, D], F32R), sb("a_wl", [P, DT, D], F32R)
        qh, ql = sb("a_qh", [P, 2, T], F32R), sb("a_ql", [P, 2, T], F32R)
        norm = Norm(nc, ctx, "a", xs, idn)
        w_in, c_in = sem("a_w_in"), sem("a_c_in")
        x_in = [sem("a_x_in0"), sem("a_x_in1")]
        wh_done, wl_done = sem("a_wh_done"), sem("a_wl_done")
        q_mm, qh_done, ql_done = sem("a_q_mm"), sem("a_qh_done"), sem("a_ql_done")
        q_stored = [sem("a_q_stored0"), sem("a_q_stored1")]
        block = ctx.enter_context(nc.Block())

        @block.sync
        def _(sp):
            for b in range(B):
                sp.dma_start(xs[:, TT * b:TT * (b + 1), :], x[b].rearrange("(t p) d -> p t d", p=P)).then_inc(x_in[b], 16)
            sp.dma_start(w[:], wq).then_inc(w_in, 16)
            sp.dma_start(idn[:], ident).then_inc(c_in, 16)
            sp.dma_start(bias[:], bq).then_inc(c_in, 16)
            for m in range(B * G):
                sp.wait_ge(qh_done, m + 1)
                sp.dma_start(q_split[m // G, 0, m % G], fp(qh[:, m % 2, :])).then_inc(q_stored[m % 2], 16)
                sp.wait_ge(ql_done, m + 1)
                sp.dma_start(q_split[m // G, 1, m % G], fp(ql[:, m % 2, :])).then_inc(q_stored[m % 2], 16)
            for stored in q_stored:
                sp.wait_ge(stored, 16 * B * G)

        @block.scalar
        def _(act):
            act.wait_ge(w_in, 16)
            act.activation(wh[:], w[:], ACT.Copy).then_inc(wh_done, 1)
            norm.scalar_3_root(act)
            norm.scalar_6_hi(act)
            act.wait_ge(c_in, 32)
            for m in range(B * G):
                act.wait_ge(q_mm, m + 1)
                if m >= 2:
                    act.wait_ge(q_stored[m % 2], 32 * (m // 2))
                act.activation(qh[:, m % 2, :], ps_q[:, m % 2, :], ACT.Identity,
                               bias=bias[:, m % G:m % G + 1]).then_inc(qh_done, 1)

        @block.vector
        def _(dve):
            for i in range(NT):
                dve.wait_ge(x_in[i // TT], 16)
                norm.vector_1_stats(dve, i)
            norm.vector_2_variance(dve)
            dve.wait_ge(wh_done, 1)
            dve.tensor_tensor(wl[:], w[:], fp(wh[:]), ALU.subtract).then_inc(wl_done, 1)
            norm.vector_4_apply(dve)
            norm.vector_7_lo(dve)
            for m in range(B * G):
                dve.wait_ge(qh_done, m + 1)
                dve.scalar_tensor_tensor(ql[:, m % 2, :], ps_q[:, m % 2, :], bias[:, m % G:m % G + 1],
                                         fp(qh[:, m % 2, :]), ALU.add, ALU.subtract).then_inc(ql_done, 1)

        @block.tensor
        def _(pe):
            pe.wait_ge(c_in, 32)
            norm.tensor_5_turn(pe)
            pe.wait_ge(wl_done, 1)
            for m in range(B * G):
                b, g = m // G, m % G
                pe.wait_ge(norm.lo_done, DT * (b + 1))
                if m >= 2:
                    pe.wait_ge(ql_done, m - 1)
                exact_product(pe, ps_q[:, m % 2, :], lambda part, d: (wh, wl)[part][:, d, g * P:(g + 1) * P],
                              lambda part, d: (norm.hi, norm.lo)[part][:, d, b * T:(b + 1) * T]).then_inc(q_mm, 1)


def cross_attention(nc, ctx_t, wk, bk, wv, bv, ident, onehot, q_split, attended, CH):
    STEPS = CH * G
    NCH = B * CH
    with ExitStack() as ctx:
        sb = lambda name, shape, dt=F32: ctx.enter_context(nc.sbuf_tensor(name, shape, dt))
        sem = lambda name: ctx.enter_context(nc.semaphore(name))
        bank = lambda name, n=1: ctx.enter_context(nc.psum_tensor(name, [P, n, 512], F32))
        ps_s, ps_m, ps_o, ps_d, ps_p, ps_x = (bank("ps_score", 2), bank("ps_max", 2), bank("ps_out"),
                                              bank("ps_den"), bank("ps_proj"), bank("ps_turn"))
        idn, idr, ones = sb("idn", [P, P]), sb("idr", [P, P], F32R), sb("ones", [P, HD])
        bk_s, bv_s = sb("bk_s", [P, G]), sb("bv_s", [P, G])
        wkh, wkl = sb("wkh", [P, DT, D], F32R), sb("wkl", [P, DT, D], F32R)
        wvh, wvl = sb("wvh", [P, DT, D], F32R), sb("wvl", [P, DT, D], F32R)
        raw = sb("raw", [P, DT, KC])
        chi, clo = sb("chi", [P, DT, KC], F32R), sb("clo", [P, DT, KC], F32R)
        knh, knl = sb("knh", [P, 2, KC], F32R), sb("knl", [P, 2, KC], F32R)
        kst = sb("kst", [P, G, HG, KC], F32R)
        qst = sb("qst", [P, G, HG, T], F32R)
        val = sb("val", [P, 2, KT, D])
        prob = sb("prob", [P, KT, HG, T])
        psum4 = sb("psum4", [P, HG, T])
        acc_o, acc_d = sb("acc_o", [P, G, T]), sb("acc_d", [P, G, T])
        scale_b = sb("scale_b", [P, T])
        scale_t = sb("scale_t", [P, TT, HG, HD])
        nmax, nmax_new = sb("nmax", [P, G, TT * HG], F32R), sb("nmax_new", [P, TT * HG], F32R)
        tile_max, drop = sb("tile_max", [P, TT, HG]), sb("drop", [P, TT * HG])
        nmax_w = sb("nmax_w", [P, TT, P], F32R)

        c_in, ready = sem("c_in"), sem("b_ready")
        raw_in, w_split = sem("raw_in"), sem("w_split")
        ctx_hi, ctx_lo = sem("ctx_hi"), sem("ctx_lo")
        proj_mm, k_hi, k_lo, v_copied = sem("proj_mm"), sem("k_hi"), sem("k_lo"), sem("v_copied")
        kst_in, qst_in = [sem("kst_in0"), sem("kst_in1")], sem("qst_in")
        max_mm, max_read = sem("max_mm"), sem("max_read")
        nmax_made, nmax_wide, drop_made, nmax_kept = sem("nmax_made"), sem("nmax_wide"), sem("drop_made"), sem("nmax_kept")
        shift_mm, shift_in, shift_in_2 = sem("shift_mm"), sem("shift_in"), sem("shift_in_2")
        scale_made, scale_mm, scale_in, scaled = sem("scale_made"), sem("scale_mm"), sem("scale_in"), sem("scaled")
        scaled_o = sem("scaled_o")
        score_mm, exp_done, pv_mm, summed = sem("score_mm"), sem("exp_done"), sem("pv_mm"), sem("summed")
        den_mm, o_added, d_added = sem("den_mm"), sem("o_added"), sem("d_added")
        inv_made, norm_mul, norm_done, stored = sem("inv_made"), sem("norm_mul"), sem("norm_done"), sem("stored")
        block = ctx.enter_context(nc.Block())

        n_exp = lambda N, t, j: 16 * N + 16 + 4 * t + j + 1
        n_max_read = lambda M, k: 16 * M + 16 + k + 1
        n_pv = lambda N, b, t: 4 * N + b + t + 6
        n_summed = lambda N, k: 3 * N + 3 + k
        n_added = lambda N, b: N + b + 2
        n_stacked = lambda C, g: 384 * C + 192 * (g // 2) + 192
        n_proj = lambda N: 2 * N + 7

        @block.sync
        def _(sp):
            sp.dma_start(idn[:], ident).then_inc(c_in, 16)
            sp.dma_start(bk_s[:], bk).then_inc(c_in, 16)
            sp.dma_start(bv_s[:], bv).then_inc(c_in, 16)
            sp.dma_start(prob[:, 0], wk).then_inc(c_in, 16)
            sp.dma_start(prob[:, 1], wv).then_inc(c_in, 16)
            sp.dma_start(psum4[STACK:P], onehot).then_inc(c_in, 16)
            sp.dma_start(raw[:], ctx_t[0]).then_inc(raw_in, 16)
            sp.wait_ge(ctx_lo, DT)
            sp.dma_start(raw[:], ctx_t[1]).then_inc(raw_in, 16)

            def stack_k(k, slot, par, free=None):
                sp.wait_ge(k_hi, k + 1)
                if free is not None:
                    sp.wait_ge(score_mm, free)
                for j in range(HG):
                    rows = slice(HD * j, HD * (j + 1))
                    for q in range(2):
                        sp.dma_start(fp(kst[HD * q:HD * (q + 1), slot, j, :]), fp(knh[rows, par, :])).then_inc(kst_in[par], 16)
                sp.wait_ge(k_lo, k + 1)
                for j in range(HG):
                    rows = slice(HD * j, HD * (j + 1))
                    sp.dma_start(fp(kst[2 * HD:STACK, slot, j, :]), fp(knl[rows, par, :])).then_inc(kst_in[par], 16)

            stack_k(0, 0, 0)
            stack_k(1, 1, 1)
            stack_k(2, 2, 0)
            with sp.Fori(0, B) as b:
                for g in range(G):
                    for q, part in enumerate((0, 1, 0)):
                        src = q_split[bass.ds(b, 1), part, g].rearrange("o (j r) t -> r (o j) t", j=HG)
                        sp.dma_start(fp(qst[HD * q:HD * (q + 1), g]), src).then_inc(qst_in, 16)
                with sp.Fori(0, CH // 2) as c2:
                    for u in range(2):
                        for g in range(G):
                            C = b * CH + c2 * 2 + u
                            N = C * G + g
                            stack_k(N + 3, (g + 3) % G, (g + 1) % 2, 16 * N + 1)
                            if g == 0:
                                sp.wait_ge(ctx_lo, DT * (C + 2))
                                sp.dma_start(raw[:], ctx_t[bass.ds((C + 2) % NCH, 1)].rearrange(
                                    "o p d k -> (o p) d k")).then_inc(raw_in, 16)
                sp.wait_ge(norm_done, G * b + G)
                sp.dma_start(attended[bass.ds(b, 1)].rearrange("o p g t -> (o p) g t"), acc_o[:]).then_inc(stored, 16)
            sp.wait_ge(stored, 16 * B)
            sp.wait_ge(kst_in[0], 96 * (B * STEPS + 4))
            sp.wait_ge(kst_in[1], 96 * (B * STEPS + 2))
            sp.wait_ge(raw_in, 16 * (NCH + 2))

        @block.scalar
        def _(act):
            act.wait_ge(c_in, 96)
            act.activation(wkh[:], prob[:, 0], ACT.Copy).then_inc(w_split, 1)
            act.activation(wvh[:], prob[:, 1], ACT.Copy).then_inc(w_split, 1)
            act.activation(idr[:], idn[:], ACT.Copy).then_inc(w_split, 1)
            for g in range(G):
                act.activation(kst[STACK:P, g], psum4[STACK:P], ACT.Copy).then_inc(w_split, 1)

            def split_hi(C, half):
                act.wait_ge(raw_in, 16 * C + 16)
                s = slice(2 * half, 2 * half + 2)
                act.activation(chi[:, s, :], raw[:, s, :], ACT.Copy).then_inc(ctx_hi, 1)

            def k_evac(k, proj, g, par, loaded=None):
                act.wait_ge(proj_mm, proj)
                if loaded is not None:
                    act.wait_ge(kst_in[par], loaded)
                act.activation(knh[:, par, :], ps_p[:, 0, :], ACT.Identity, bias=bk_s[:, g:g + 1]).then_inc(k_hi, 1)

            def v_evac(t, par, proj, pv=None):
                act.wait_ge(proj_mm, proj)
                if pv is not None:
                    act.wait_ge(pv_mm, pv)
                act.copy(val[:, par, t, :], ps_p[:, 0, :]).then_inc(v_copied, 1)

            def shift_copy(M, g):
                act.wait_ge(shift_mm, M + 1)
                act.activation(qst[STACK:ROWS, g, 0], ps_x[STACK:ROWS, 0, :],
                               ACT.Copy).then_inc(shift_in, 1)

            def scale_exp(M):
                act.wait_ge(drop_made, M + 1)
                act.wait_ge(scale_made, M + 1)
                act.activation(scale_t[:], drop[:].rearrange("p (t j) -> p t j", t=TT).unsqueeze(3).to_broadcast(
                    [P, TT, HG, HD]), ACT.Exp, scale=SCALE).then_inc(scale_made, 1)

            def exps(N, b, t, heads):
                for j in heads:
                    if j == 0:
                        act.wait_ge(pv_mm, n_pv(N, b, -1) if t == 3 else n_pv(N - 1, b, t))
                        act.wait_ge(summed, n_summed(N - 1, max(t, 1)))
                    act.wait_ge(score_mm, 16 * N + 4 * t + j + 1)
                    act.activation(prob[:, t, j, :], ps_s[:, j % 2, :], ACT.Exp, scale=SCALE).then_inc(exp_done, 1)

            split_hi(0, 0)
            split_hi(0, 1)
            for k in range(3):
                k_evac(k, k + 1, k, k % 2, 192 if k == 2 else None)
            for t in range(KT):
                v_evac(t, 0, 4 + t)
            with act.Fori(0, B) as b:
                shift_copy(b * (STEPS + 1), 0)
                scale_exp(b * (STEPS + 1))
                with act.Fori(0, CH // 2) as c2:
                    for u in range(2):
                        for g in range(G):
                            C = b * CH + c2 * 2 + u
                            N = C * G + g
                            exps(N, b, 0, range(4))
                            act.wait_ge(scale_mm, N + 1)
                            act.wait_ge(scaled, N + 1)
                            act.copy(scale_b[:], ps_x[:, 0, :]).then_inc(scale_in, 1)
                            k_evac(N + 3, n_proj(N) + 1, (g + 3) % G, (g + 1) % 2, n_stacked(C, g + 1))
                            if g == 0:
                                exps(N, b, 1, range(1))
                                split_hi(C + 1, 0)
                                exps(N, b, 1, range(1, 3))
                                split_hi(C + 1, 1)
                                exps(N, b, 1, range(3, 4))
                            else:
                                exps(N, b, 1, range(4))
                            exps(N, b, 2, range(4))
                            exps(N, b, 3, range(1))
                            v_evac(g, 1 - u, n_proj(N) + 2, n_pv(N, b, -1))
                            shift_copy(N + b + 1, (g + 1) % G)
                            exps(N, b, 3, range(1, 4))
                            scale_exp(N + b + 1)

        @block.vector
        def _(dve):
            dve.memset(ones[:], 1.0).then_inc(ready, 1)
            dve.memset(val[:, 1, KT - 1], 0.0).then_inc(ready, 1)
            dve.memset(fp(nmax_w[:]), 0.0).then_inc(shift_in, 1)
            dve.memset(scale_t[:], 0.0).then_inc(scale_made, 1)
            dve.memset(nmax_new[:].bitcast(F32), BIG).then_inc(shift_in_2, 1)
            dve.memset(acc_o[:], 0.0).then_inc(o_added, 1)
            dve.memset(acc_d[:], 0.0).then_inc(d_added, 1)
            dve.memset(ps_o[:], 0.0).then_inc(pv_mm, 4)
            dve.memset(fp(nmax[:]), BIG).then_inc(nmax_kept, 1)
            dve.memset(scale_b[:], 0.0).then_inc(scaled, 1)
            dve.memset(tile_max[:], 0.0).then_inc(max_read, 16)
            dve.wait_ge(w_split, 2)
            dve.tensor_tensor(wkl[:], prob[:, 0], fp(wkh[:]), ALU.subtract).then_inc(w_split, 1)
            dve.tensor_tensor(wvl[:], prob[:, 1], fp(wvh[:]), ALU.subtract).then_inc(w_split, 1)
            dve.wait_ge(w_split, 9)
            dve.memset(prob[:], 0.0).then_inc(exp_done, 16)
            dve.memset(psum4[:], 0.0).then_inc(summed, 3)

            def split_lo(C, d):
                dve.wait_ge(ctx_hi, 2 * C + 1 + d // 2)
                dve.tensor_tensor(clo[:, d, :], raw[:, d, :], fp(chi[:, d, :]), ALU.subtract).then_inc(ctx_lo, 1)

            def k_evac(k, g, par):
                dve.wait_ge(k_hi, k + 1)
                dve.scalar_tensor_tensor(knl[:, par, :], ps_p[:, 0, :], bk_s[:, g:g + 1], fp(knh[:, par, :]),
                                         ALU.add, ALU.subtract).then_inc(k_lo, 1)

            def maxima(M, first, n):
                for k in range(first, first + n):
                    j, t = k // TT, k % TT
                    dve.wait_ge(max_mm, 16 * M + k + 1)
                    dve.tensor_reduce(tile_max[:, t, j:j + 1], ps_m[:, k % 2, :], AX_X, ALU.max,
                                      negate=True).then_inc(max_read, 1)

            def update_max(M, b, g):
                dve.wait_ge(max_read, n_max_read(M, 15))
                dve.wait_ge(nmax_kept, M + b + 2)
                dve.tensor_tensor(nmax_new[:], fp(nmax[:, g, :]), tile_max[:].rearrange("p t j -> p (t j)"),
                                  ALU.min).then_inc(nmax_made, 1)
                dve.wait_ge(nmax_made, M + 1)
                dve.wait_ge(shift_in, M + 1)
                dve.tensor_copy(nmax_w[:, :, STACK:ROWS], fp(nmax_new[:]).rearrange("p (t j) -> p t j", t=TT)
                                ).then_inc(nmax_wide, 1)
                dve.wait_ge(scale_made, M + 1)
                dve.tensor_tensor(drop[:], fp(nmax_new[:]), fp(nmax[:, g, :]), ALU.subtract).then_inc(drop_made, 1)
                dve.wait_ge(drop_made, M + 1)
                dve.tensor_copy(nmax[:, g, :], fp(nmax_new[:])).then_inc(nmax_kept, 1)

            def shift_copy(M, g):
                dve.wait_ge(shift_in, M + 2)
                for j in range(1, HG):
                    dve.tensor_copy(qst[STACK:ROWS, g, j], fp(qst[STACK:ROWS, g, 0])).then_inc(shift_in_2, 1)

            def add_out(N, b, g):
                dve.wait_ge(pv_mm, n_pv(N, b, -1))
                dve.wait_ge(scaled, N + 1)
                dve.tensor_tensor(acc_o[:, g, :], ps_o[:, 0, :], acc_o[:, g, :], ALU.add).then_inc(o_added, 1)

            def add_den(N, b, g):
                dve.wait_ge(den_mm, N + b + 1)
                dve.tensor_tensor(acc_d[:, g, :], ps_d[:, 0, :], acc_d[:, g, :], ALU.add).then_inc(d_added, 1)

            for d in range(DT):
                split_lo(0, d)
            k_evac(0, 0, 0)
            k_evac(1, 1, 1)
            k_evac(2, 2, 0)
            with dve.Fori(0, B) as b:
                dve.wait_ge(nmax_kept, b * (STEPS + 2) + 1)
                dve.memset(fp(nmax[:]), BIG).then_inc(nmax_kept, 1)
                maxima(b * (STEPS + 1), 0, 16)
                update_max(b * (STEPS + 1), b, 0)
                shift_copy(b * (STEPS + 1), 0)
                with dve.Fori(0, CH // 2) as c2:
                    for u in range(2):
                        for g in range(G):
                            C = b * CH + c2 * 2 + u
                            N = C * G + g
                            M = N + b + 1
                            maxima(M, 0, 5)
                            add_out(N, b, (g + 3) % G)
                            maxima(M, 5, 2)
                            k_evac(N + 3, (g + 3) % G, (g + 1) % 2)
                            for d in range(DT):
                                maxima(M, 7 + 2 * d, 2)
                                if g == 0:
                                    split_lo(C + 1, d)
                            maxima(M, 15, 1)
                            update_max(M, b, (g + 1) % G)
                            add_den(N, b, (g + 3) % G)
                            shift_copy(M, (g + 1) % G)
                N = (b + 1) * STEPS
                add_out(N, b, G - 1)
                add_den(N, b, G - 1)
                dve.wait_ge(d_added, n_added(N, b))
                dve.reciprocal(acc_d[:], acc_d[:]).then_inc(inv_made, 1)
                dve.wait_ge(inv_made, b + 1)
                dve.tensor_tensor(acc_o[:], acc_o[:], acc_d[:], ALU.mult).then_inc(norm_mul, 1)
                dve.wait_ge(norm_mul, b + 1)
                for g in range(G):
                    dve.tensor_scalar(acc_o[:, g, :], acc_o[:, g, :], bv_s[:, g:g + 1], None, ALU.add
                                      ).then_inc(norm_done, 1)
                dve.wait_ge(stored, 16 * b + 16)

        @block.gpsimd
        def _(pool):
            with pool.Fori(0, B) as b:
                with pool.Fori(0, STEPS // G) as c:
                    for g in range(G):
                        N = (b * CH + c) * G + g
                        if g == 0:
                            pool.wait_ge(nmax_kept, b * (STEPS + 2) + 2)
                        pool.wait_ge(scale_in, N + 1)
                        pool.wait_ge(d_added, n_added(N, b) - 1)
                        pool.tensor_tensor(acc_o[:, g, :], acc_o[:, g, :], scale_b[:], ALU.mult).then_inc(scaled_o, 1)
                        pool.tensor_tensor(acc_d[:, g, :], acc_d[:, g, :], scale_b[:], ALU.mult).then_inc(scaled, 1)
                        pool.wait_ge(exp_done, n_exp(N, 1, 3))
                        pool.wait_ge(den_mm, N + b + 1)
                        pool.tensor_tensor(psum4[:], prob[:, 0], prob[:, 1], ALU.add).then_inc(summed, 1)
                        for k in (1, 2):
                            pool.wait_ge(exp_done, n_exp(N, k + 1, 3))
                            pool.wait_ge(summed, n_summed(N, k))
                            pool.tensor_tensor(psum4[:], psum4[:], prob[:, k + 1], ALU.add).then_inc(summed, 1)

        @block.tensor
        def _(pe):
            pe.wait_ge(ready, 2)
            pe.wait_ge(w_split, 9)

            def project_k(part, g):
                wp, cp = ((wkh, chi), (wkh, clo), (wkl, chi))[part]
                for d in range(DT):
                    mm = pe.matmul(ps_p[:, 0, :], wp[:, d, g * P:(g + 1) * P], cp[:, d, :],
                                   start=(part == 0 and d == 0), stop=(part == 2 and d == DT - 1))
                if part == 2:
                    mm.then_inc(proj_mm, 1)

            def project_v(part, t):
                cp, wp = ((chi, wvh), (chi, wvl), (clo, wvh))[part]
                for d in range(DT):
                    mm = pe.matmul(ps_p[:, 0, :], cp[:, d, t * P:(t + 1) * P], wp[:, d, :],
                                   start=(part == 0 and d == 0), stop=(part == 2 and d == DT - 1))
                if part == 2:
                    mm.then_inc(proj_mm, 1)

            def max_scores(M, g, k):
                j, t = k // TT, k % TT
                pe.wait_ge(max_read, n_max_read(M, k - 2))
                pe.matmul(ps_m[:, k % 2, :], qst[0:STACK, g, j, t * P:(t + 1) * P], kst[0:STACK, g, j, :],
                          start=True, stop=True).then_inc(max_mm, 1)

            def shift_rows(M):
                pe.wait_ge(nmax_wide, M + 1)
                for t in range(TT):
                    mm = pe.matmul(ps_x[:, 0, t * P:(t + 1) * P], nmax_w[:, t, :], idr[:], start=True, stop=True)
                mm.then_inc(shift_mm, 1)

            def scores(N, g, t, j):
                pe.wait_ge(exp_done, n_exp(N, t, j) - 2)
                pe.matmul(ps_s[:, j % 2, :], kst[0:ROWS, g, j, t * P:(t + 1) * P], qst[0:ROWS, g, j, :],
                          start=True, stop=True).then_inc(score_mm, 1)

            def values(N, par, g, t):
                pe.wait_ge(exp_done, n_exp(N, t, 3))
                for j in range(HG):
                    c = (g * HG + j) * HD
                    mm = pe.matmul(ps_o[j * HD:(j + 1) * HD, 0, :], val[:, par, t, c:c + HD], prob[:, t, j, :],
                                   start=(t == 0), stop=(t == KT - 1))
                mm.then_inc(pv_mm, 1)

            def denominators(N, b):
                pe.wait_ge(summed, n_summed(N - 1, 3))
                pe.wait_ge(d_added, n_added(N, b) - 1)
                for j in range(HG):
                    mm = pe.matmul(ps_d[j * HD:(j + 1) * HD, 0, :], ones[:], psum4[:, j, :], start=True, stop=True)
                mm.then_inc(den_mm, 1)

            def scale_rows(N, b):
                pe.wait_ge(scale_made, N + b + 2)
                pe.wait_ge(shift_in, N + b + 2)
                for t in range(TT):
                    mm = pe.transpose(ps_x[:, 0, t * P:(t + 1) * P], scale_t[:, t].rearrange("p j r -> p (j r)"), idn[:])
                mm.then_inc(scale_mm, 1)

            pe.wait_ge(ctx_lo, DT)
            for k in range(3):
                if k:
                    pe.wait_ge(k_lo, k)
                for part in range(3):
                    project_k(part, k)
            for t in range(KT):
                if t == 0:
                    pe.wait_ge(k_lo, 3)
                else:
                    pe.wait_ge(v_copied, t)
                for part in range(3):
                    project_v(part, t)

            with pe.Fori(0, B) as b:
                M0 = b * (STEPS + 1)
                pe.wait_ge(qst_in, 192 * b + 192)
                pe.wait_ge(kst_in[0], b * (96 * STEPS) + 384)
                for k in range(16):
                    max_scores(M0, 0, k)
                pe.wait_ge(shift_in, M0 + 1)
                shift_rows(M0)
                pe.wait_ge(o_added, b * (STEPS + 1) + 1)
                pe.wait_ge(exp_done, b * (16 * STEPS) + 16)
                for j in range(HG):
                    c = (3 * HG + j) * HD
                    pe.matmul(ps_o[j * HD:(j + 1) * HD, 0, :], val[:, 0, 0, c:c + HD], prob[:, 3, j, :],
                              start=True, stop=False)
                with pe.Fori(0, CH // 2) as c2:
                    for u in range(2):
                        for g in range(G):
                            C = b * CH + c2 * 2 + u
                            N = C * G + g
                            M = N + b + 1
                            score = lambda t, j: scores(N, g, t, j)
                            peak = lambda k: max_scores(M, (g + 1) % G, k)

                            pe.wait_ge(kst_in[(g + 1) % 2], n_stacked(C, g + 1))
                            peak(0)
                            pe.wait_ge(v_copied, N + 4)
                            project_k(0, (g + 3) % G)
                            peak(1)
                            pe.wait_ge(shift_in, N + b + 2)
                            score(0, 0)
                            pe.wait_ge(shift_in_2, 3 * (N + b) + 2)
                            score(0, 1)
                            peak(2)
                            values(N - 1, u if g else 1 - u, (g + 3) % G, 3)
                            peak(3)
                            pe.wait_ge(shift_in_2, 3 * (N + b) + 3)
                            score(0, 2)
                            project_k(1, (g + 3) % G)
                            peak(4)
                            pe.wait_ge(shift_in_2, 3 * (N + b) + 4)
                            score(0, 3)
                            scale_rows(N, b)
                            peak(5)
                            project_k(2, (g + 3) % G)
                            peak(6)
                            score(1, 0)
                            pe.wait_ge(o_added, n_added(N, b))
                            peak(7)
                            values(N, u, g, 0)
                            peak(8)
                            score(1, 1)
                            score(1, 2)
                            peak(9)
                            denominators(N, b)
                            peak(10)
                            score(1, 3)
                            score(2, 0)
                            peak(11)
                            pe.wait_ge(k_lo, N + 4)
                            if g == 0:
                                pe.wait_ge(ctx_hi, 2 * C + 4)
                            project_v(0, g)
                            peak(12)
                            score(2, 1)
                            peak(13)
                            values(N, u, g, 1)
                            peak(14)
                            score(2, 2)
                            score(2, 3)
                            peak(15)
                            project_v(1, g)
                            score(3, 0)
                            if g == 0:
                                pe.wait_ge(ctx_lo, DT * (C + 2))
                            project_v(2, g)
                            pe.wait_ge(scale_in, N + 1)
                            shift_rows(M)
                            score(3, 1)
                            values(N, u, g, 2)
                            score(3, 2)
                            score(3, 3)
                N = (b + 1) * STEPS
                values(N - 1, 1, G - 1, 3)
                denominators(N, b)


class Merge:

    def __init__(self, nc, ctx, tag):
        sb = lambda name, shape, dt=F32: ctx.enter_context(nc.sbuf_tensor(f"{tag}_{name}", shape, dt))
        sem = lambda name: ctx.enter_context(nc.semaphore(f"{tag}_{name}"))
        self.ps = ctx.enter_context(nc.psum_tensor(f"{tag}_ps_merge", [P, 2, 512], F32))
        self.y, self.bias = sb("y", [P, NT, D]), sb("bias", [P, D])
        self.o, self.oh, self.ol = sb("o", [P, B, G, T]), sb("oh", [P, B, G, T], F32R), sb("ol", [P, B, G, T], F32R)
        self.w, self.wh, self.wl = sb("w", [P, DT, D]), sb("wh", [P, DT, D], F32R), sb("wl", [P, DT, D], F32R)
        self.w_in, self.bias_in = sem("w_in"), sem("bias_in")
        self.o_in, self.y_in = [sem(f"o_in{b}") for b in range(B)], [sem(f"y_in{b}") for b in range(B)]
        self.wh_done, self.wl_done, self.oh_done, self.ol_done = sem("wh_done"), sem("wl_done"), sem("oh_done"), sem("ol_done")
        self.biased, self.mm, self.y_done = sem("biased"), sem("mm"), sem("y_done")

    def sync_1_load(self, sp, x, attended, w, bias):
        sp.dma_start(self.w[:], w).then_inc(self.w_in, 16)
        sp.dma_start(self.bias[:], bias.partition_broadcast(P)).then_inc(self.bias_in, 16)
        for b in range(B):
            sp.dma_start(self.o[:, b], attended[b]).then_inc(self.o_in[b], 16)
            sp.dma_start(self.y[:, TT * b:TT * (b + 1), :], x[b].rearrange("(t p) d -> p t d", p=P)).then_inc(self.y_in[b], 16)

    def scalar_2_hi(self, act):
        act.wait_ge(self.w_in, 16)
        act.activation(self.wh[:], self.w[:], ACT.Copy).then_inc(self.wh_done, 1)
        for b in range(B):
            act.wait_ge(self.o_in[b], 16)
            act.activation(self.oh[:, b], self.o[:, b], ACT.Copy).then_inc(self.oh_done, 1)

    def gpsimd_2_bias(self, pool):
        pool.wait_ge(self.bias_in, 16)
        for b in range(B):
            pool.wait_ge(self.y_in[b], 16)
            for i in range(TT * b, TT * (b + 1)):
                pool.tensor_tensor(self.y[:, i, :], self.y[:, i, :], self.bias[:], ALU.add).then_inc(self.biased, 1)

    def vector_3_lo(self, dve):
        dve.wait_ge(self.wh_done, 1)
        dve.tensor_tensor(self.wl[:], self.w[:], fp(self.wh[:]), ALU.subtract).then_inc(self.wl_done, 1)
        for b in range(B):
            dve.wait_ge(self.oh_done, b + 1)
            dve.tensor_tensor(self.ol[:, b], self.o[:, b], fp(self.oh[:, b]), ALU.subtract).then_inc(self.ol_done, 1)

    def tensor_4_product(self, pe):
        pe.wait_ge(self.wl_done, 1)
        for i in range(NT):
            b, t = i // TT, i % TT
            pe.wait_ge(self.ol_done, b + 1)
            if i >= 2:
                pe.wait_ge(self.y_done, i - 1)
            exact_product(pe, self.ps[:, i % 2, :], lambda part, d: (self.oh, self.ol)[part][:, b, d, t * P:(t + 1) * P],
                          lambda part, d: (self.wh, self.wl)[part][:, d, :]).then_inc(self.mm, 1)

    def vector_5_add(self, dve, i):
        dve.wait_ge(self.mm, i + 1)
        dve.wait_ge(self.biased, i + 1)
        dve.tensor_tensor(self.y[:, i, :], self.ps[:, i % 2, :], self.y[:, i, :], ALU.add).then_inc(self.y_done, 1)
        dve.wait_ge(self.y_done, i + 1)


def project_self(nc, x, attended, wo, bo, w_qkv, cos, sin, ident, x1, qk_split, v_out):
    with ExitStack() as ctx:
        sb = lambda name, shape, dt=F32: ctx.enter_context(nc.sbuf_tensor(name, shape, dt))
        sem = lambda name: ctx.enter_context(nc.semaphore(name))
        idn = sb("c_id", [P, P])
        merge = Merge(nc, ctx, "cm")
        ps_e, ps_v = (ctx.enter_context(nc.psum_tensor("c_ps_pair", [P, 2, 512], F32)),
                      ctx.enter_context(nc.psum_tensor("c_ps_v", [P, 2, 512], F32)))
        norm = Norm(nc, ctx, "cn", merge.y, idn)
        table = sb("c_table", [P, 2, 2, T])
        wh, wl = sb("c_qh", [P, DT, D], F32R), sb("c_ql", [P, DT, D], F32R)
        prod = sb("c_prod", [P, 4, T])
        part_h, part_l = sb("c_part_h", [P, 2, T], F32R), sb("c_part_l", [P, 2, T], F32R)
        turned_qk = sb("c_turned", [P, 2, T])
        val = sb("c_val", [P, 2, D])
        c_in, w_in = sem("c_c_in"), sem("c_w2_in")
        wh_done, wl_done = sem("c_wh2_done"), sem("c_wl2_done")
        pair_mm, mults, turns, ph_done, pl_done = (sem("c_pair_mm"), sem("c_mults"), sem("c_turns"), sem("c_ph_done"), sem("c_pl_done"))
        v_mm, v_done = sem("c_v_mm"), sem("c_v_done")
        parts_out, v_sent, x1_out = sem("c_parts_out"), [sem("c_v_sent0"), sem("c_v_sent1")], sem("c_x1_out")
        block = ctx.enter_context(nc.Block())
        PAIRS = 2 * B * 2

        @block.sync
        def _(sp):
            sp.dma_start(idn[:], ident).then_inc(c_in, 16)
            sp.dma_start(table[:, 0], cos).then_inc(c_in, 16)
            sp.dma_start(table[:, 1], sin).then_inc(c_in, 16)
            merge.sync_1_load(sp, x, attended, wo, bo)
            for n in range(3):
                if n == 0:
                    sp.wait_ge(merge.wl_done, 1)
                else:
                    sp.wait_ge(wl_done, n)
                sp.dma_start(merge.w[:], w_qkv[n]).then_inc(w_in, 16)
                if n == 0:
                    for b in range(B):
                        sp.wait_ge(merge.y_done, TT * (b + 1))
                        sp.dma_start(x1[b].rearrange("(t p) d -> p t d", p=P), merge.y[:, TT * b:TT * (b + 1), :]).then_inc(x1_out, 16)
                else:
                    for m in range(2 * B * (n - 1), 2 * B * n):
                        b, e = (m // 2) % B, m % 2
                        for r in range(2):
                            sp.wait_ge(pl_done, 2 * m + r + 1)
                            sp.dma_start(qk_split[b, n - 1, r, 0, e], fp(part_h[:, r, :])).then_inc(parts_out, 16)
                            sp.dma_start(qk_split[b, n - 1, r, 1, e], fp(part_l[:, r, :])).then_inc(parts_out, 16)
            for i in range(NT):
                sp.wait_ge(v_done, i + 1)
                sp.dma_start(v_out[i // TT, :, i % TT, :], val[:, i % 2, :]).then_inc(v_sent[i % 2], 16)
            sp.wait_ge(x1_out, 16 * B)
            sp.wait_ge(parts_out, 64 * PAIRS)
            for sent in v_sent:
                sp.wait_ge(sent, 8 * NT)

        @block.gpsimd
        def _(pool):
            merge.gpsimd_2_bias(pool)
            for m in range(PAIRS):
                pool.wait_ge(mults, 4 * m + 2)
                if m:
                    pool.wait_ge(pl_done, 2 * m - 1)
                pool.tensor_tensor(turned_qk[:, 0], prod[:, 0], prod[:, 1], ALU.subtract).then_inc(turns, 1)
                pool.wait_ge(mults, 4 * m + 4)
                if m:
                    pool.wait_ge(pl_done, 2 * m)
                pool.tensor_tensor(turned_qk[:, 1], prod[:, 2], prod[:, 3], ALU.add).then_inc(turns, 1)

        @block.scalar
        def _(act):
            merge.scalar_2_hi(act)
            norm.scalar_3_root(act)
            norm.scalar_6_hi(act)

            def weights(n):
                act.wait_ge(w_in, 16 * (n + 1))
                if n == 1:
                    act.wait_ge(pair_mm, PAIRS // 2)
                if n == 2:
                    act.wait_ge(pair_mm, PAIRS)
                act.activation(wh[:], merge.w[:], ACT.Copy).then_inc(wh_done, 1)

            weights(0)
            for m in range(PAIRS):
                for r in range(2):
                    act.wait_ge(turns, 2 * m + r + 1)
                    if m:
                        act.wait_ge(parts_out, 64 * m)
                    act.activation(part_h[:, r, :], turned_qk[:, r], ACT.Copy).then_inc(ph_done, 1)
                if m == PAIRS // 2 - 1:
                    weights(1)
            weights(2)
            for i in range(NT):
                act.wait_ge(v_mm, i + 1)
                if i >= 2:
                    act.wait_ge(v_sent[i % 2], 16 * (i // 2))
                act.copy(val[:, i % 2, :], ps_v[:, i % 2, :]).then_inc(v_done, 1)

        @block.vector
        def _(dve):
            merge.vector_3_lo(dve)
            for i in range(NT):
                merge.vector_5_add(dve, i)
                norm.vector_1_stats(dve, i)
            norm.vector_2_variance(dve)
            norm.vector_4_apply(dve)
            norm.vector_7_lo(dve)

            def weights(n):
                dve.wait_ge(wh_done, n + 1)
                dve.tensor_tensor(wl[:], merge.w[:], fp(wh[:]), ALU.subtract).then_inc(wl_done, 1)

            weights(0)
            dve.wait_ge(c_in, 48)
            for m in range(PAIRS):
                e = m % 2
                dve.wait_ge(pair_mm, m + 1)
                if m:
                    dve.wait_ge(turns, 2 * m)
                for n, (half, tab) in enumerate(((0, 0), (1, 1), (0, 1), (1, 0))):
                    dve.tensor_tensor(prod[:, n], ps_e[:, half, :], table[:, tab, e, :], ALU.mult).then_inc(mults, 1)
                for r in range(2):
                    dve.wait_ge(ph_done, 2 * m + r + 1)
                    dve.tensor_tensor(part_l[:, r, :], turned_qk[:, r], fp(part_h[:, r, :]), ALU.subtract).then_inc(pl_done, 1)
                if m == PAIRS // 2 - 1:
                    weights(1)
            weights(2)

        @block.tensor
        def _(pe):
            pe.wait_ge(c_in, 48)
            merge.tensor_4_product(pe)
            norm.tensor_5_turn(pe)
            for m in range(PAIRS):
                b, e = (m // 2) % B, m % 2
                pe.wait_ge(wl_done, 1 + m // (2 * B))
                pe.wait_ge(norm.lo_done, DT * (b + 1))
                if m:
                    pe.wait_ge(mults, 4 * m)
                for half in range(2):
                    c = (2 * half + e) * P
                    mm = exact_product(pe, ps_e[:, half, :], lambda part, d: (wh, wl)[part][:, d, c:c + P],
                                       lambda part, d: (norm.hi, norm.lo)[part][:, d, b * T:(b + 1) * T])
                mm.then_inc(pair_mm, 1)
            pe.wait_ge(wl_done, 3)
            for i in range(NT):
                if i >= 2:
                    pe.wait_ge(v_done, i - 1)
                exact_product(pe, ps_v[:, i % 2, :], lambda part, d: (norm.hi, norm.lo)[part][:, d, i * P:(i + 1) * P],
                              lambda part, d: (wh, wl)[part][:, d, :]).then_inc(v_mm, 1)


def self_attention(nc, qk_split, v_in, ident, onehot, attended):
    STEPS = B * G
    with ExitStack() as ctx:
        sb = lambda name, shape, dt=F32: ctx.enter_context(nc.sbuf_tensor(name, shape, dt))
        sem = lambda name: ctx.enter_context(nc.semaphore(name))
        bank = lambda name, n=1: ctx.enter_context(nc.psum_tensor(name, [P, n, 512], F32))
        ps_s, ps_m, ps_o, ps_d, ps_x = (bank("d_ps_score", 2), bank("d_ps_max", 2), bank("d_ps_out"),
                                        bank("d_ps_den"), bank("d_ps_turn"))
        idn, idr, ones = sb("d_idn", [P, P]), sb("d_idr", [P, P], F32R), sb("d_ones", [P, HD])
        hot = sb("d_hot", [P, HG, T])
        kst, qst = sb("d_kst", [P, 2, HG, T], F32R), sb("d_qst", [P, 2, HG, T], F32R)
        val = sb("d_val", [P, B, TT, D])
        prob, psum4 = sb("d_prob", [P, TT, HG, T]), sb("d_psum4", [P, HG, T])
        tile_max, nmax_w = sb("d_tile_max", [P, TT, HG]), sb("d_nmax_w", [P, TT, P], F32R)
        inv, out = sb("d_inv", [P, T]), sb("d_out", [P, 2, T])
        c_in, v_in_sem, zeroed, consts = sem("d_c_in"), sem("d_v_in"), sem("d_zeroed"), sem("d_consts")
        stack_in = [sem("d_stack_in0"), sem("d_stack_in1")]
        max_mm, max_read, wide, shift_mm, shift_in, shift_in_2 = (sem("d_max_mm"), sem("d_max_read"), sem("d_wide"),
                                                                  sem("d_shift_mm"), sem("d_shift_in"), sem("d_shift_in_2"))
        score_mm, exp_done, pv_mm, summed, den_mm = (sem("d_score_mm"), sem("d_exp_done"), sem("d_pv_mm"),
                                                     sem("d_summed"), sem("d_den_mm"))
        inv_done, out_done, out_sent = sem("d_inv_done"), sem("d_out_done"), [sem("d_out_sent0"), sem("d_out_sent1")]
        block = ctx.enter_context(nc.Block())

        @block.sync
        def _(sp):
            sp.dma_start(idn[:], ident).then_inc(c_in, 16)
            sp.dma_start(hot[STACK:P], onehot).then_inc(c_in, 16)

            def stacks(n):
                b, g = n // G, n % G
                for which, dst, order in ((1, kst, (0, 0, 1)), (0, qst, (0, 1, 0))):
                    for q, part in enumerate(order):
                        for r in range(2):
                            src = qk_split[b, which, r, part, g // 2, (g % 2) * 64:(g % 2 + 1) * 64].rearrange(
                                "(j i) t -> i j t", j=HG)
                            row = HD * q + 16 * r
                            sp.dma_start(fp(dst[row:row + 16, n % 2]), src).then_inc(stack_in[n % 2], 16)

            stacks(0)
            for b in range(B):
                sp.dma_start(val[:, b], v_in[b]).then_inc(v_in_sem, 16)
            stacks(1)
            for n in range(STEPS):
                if n + 2 < STEPS:
                    sp.wait_ge(score_mm, 16 * (n + 1))
                    stacks(n + 2)
                sp.wait_ge(out_done, n + 1)
                sp.dma_start(attended[n // G, :, n % G, :], out[:, n % 2, :]).then_inc(out_sent[n % 2], 16)
            for sent in out_sent:
                sp.wait_ge(sent, 8 * STEPS)

        @block.gpsimd
        def _(pool):
            for n in range(STEPS):
                pool.wait_ge(exp_done, 16 * n + 8)
                if n:
                    pool.wait_ge(den_mm, n)
                pool.tensor_tensor(psum4[:], prob[:, 0], prob[:, 1], ALU.add).then_inc(summed, 1)
                for k in (2, 3):
                    pool.wait_ge(exp_done, 16 * n + 4 * k + 4)
                    pool.wait_ge(summed, 3 * n + k - 1)
                    pool.tensor_tensor(psum4[:], psum4[:], prob[:, k], ALU.add).then_inc(summed, 1)

        @block.scalar
        def _(act):
            act.wait_ge(c_in, 32)
            act.activation(idr[:], idn[:], ACT.Copy).then_inc(consts, 1)
            for s in range(2):
                act.activation(kst[STACK:P, s], hot[STACK:P], ACT.Copy).then_inc(consts, 1)

            def shift_copy(n):
                act.wait_ge(shift_mm, n + 1)
                act.activation(qst[STACK:ROWS, n % 2, 0], ps_x[STACK:ROWS, 0, :], ACT.Copy).then_inc(shift_in, 1)

            shift_copy(0)
            for n in range(STEPS):
                for t in range(TT):
                    for j in range(HG):
                        if n and j == 0:
                            act.wait_ge(pv_mm, 4 * (n - 1) + t + 1)
                            act.wait_ge(summed, 3 * (n - 1) + max(t, 1))
                        act.wait_ge(score_mm, 16 * n + 4 * t + j + 1)
                        act.activation(prob[:, t, j, :], ps_s[:, j % 2, :], ACT.Exp, scale=SCALE).then_inc(exp_done, 1)
                    if t == 3 and n + 1 < STEPS:
                        shift_copy(n + 1)

        @block.vector
        def _(dve):
            dve.memset(ones[:], 1.0).then_inc(zeroed, 1)
            dve.memset(fp(nmax_w[:]), 0.0).then_inc(zeroed, 1)

            def maxima(n, first, count):
                for k in range(first, first + count):
                    dve.wait_ge(max_mm, 16 * n + k + 1)
                    dve.tensor_reduce(tile_max[:, k % TT, k // TT:k // TT + 1], ps_m[:, k % 2, :], AX_X, ALU.max,
                                      negate=True).then_inc(max_read, 1)

            def shift(n):
                dve.wait_ge(max_read, 16 * n + 16)
                if n:
                    dve.wait_ge(shift_mm, n)
                else:
                    dve.wait_ge(zeroed, 2)
                dve.tensor_copy(nmax_w[:, :, STACK:ROWS], tile_max[:]).then_inc(wide, 1)
                dve.wait_ge(shift_in, n + 1)
                dve.tensor_copy(qst[STACK:ROWS, n % 2, 1:HG], fp(qst[STACK:ROWS, n % 2, 0:1]).to_broadcast(
                    [HG, HG - 1, T])).then_inc(shift_in_2, 1)

            def finish(n):
                dve.wait_ge(den_mm, n + 1)
                dve.reciprocal(inv[:], ps_d[:, 0, :]).then_inc(inv_done, 1)
                dve.wait_ge(inv_done, n + 1)
                dve.wait_ge(pv_mm, 4 * n + 4)
                if n >= 2:
                    dve.wait_ge(out_sent[n % 2], 16 * (n // 2))
                dve.tensor_tensor(out[:, n % 2, :], ps_o[:, 0, :], inv[:], ALU.mult).then_inc(out_done, 1)

            maxima(0, 0, 16)
            shift(0)
            for n in range(STEPS):
                if n + 1 < STEPS:
                    maxima(n + 1, 0, 16)
                    shift(n + 1)
                finish(n)

        @block.tensor
        def _(pe):
            pe.wait_ge(zeroed, 2)
            pe.wait_ge(consts, 3)

            def max_scores(n, k):
                s, j, t = n % 2, k // TT, k % TT
                if 16 * n + k >= 2:
                    pe.wait_ge(max_read, 16 * n + k - 1)
                pe.matmul(ps_m[:, k % 2, :], qst[0:STACK, s, j, t * P:(t + 1) * P], kst[0:STACK, s, j, :],
                          start=True, stop=True).then_inc(max_mm, 1)

            def shift_rows(n):
                pe.wait_ge(wide, n + 1)
                for t in range(TT):
                    mm = pe.matmul(ps_x[:, 0, t * P:(t + 1) * P], nmax_w[:, t, :], idr[:], start=True, stop=True)
                mm.then_inc(shift_mm, 1)

            def values(n, t):
                pe.wait_ge(exp_done, 16 * n + 4 * t + 4)
                for j in range(HG):
                    c = ((n % G) * HG + j) * HD
                    mm = pe.matmul(ps_o[j * HD:(j + 1) * HD, 0, :], val[:, n // G, t, c:c + HD], prob[:, t, j, :],
                                   start=(t == 0), stop=(t == TT - 1))
                mm.then_inc(pv_mm, 1)

            pe.wait_ge(stack_in[0], 192)
            for k in range(16):
                max_scores(0, k)
            shift_rows(0)
            pe.wait_ge(v_in_sem, 16 * B)
            for n in range(STEPS):
                for t in range(TT):
                    if t == 0:
                        pe.wait_ge(shift_in, n + 1)
                        pe.wait_ge(shift_in_2, n + 1)
                        if n + 1 < STEPS:
                            pe.wait_ge(stack_in[(n + 1) % 2], 192 * ((n + 1) // 2 + 1))
                    for j in range(HG):
                        if 16 * n + 4 * t + j >= 2:
                            pe.wait_ge(exp_done, 16 * n + 4 * t + j - 1)
                        pe.matmul(ps_s[:, j % 2, :], kst[0:ROWS, n % 2, j, t * P:(t + 1) * P], qst[0:ROWS, n % 2, j, :],
                                  start=True, stop=True).then_inc(score_mm, 1)
                        if n + 1 < STEPS:
                            if t == 3 and j == 2:
                                shift_rows(n + 1)
                            if t < 3:
                                first = (0, 6, 12)[t]
                                ends = (0, 1, 3, 5, 6) if t < 2 else (0, 1, 2, 3, 4)
                                for k in range(first + ends[j], first + ends[j + 1]):
                                    max_scores(n + 1, k)
                    if t:
                        if t == 1 and n:
                            pe.wait_ge(out_done, n)
                        values(n, t - 1)
                values(n, 3)
                pe.wait_ge(summed, 3 * n + 3)
                for j in range(HG):
                    mm = pe.matmul(ps_d[j * HD:(j + 1) * HD, 0, :], ones[:], psum4[:, j, :], start=True, stop=True)
                mm.then_inc(den_mm, 1)


def experts(nc, x1, attended, wu, bu, ident, router_w, router_b, index, expert_w, expert_b, out):
    with ExitStack() as ctx:
        sb = lambda name, shape, dt=F32: ctx.enter_context(nc.sbuf_tensor(name, shape, dt))
        sem = lambda name: ctx.enter_context(nc.semaphore(name))
        idn = sb("e_id", [P, P])
        ps_y = ctx.enter_context(nc.psum_tensor("e_ps_y", [P, 2, 512], F32))
        ps_r = ctx.enter_context(nc.psum_tensor("e_ps_router", [P, 512], F32))
        ps_c = ctx.enter_context(nc.psum_tensor("e_ps_coef", [P, 512], F32))
        merge = Merge(nc, ctx, "em")
        norm = Norm(nc, ctx, "en", merge.y, idn)
        rw, rwh, rwl = sb("e_rw", [P, DT, E]), sb("e_rwh", [P, DT, E], F32R), sb("e_rwl", [P, DT, E], F32R)
        rb, idx8, eb = sb("e_rb", [P, NT, E]), sb("e_idx", [P, NT, E]), sb("e_eb", [E, D])
        logit, top = sb("e_logit", [P, NT, E]), sb("e_top", [P, NT])
        ex, total, gate = sb("e_ex", [P, NT, E]), sb("e_total", [P, NT]), sb("e_gate", [P, NT])
        pick, first, coef = sb("e_pick", [P, NT, E]), sb("e_first", [P, NT]), sb("e_coef", [P, NT, E])
        coef_t = sb("e_coef_t", [E, B * T])
        raw = sb("e_raw", [P, DT, D])
        wh, wl = sb("e_wh", [P, 2, DT, D], F32R), sb("e_wl", [P, 2, DT, D], F32R)
        c_in, raw_in = sem("e_c_in"), sem("e_raw_in")
        rwh_done, rwl_done, chain, router_mm, ex_done = sem("e_rwh_done"), sem("e_rwl_done"), sem("e_chain"), sem("e_router_mm"), sem("e_ex_done")
        coef_done, coef_mm, coef_in, bias_mm, based = sem("e_coef_done"), sem("e_coef_mm"), sem("e_coef_in"), sem("e_bias_mm"), sem("e_based")
        wh_done, wl_done, y_mm, y_read = sem("e_wh2_done"), sem("e_wl2_done"), sem("e_y_mm"), sem("e_y_read")
        sent = sem("e_sent")
        block = ctx.enter_context(nc.Block())

        @block.sync
        def _(sp):
            sp.dma_start(idn[:], ident).then_inc(c_in, 16)
            sp.dma_start(rw[:], router_w).then_inc(c_in, 16)
            sp.dma_start(rb[:], router_b.partition_broadcast(P)).then_inc(c_in, 16)
            sp.dma_start(idx8[:], index.partition_broadcast(P)).then_inc(c_in, 16)
            sp.dma_start(eb[:], expert_b).then_inc(c_in, 16)
            merge.sync_1_load(sp, x1, attended, wu, bu)
            sp.dma_start(raw[:], expert_w[0]).then_inc(raw_in, 16)
            with sp.Fori(1, E) as e:
                sp.wait_ge(wl_done, e)
                sp.dma_start(raw[:], expert_w[bass.ds(e, 1)].rearrange("o p d n -> (o p) d n")).then_inc(raw_in, 16)
            for b in range(B):
                sp.wait_ge(y_read, NT * (E - 1) + TT * (b + 1))
                sp.dma_start(out[b].rearrange("(t p) d -> p t d", p=P), merge.y[:, TT * b:TT * (b + 1), :]).then_inc(sent, 16)
            sp.wait_ge(sent, 16 * B)

        @block.gpsimd
        def _(pool):
            merge.gpsimd_2_bias(pool)

        @block.scalar
        def _(act):
            act.wait_ge(c_in, 80)
            act.activation(rwh[:], rw[:], ACT.Copy).then_inc(rwh_done, 1)
            merge.scalar_2_hi(act)
            norm.scalar_3_root(act)
            norm.scalar_6_hi(act)

            def weights(e, slot, free=None):
                act.wait_ge(raw_in, 16 * e + 16)
                if free is not None:
                    act.wait_ge(y_mm, free)
                act.activation(wh[:, slot], raw[:], ACT.Copy).then_inc(wh_done, 1)

            weights(0, 0)
            act.wait_ge(chain, 3)
            act.activation(ex[:], pick[:], ACT.Exp).then_inc(ex_done, 1)
            act.wait_ge(coef_mm, 1)
            act.copy(coef_t[:, 0:T], ps_c[0:E, :]).then_inc(coef_in, 1)
            act.wait_ge(coef_mm, 2)
            act.copy(coef_t[:, T:2 * T], ps_c[0:E, :]).then_inc(coef_in, 1)
            weights(1, 1)
            with act.Fori(0, E // 2 - 1) as h:
                for slot in range(2):
                    weights(2 * h + 2 + slot, slot, NT * (2 * h + 1 + slot))

        @block.vector
        def _(dve):
            dve.wait_ge(rwh_done, 1)
            dve.tensor_tensor(rwl[:], rw[:], fp(rwh[:]), ALU.subtract).then_inc(rwl_done, 1)
            merge.vector_3_lo(dve)
            for i in range(NT):
                merge.vector_5_add(dve, i)
                norm.vector_1_stats(dve, i)
            norm.vector_2_variance(dve)
            norm.vector_4_apply(dve)
            norm.vector_7_lo(dve)

            def weights(e, slot):
                dve.wait_ge(wh_done, e + 1)
                dve.tensor_tensor(wl[:, slot], raw[:], fp(wh[:, slot]), ALU.subtract).then_inc(wl_done, 1)

            steps = [0]

            def link(ins):
                steps[0] += 1
                ins.then_inc(chain, 1)
                dve.wait_ge(chain, steps[0])

            weights(0, 0)
            wide = lambda small: small[:].unsqueeze(2).to_broadcast([P, NT, E])
            dve.wait_ge(router_mm, 1)
            link(dve.tensor_tensor(logit[:], ps_r[:, 0:NT * E].rearrange("p (n e) -> p n e", n=NT), rb[:], ALU.add))
            link(dve.tensor_reduce(top[:], logit[:], AX_X, ALU.max))
            link(dve.tensor_tensor(pick[:], logit[:], wide(top), ALU.subtract))
            dve.wait_ge(ex_done, 1)
            link(dve.tensor_reduce(total[:], ex[:], AX_X, ALU.add))
            link(dve.reciprocal(gate[:], total[:]))
            link(dve.tensor_scalar(logit[:], pick[:], 0.0, -float(E), ALU.is_ge, ALU.mult))
            link(dve.tensor_tensor(pick[:], logit[:], idx8[:], ALU.add))
            link(dve.tensor_reduce(first[:], pick[:], AX_X, ALU.min))
            link(dve.tensor_tensor(logit[:], pick[:], wide(first), ALU.is_equal))
            dve.tensor_tensor(coef[:], logit[:], wide(gate), ALU.mult).then_inc(coef_done, 1)
            for i in range(NT):
                dve.wait_ge(bias_mm, i + 1)
                dve.tensor_tensor(merge.y[:, i, :], ps_y[:, i % 2, :], merge.y[:, i, :], ALU.add).then_inc(based, 1)
            weights(1, 1)
            dve.wait_ge(based, NT)

            def add(e, i):
                dve.wait_ge(y_mm, e * NT + i + 1)
                if not isinstance(e, int) or e:
                    dve.wait_ge(y_read, (e - 1) * NT + i + 1)
                dve.scalar_tensor_tensor(merge.y[:, i, :], ps_y[:, i % 2, :], coef[:, i, bass.ds(e, 1)] if not isinstance(e, int)
                                         else coef[:, i, e:e + 1], merge.y[:, i, :], ALU.mult, ALU.add).then_inc(y_read, 1)

            for i in range(NT):
                add(0, i)
            for i in range(NT):
                add(1, i)
            with dve.Fori(0, E // 2 - 1) as h:
                for slot in range(2):
                    weights(2 * h + 2 + slot, slot)
                    for i in range(NT):
                        add(2 * h + 2 + slot, i)

        @block.tensor
        def _(pe):
            pe.wait_ge(c_in, 80)
            merge.tensor_4_product(pe)
            norm.tensor_5_turn(pe)
            pe.wait_ge(rwl_done, 1)
            pe.wait_ge(norm.lo_done, B * DT)
            for i in range(NT):
                mm = exact_product(pe, ps_r[:, i * E:(i + 1) * E], lambda part, d: (norm.hi, norm.lo)[part][:, d, i * P:(i + 1) * P],
                                   lambda part, d: (rwh, rwl)[part][:, d, :])
            mm.then_inc(router_mm, 1)
            pe.wait_ge(coef_done, 1)
            for b in range(B):
                if b:
                    pe.wait_ge(coef_in, b)
                for t in range(TT):
                    mm = pe.transpose(ps_c[0:E, t * P:(t + 1) * P], coef[:, b * TT + t, :], idn[:])
                mm.then_inc(coef_mm, 1)
            pe.wait_ge(coef_in, B)
            for i in range(NT):
                if i >= 2:
                    pe.wait_ge(based, i - 1)
                pe.matmul(ps_y[:, i % 2, :], coef_t[:, i * P:(i + 1) * P], eb[:], start=True, stop=True).then_inc(bias_mm, 1)

            def apply(e, slot, first=False):
                pe.wait_ge(wl_done, e + 1)
                for i in range(NT):
                    if first and i < 2:
                        pe.wait_ge(based, NT)
                    else:
                        pe.wait_ge(y_read, e * NT + i - 1)
                    exact_product(pe, ps_y[:, i % 2, :], lambda part, d: (norm.hi, norm.lo)[part][:, d, i * P:(i + 1) * P],
                                  lambda part, d: (wh, wl)[part][:, slot, d, :]).then_inc(y_mm, 1)

            apply(0, 0, True)
            apply(1, 1)
            with pe.Fori(0, E // 2 - 1) as h:
                for slot in range(2):
                    apply(2 * h + 2 + slot, slot)


def perceiver_block(nc, a, out):
    scratch = lambda name, shape: nc.dram_tensor(name, shape, F32, kind="Internal").ap()
    q_split = scratch("q_split", [B, 2, G, P, T])
    crossed, selfed = scratch("crossed", [B, P, G, T]), scratch("selfed", [B, P, G, T])
    x1, v_self = scratch("x1", [B, T, D]), scratch("v_self", [B, P, TT, D])
    qk_split = scratch("qk_split", [B, 2, 2, 2, 2, P, T])
    project_queries(nc, a["x"], a["x_wq"], a["x_bq"], a["ident"], q_split)
    cross_attention(nc, a["ctx_t"], a["x_wk"], a["x_bk"], a["x_wv"], a["x_bv"], a["ident"], a["onehot"], q_split,
                    crossed, a["ctx_t"].shape[0] // B)
    project_self(nc, a["x"], crossed, a["x_wo"], a["x_bo"], a["w_qkv"], a["cos"], a["sin"], a["ident"], x1, qk_split, v_self)
    self_attention(nc, qk_split, v_self, a["ident"], a["onehot"], selfed)
    experts(nc, x1, selfed, a["s_wu"], a["s_bu"], a["ident"], a["router_w"], a["router_b"], a["index"], a["expert_w"],
            a["expert_b"], out)


def kernel(**inputs):
    import numpy as np
    import concourse.bacc as bacc
    from concourse.bass_utils import run_bass_kernel_spmd

    x = {k: np.asarray(v) for k, v in inputs.items()}
    tiles = lambda w: np.ascontiguousarray(w.reshape(DT, P, -1).transpose(1, 0, 2))
    column = lambda v: np.ascontiguousarray(v.reshape(DT, P).T)
    row = lambda v: np.ascontiguousarray(v.reshape(1, -1))
    halves = lambda w: np.concatenate([w[0::2], w[1::2]])
    ctx = x["ctx_1024"]
    chunks = ctx.shape[1] // KC
    half = D // 2
    theta = np.float32(1.0) / np.float32(10000.0) ** (np.arange(half, dtype=np.float32) / np.float32(half))
    angle = np.arange(T, dtype=np.float32)[:, None] * theta[None, :]
    onehot = np.zeros((P - STACK, HG, T), np.float32)
    for j in range(HG):
        onehot[j, j] = 1.0
    turn = lambda v: np.ascontiguousarray(v.astype(np.float32).T.reshape(2, P, T).transpose(1, 0, 2))
    arrays = {
        "x": x["x"],
        "ctx_t": np.ascontiguousarray(ctx.reshape(B, chunks, KC, DT, P).transpose(0, 1, 4, 3, 2)).reshape(B * chunks, P, DT, KC),
        "x_wq": tiles(x["L0_xattn_Wq"].T), "x_bq": column(x["L0_xattn_bq"]),
        "x_wk": tiles(x["L0_xattn_Wk"].T), "x_bk": column(x["L0_xattn_bk"]),
        "x_wv": tiles(x["L0_xattn_Wv"].T), "x_bv": column(x["L0_xattn_bv"]),
        "x_wo": tiles(x["L0_xattn_Wo"].T), "x_bo": row(x["L0_xattn_bo"]),
        "w_qkv": np.stack([tiles(halves(x["L0_attn_Wq"]).T), tiles(halves(x["L0_attn_Wk"]).T), tiles(x["L0_attn_Wv"].T)]),
        "cos": turn(np.cos(angle)), "sin": turn(np.sin(angle)),
        "s_wu": tiles(x["L0_attn_Wu"].T), "s_bu": row(x["L0_attn_bu"]),
        "router_w": tiles(x["L0_ffn_router_w"]), "router_b": np.ascontiguousarray(np.tile(x["L0_ffn_router_b"], NT)).reshape(1, NT, E),
        "index": (np.arange(NT * E, dtype=np.float32) % E + E).reshape(1, NT, E).astype(np.float32),
        "expert_w": np.ascontiguousarray(x["L0_ffn_expert_w"].reshape(E, DT, P, D).transpose(0, 2, 1, 3)),
        "expert_b": x["L0_ffn_expert_b"],
        "ident": np.eye(P, dtype=np.float32), "onehot": onehot,
    }
    nc = bacc.Bacc("TRN2", target_bir_lowering=False, num_devices=1)
    ins, feed = {}, {}
    for name, a in arrays.items():
        feed[f"in_{name}"] = np.ascontiguousarray(a)
        ins[name] = nc.dram_tensor(f"in_{name}", a.shape, F32, kind="ExternalInput").ap()
    out = nc.dram_tensor("out", (B, T, D), F32, kind="ExternalOutput").ap()
    perceiver_block(nc, ins, out)
    r = run_bass_kernel_spmd(nc, [feed], core_ids=[0])
    return r.results[0]["out"]
```

```python
from contextlib import ExitStack

import concourse.bass as bass
from concourse import mybir

F32 = mybir.dt.float32
F32R = mybir.dt.float32r
ALU = mybir.AluOpType
ACT = mybir.ActivationFunctionType
AX_X = mybir.AxisListType.X

P = 128
B = 2
T = 512
D = 512
DT = D // P
H = 16
HD = D // H
HG = P // HD
G = H // HG
KC = 512
KT = KC // P
TT = T // P
SCALE = float(HD) ** -0.5
EPS = 1e-5
STACK = 3 * HD
NT = B * TT
E = 8
ROWS = STACK + HG
BIG = 1e30


def fp(ap):
    return ap.bitcast(F32)


class Norm:

    def __init__(self, nc, ctx, tag, x, ident):
        sb = lambda name, shape, dt=F32: ctx.enter_context(nc.sbuf_tensor(f"{tag}_{name}", shape, dt))
        sem = lambda name: ctx.enter_context(nc.semaphore(f"{tag}_{name}"))
        self.x, self.ident = x, ident
        self.ps = ctx.enter_context(nc.psum_tensor(f"{tag}_ps_turn", [P, 2, 512], F32))
        self.xn = sb("xn", [P, NT, D])
        self.hi, self.lo = sb("nh", [P, DT, B * T], F32R), sb("nl", [P, DT, B * T], F32R)
        self.stats, self.mv, self.var = sb("stats", [P, NT, 6]), sb("mv", [P, NT, 2]), sb("var", [P, NT])
        self.std, self.rstd, self.work = sb("std", [P, NT]), sb("rstd", [P, NT]), sb("work", [P, NT])
        self.vector_steps, self.std_done, self.xn_done = sem("vector_steps"), sem("std_done"), sem("xn_done")
        self.turned, self.hi_done, self.lo_done = sem("turned"), sem("hi_done"), sem("lo_done")

    def vector_1_stats(self, dve, i):
        dve.bn_stats(self.stats[:, i, :], self.x[:, i, :]).then_inc(self.vector_steps, 1)

    def vector_2_variance(self, dve):
        for i in range(NT):
            dve.wait_ge(self.vector_steps, NT + i)
            dve.bn_aggr(self.mv[:, i, :], self.stats[:, i, :]).then_inc(self.vector_steps, 1)
        dve.wait_ge(self.vector_steps, 2 * NT)
        dve.tensor_scalar(self.var[:], self.mv[:, :, 1], EPS, None, ALU.add).then_inc(self.vector_steps, 1)

    def scalar_3_root(self, act):
        act.wait_ge(self.vector_steps, 2 * NT + 1)
        act.activation(self.std[:], self.var[:], ACT.Sqrt).then_inc(self.std_done, 1)

    def vector_4_apply(self, dve):
        y, w, step = self.rstd, self.work, self.vector_steps
        dve.wait_ge(self.std_done, 1)
        dve.reciprocal(y[:], self.std[:]).then_inc(step, 1)
        dve.wait_ge(step, 2 * NT + 2)
        dve.tensor_tensor(w[:], y[:], y[:], ALU.mult).then_inc(step, 1)
        dve.wait_ge(step, 2 * NT + 3)
        dve.tensor_tensor(w[:], w[:], self.var[:], ALU.mult).then_inc(step, 1)
        dve.wait_ge(step, 2 * NT + 4)
        dve.tensor_scalar(w[:], w[:], -0.5, 1.5, ALU.mult, ALU.add).then_inc(step, 1)
        dve.wait_ge(step, 2 * NT + 5)
        dve.tensor_tensor(y[:], y[:], w[:], ALU.mult).then_inc(step, 1)
        dve.wait_ge(step, 2 * NT + 6)
        for i in range(NT):
            dve.tensor_scalar(self.xn[:, i, :], self.x[:, i, :], self.mv[:, i, 0:1], y[:, i:i + 1],
                              ALU.subtract, ALU.mult).then_inc(self.xn_done, 1)

    def tensor_5_turn(self, pe):
        for k in range(B * DT):
            b, d = k // DT, k % DT
            pe.wait_ge(self.xn_done, TT * (b + 1))
            if k >= 2:
                pe.wait_ge(self.lo_done, k - 1)
            for t in range(TT):
                mm = pe.transpose(self.ps[:, k % 2, t * P:(t + 1) * P],
                                  self.xn[:, b * TT + t, d * P:(d + 1) * P], self.ident[:])
            mm.then_inc(self.turned, 1)

    def _tokens(self, k):
        return slice((k // DT) * T, (k // DT + 1) * T)

    def scalar_6_hi(self, act):
        for k in range(B * DT):
            act.wait_ge(self.turned, k + 1)
            act.activation(self.hi[:, k % DT, self._tokens(k)], self.ps[:, k % 2, :], ACT.Copy).then_inc(self.hi_done, 1)

    def vector_7_lo(self, dve):
        for k in range(B * DT):
            dve.wait_ge(self.hi_done, k + 1)
            s = self._tokens(k)
            dve.tensor_tensor(self.lo[:, k % DT, s], self.ps[:, k % 2, :], fp(self.hi[:, k % DT, s]),
                              ALU.subtract).then_inc(self.lo_done, 1)


def exact_product(pe, out, left, right):
    for n, (lp, rp) in enumerate(((0, 0), (0, 1), (1, 0))):
        for d in range(DT):
            mm = pe.matmul(out, left(lp, d), right(rp, d), start=(n == 0 and d == 0), stop=(n == 2 and d == DT - 1))
    return mm


class Projection:

    def __init__(self, nc, ctx):
        sb = lambda name, shape, dt=F32: ctx.enter_context(nc.sbuf_tensor(name, shape, dt))
        self.wkh, self.wkl = sb("wkh", [P, DT, D], F32R), sb("wkl", [P, DT, D], F32R)
        self.wvh, self.wvl = sb("wvh", [P, DT, D], F32R), sb("wvl", [P, DT, D], F32R)
        self.raw = sb("raw", [P, DT, KC])
        self.chi, self.clo = sb("chi", [P, DT, KC], F32R), sb("clo", [P, DT, KC], F32R)


def project_queries(nc, proj, x, wq, bq, ident, wk, wv, ctx_t, q_split):
    with ExitStack() as ctx:
        sb = lambda name, shape, dt=F32: ctx.enter_context(nc.sbuf_tensor(name, shape, dt))
        sem = lambda name: ctx.enter_context(nc.semaphore(name))
        ps_q = ctx.enter_context(nc.psum_tensor("a_ps_q", [P, 2, 512], F32))
        xs, idn, bias = sb("a_x", [P, NT, D]), sb("a_id", [P, P]), sb("a_b", [P, DT])
        w, wh, wl = sb("a_w", [P, DT, D]), sb("a_wh", [P, DT, D], F32R), sb("a_wl", [P, DT, D], F32R)
        qh, ql = sb("a_qh", [P, 2, T], F32R), sb("a_ql", [P, 2, T], F32R)
        stage = sb("a_stage", [P, 2, DT, D])
        splits = ((stage[:, 0], proj.wkh, proj.wkl), (proj.raw, proj.chi, proj.clo), (stage[:, 1], proj.wvh, proj.wvl))
        norm = Norm(nc, ctx, "a", xs, idn)
        w_in, c_in, later_in, later_hi, later_lo = sem("a_w_in"), sem("a_c_in"), sem("a_later_in"), sem("a_later_hi"), sem("a_later_lo")
        x_in = [sem("a_x_in0"), sem("a_x_in1")]
        wh_done, wl_done = sem("a_wh_done"), sem("a_wl_done")
        q_mm, qh_done, ql_done = sem("a_q_mm"), sem("a_qh_done"), sem("a_ql_done")
        q_stored = [sem("a_q_stored0"), sem("a_q_stored1")]
        block = ctx.enter_context(nc.Block())

        @block.sync
        def _(sp):
            for b in range(B):
                sp.dma_start(xs[:, TT * b:TT * (b + 1), :], x[b].rearrange("(t p) d -> p t d", p=P)).then_inc(x_in[b], 16)
            sp.dma_start(w[:], wq).then_inc(w_in, 16)
            sp.dma_start(idn[:], ident).then_inc(c_in, 16)
            sp.dma_start(bias[:], bq).then_inc(c_in, 16)
            for dst, src in ((stage[:, 0], wk), (proj.raw[:], ctx_t[0]), (stage[:, 1], wv)):
                sp.dma_start(dst, src).then_inc(later_in, 16)
            for m in range(B * G):
                sp.wait_ge(qh_done, m + 1)
                sp.dma_start(q_split[m // G, 0, m % G], fp(qh[:, m % 2, :])).then_inc(q_stored[m % 2], 16)
                sp.wait_ge(ql_done, m + 1)
                sp.dma_start(q_split[m // G, 1, m % G], fp(ql[:, m % 2, :])).then_inc(q_stored[m % 2], 16)
            for stored in q_stored:
                sp.wait_ge(stored, 16 * B * G)

        @block.scalar
        def _(act):
            act.wait_ge(w_in, 16)
            act.activation(wh[:], w[:], ACT.Copy).then_inc(wh_done, 1)
            norm.scalar_3_root(act)
            norm.scalar_6_hi(act)
            act.wait_ge(c_in, 32)
            for m in range(B * G):
                act.wait_ge(q_mm, m + 1)
                if m >= 2:
                    act.wait_ge(q_stored[m % 2], 32 * (m // 2))
                act.activation(qh[:, m % 2, :], ps_q[:, m % 2, :], ACT.Identity,
                               bias=bias[:, m % G:m % G + 1]).then_inc(qh_done, 1)
                if m % 2 == 1 and m // 2 < len(splits):
                    src, high, low = splits[m // 2]
                    act.wait_ge(later_in, 16 * len(splits))
                    act.activation(high[:], src[:], ACT.Copy).then_inc(later_hi, 1)

        @block.vector
        def _(dve):
            for i in range(NT):
                dve.wait_ge(x_in[i // TT], 16)
                norm.vector_1_stats(dve, i)
            norm.vector_2_variance(dve)
            dve.wait_ge(wh_done, 1)
            dve.tensor_tensor(wl[:], w[:], fp(wh[:]), ALU.subtract).then_inc(wl_done, 1)
            norm.vector_4_apply(dve)
            norm.vector_7_lo(dve)
            for m in range(B * G):
                dve.wait_ge(qh_done, m + 1)
                dve.scalar_tensor_tensor(ql[:, m % 2, :], ps_q[:, m % 2, :], bias[:, m % G:m % G + 1],
                                         fp(qh[:, m % 2, :]), ALU.add, ALU.subtract).then_inc(ql_done, 1)
                if m % 2 == 0 and m:
                    src, high, low = splits[m // 2 - 1]
                    dve.wait_ge(later_hi, m // 2)
                    dve.tensor_tensor(low[:], src[:], fp(high[:]), ALU.subtract).then_inc(later_lo, 1)

        @block.tensor
        def _(pe):
            pe.wait_ge(c_in, 32)
            norm.tensor_5_turn(pe)
            pe.wait_ge(wl_done, 1)
            for m in range(B * G):
                b, g = m // G, m % G
                pe.wait_ge(norm.lo_done, DT * (b + 1))
                if m >= 2:
                    pe.wait_ge(ql_done, m - 1)
                exact_product(pe, ps_q[:, m % 2, :], lambda part, d: (wh, wl)[part][:, d, g * P:(g + 1) * P],
                              lambda part, d: (norm.hi, norm.lo)[part][:, d, b * T:(b + 1) * T]).then_inc(q_mm, 1)


def cross_attention(nc, proj, ctx_t, bk, bv, ident, onehot, q_split, attended, CH):
    STEPS = CH * G
    NCH = B * CH
    with ExitStack() as ctx:
        sb = lambda name, shape, dt=F32: ctx.enter_context(nc.sbuf_tensor(name, shape, dt))
        sem = lambda name: ctx.enter_context(nc.semaphore(name))
        bank = lambda name, n=1: ctx.enter_context(nc.psum_tensor(name, [P, n, 512], F32))
        ps_s, ps_m, ps_o, ps_d, ps_p, ps_x = (bank("ps_score", 2), bank("ps_max", 2), bank("ps_out"),
                                              bank("ps_den"), bank("ps_proj"), bank("ps_turn"))
        idn, idr, ones = sb("idn", [P, P]), sb("idr", [P, P], F32R), sb("ones", [P, HD])
        bk_s, bv_s = sb("bk_s", [P, G]), sb("bv_s", [P, G])
        wkh, wkl, wvh, wvl = proj.wkh, proj.wkl, proj.wvh, proj.wvl
        raw, chi, clo = proj.raw, proj.chi, proj.clo
        knh, knl = sb("knh", [P, 2, KC], F32R), sb("knl", [P, 2, KC], F32R)
        kst = sb("kst", [P, G, HG, KC], F32R)
        qst = sb("qst", [P, G, HG, T], F32R)
        val = sb("val", [P, 2, KT, D])
        prob = sb("prob", [P, KT, HG, T])
        psum4 = sb("psum4", [P, HG, T])
        acc_o, acc_d = sb("acc_o", [P, G, T]), sb("acc_d", [P, G, T])
        scale_b = sb("scale_b", [P, T])
        scale_t = sb("scale_t", [P, TT, HG, HD])
        nmax, nmax_new = sb("nmax", [P, G, TT * HG], F32R), sb("nmax_new", [P, TT * HG], F32R)
        tile_max, drop = sb("tile_max", [P, TT, HG]), sb("drop", [P, TT * HG])
        nmax_w = sb("nmax_w", [P, TT, P], F32R)

        c_in, ready = sem("c_in"), sem("b_ready")
        raw_in = sem("raw_in")
        ctx_hi, ctx_lo = sem("ctx_hi"), sem("ctx_lo")
        proj_mm, k_hi, k_lo, v_copied = sem("proj_mm"), sem("k_hi"), sem("k_lo"), sem("v_copied")
        kst_in, qst_in = [sem("kst_in0"), sem("kst_in1")], sem("qst_in")
        max_mm, max_read = sem("max_mm"), sem("max_read")
        nmax_made, nmax_wide, drop_made, nmax_kept = sem("nmax_made"), sem("nmax_wide"), sem("drop_made"), sem("nmax_kept")
        shift_mm, shift_in, shift_in_2 = sem("shift_mm"), sem("shift_in"), sem("shift_in_2")
        scale_made, scale_mm, scale_in, scaled = sem("scale_made"), sem("scale_mm"), sem("scale_in"), sem("scaled")
        score_mm, exp_done, pv_mm, summed = sem("score_mm"), sem("exp_done"), sem("pv_mm"), sem("summed")
        den_mm, o_added, d_added = sem("den_mm"), sem("o_added"), sem("d_added")
        inv_made, divided, biased, stored = sem("inv_made"), sem("divided"), sem("biased"), sem("stored")
        block = ctx.enter_context(nc.Block())

        n_exp = lambda N, t, j: 16 * N + 16 + 4 * t + j + 1
        n_max_read = lambda M, k: 16 * M + 16 + k + 1
        n_pv = lambda N, b, t: 4 * N + b + t + 6
        n_summed = lambda N, k: 3 * N + 3 + k
        n_added = lambda N, b: N + b + 2
        n_stacked = lambda C, g: 384 * C + 192 * (g // 2) + 192
        n_proj = lambda N: 2 * N + 7

        @block.sync
        def _(sp):
            sp.dma_start(bk_s[:], bk).then_inc(c_in, 16)
            sp.dma_start(bv_s[:], bv).then_inc(c_in, 16)
            sp.dma_start(raw[:], ctx_t[1]).then_inc(raw_in, 16)
            sp.dma_start(idn[:], ident).then_inc(c_in, 16)
            sp.dma_start(psum4[STACK:P], onehot).then_inc(c_in, 16)

            def queries(b):
                for g in range(G):
                    for q, part in enumerate((0, 1, 0)):
                        src = q_split[b, part, g].rearrange("o (j r) t -> r (o j) t", j=HG)
                        sp.dma_start(fp(qst[HD * q:HD * (q + 1), g]), src).then_inc(qst_in, 16)

            def stack_k(k, slot, par, free=None):
                sp.wait_ge(k_hi, k + 1)
                if free is not None:
                    sp.wait_ge(score_mm, free)
                for j in range(HG):
                    rows = slice(HD * j, HD * (j + 1))
                    for q in range(2):
                        sp.dma_start(fp(kst[HD * q:HD * (q + 1), slot, j, :]), fp(knh[rows, par, :])).then_inc(kst_in[par], 16)
                sp.wait_ge(k_lo, k + 1)
                for j in range(HG):
                    rows = slice(HD * j, HD * (j + 1))
                    sp.dma_start(fp(kst[2 * HD:STACK, slot, j, :]), fp(knl[rows, par, :])).then_inc(kst_in[par], 16)

            queries(slice(0, 1))
            stack_k(0, 0, 0)
            stack_k(1, 1, 1)
            stack_k(2, 2, 0)
            with sp.Fori(0, B) as b:
                with sp.Fori(0, CH // 2) as c2:
                    for u in range(2):
                        for g in range(G):
                            C = b * CH + c2 * 2 + u
                            N = C * G + g
                            stack_k(N + 3, (g + 3) % G, (g + 1) % 2, 16 * N + 1)
                            if g == 0:
                                sp.wait_ge(ctx_lo, DT * (C + 1))
                                sp.dma_start(raw[:], ctx_t[bass.ds((C + 2) % NCH, 1)].rearrange(
                                    "o p d k -> (o p) d k")).then_inc(raw_in, 16)
                sp.wait_ge(score_mm, (b + 1) * (16 * STEPS))
                queries(bass.ds((b + 1) % B, 1))
                sp.wait_ge(biased, G * b + G)
                sp.dma_start(attended[bass.ds(b, 1)].rearrange("o p g t -> (o p) g t"), acc_o[:]).then_inc(stored, 16)
            sp.wait_ge(stored, 16 * B + 16)
            sp.wait_ge(qst_in, 192 * (B + 1))
            sp.wait_ge(kst_in[0], 96 * (B * STEPS + 4))
            sp.wait_ge(kst_in[1], 96 * (B * STEPS + 2))
            sp.wait_ge(raw_in, 16 * (NCH + 1))

        @block.scalar
        def _(act):
            act.wait_ge(c_in, 64)

            def split_hi(C, half):
                act.wait_ge(raw_in, 16 * C)
                s = slice(2 * half, 2 * half + 2)
                act.activation(chi[:, s, :], raw[:, s, :], ACT.Copy).then_inc(ctx_hi, 1)

            def k_evac(k, proj, g, par, loaded=None):
                act.wait_ge(proj_mm, proj)
                if loaded is not None:
                    act.wait_ge(kst_in[par], loaded)
                act.activation(knh[:, par, :], ps_p[:, 0, :], ACT.Identity, bias=bk_s[:, g:g + 1]).then_inc(k_hi, 1)

            def v_evac(t, par, proj, pv=None):
                act.wait_ge(proj_mm, proj)
                if pv is not None:
                    act.wait_ge(pv_mm, pv)
                act.copy(val[:, par, t, :], ps_p[:, 0, :]).then_inc(v_copied, 1)

            def shift_copy(M, g):
                act.wait_ge(shift_mm, M + 1)
                act.activation(qst[STACK:ROWS, g, 0], ps_x[STACK:ROWS, 0, :],
                               ACT.Copy).then_inc(shift_in, 1)

            def scale_exp(M):
                act.wait_ge(drop_made, M + 1)
                act.wait_ge(scale_made, M + 1)
                act.activation(scale_t[:], drop[:].rearrange("p (t j) -> p t j", t=TT).unsqueeze(3).to_broadcast(
                    [P, TT, HG, HD]), ACT.Exp, scale=SCALE).then_inc(scale_made, 1)

            def exps(N, b, t, heads):
                for j in heads:
                    if j == 0:
                        act.wait_ge(pv_mm, n_pv(N, b, -1) if t == 3 else n_pv(N - 1, b, t))
                        act.wait_ge(summed, n_summed(N - 1, max(t, 1)))
                    act.wait_ge(score_mm, 16 * N + 4 * t + j + 1)
                    act.activation(prob[:, t, j, :], ps_s[:, j % 2, :], ACT.Exp, scale=SCALE).then_inc(exp_done, 1)

            for k in range(3):
                k_evac(k, k + 1, k, k % 2, 192 if k == 2 else None)
            act.activation(idr[:], idn[:], ACT.Copy).then_inc(ready, 1)
            for t in range(KT):
                v_evac(t, 0, 4 + t)
                act.activation(kst[STACK:P, t], psum4[STACK:P], ACT.Copy).then_inc(ready, 1)
            with act.Fori(0, B) as b:
                shift_copy(b * (STEPS + 1), 0)
                scale_exp(b * (STEPS + 1))
                with act.Fori(0, CH // 2) as c2:
                    for u in range(2):
                        for g in range(G):
                            C = b * CH + c2 * 2 + u
                            N = C * G + g
                            exps(N, b, 0, range(4))
                            act.wait_ge(scale_mm, N + 1)
                            act.wait_ge(scaled, N + 1)
                            act.copy(scale_b[:], ps_x[:, 0, :]).then_inc(scale_in, 1)
                            k_evac(N + 3, n_proj(N) + 1, (g + 3) % G, (g + 1) % 2, n_stacked(C, g + 1))
                            if g == 0:
                                exps(N, b, 1, range(1))
                                split_hi(C + 1, 0)
                                exps(N, b, 1, range(1, 3))
                                split_hi(C + 1, 1)
                                exps(N, b, 1, range(3, 4))
                            else:
                                exps(N, b, 1, range(4))
                            exps(N, b, 2, range(4))
                            exps(N, b, 3, range(1))
                            v_evac(g, 1 - u, n_proj(N) + 2, n_pv(N, b, -1))
                            shift_copy(N + b + 1, (g + 1) % G)
                            exps(N, b, 3, range(1, 4))
                            scale_exp(N + b + 1)
                for g in range(G):
                    act.wait_ge(divided, G * b + g + 1)
                    act.activation(acc_o[:, g, :], acc_o[:, g, :], ACT.Identity, bias=bv_s[:, g:g + 1]).then_inc(biased, 1)

        @block.vector
        def _(dve):
            dve.memset(ones[:], 1.0).then_inc(ready, 1)
            dve.memset(val[:, 1, KT - 1], 0.0).then_inc(ready, 1)
            dve.memset(fp(nmax_w[:]), 0.0).then_inc(shift_in, 1)
            dve.memset(drop[:], 0.0).then_inc(stored, 16)
            dve.memset(nmax_new[:].bitcast(F32), BIG).then_inc(shift_in_2, 1)
            dve.memset(ps_o[:], 0.0).then_inc(pv_mm, 4)
            dve.memset(fp(nmax[:]), BIG).then_inc(nmax_kept, 1)
            dve.memset(scale_b[:], 0.0).then_inc(scaled, 1)
            dve.memset(tile_max[:], 0.0).then_inc(max_read, 16)
            def split_lo(C, d):
                dve.wait_ge(ctx_hi, 2 * C - 1 + d // 2)
                dve.tensor_tensor(clo[:, d, :], raw[:, d, :], fp(chi[:, d, :]), ALU.subtract).then_inc(ctx_lo, 1)

            def k_evac(k, g, par):
                dve.wait_ge(k_hi, k + 1)
                dve.scalar_tensor_tensor(knl[:, par, :], ps_p[:, 0, :], bk_s[:, g:g + 1], fp(knh[:, par, :]),
                                         ALU.add, ALU.subtract).then_inc(k_lo, 1)

            def maxima(M, first, n):
                for k in range(first, first + n):
                    j, t = k // TT, k % TT
                    dve.wait_ge(max_mm, 16 * M + k + 1)
                    dve.tensor_reduce(tile_max[:, t, j:j + 1], ps_m[:, k % 2, :], AX_X, ALU.max,
                                      negate=True).then_inc(max_read, 1)

            def update_max(M, b, g):
                dve.wait_ge(max_read, n_max_read(M, 15))
                dve.wait_ge(nmax_kept, M + b + 2)
                dve.tensor_tensor(nmax_new[:], fp(nmax[:, g, :]), tile_max[:].rearrange("p t j -> p (t j)"),
                                  ALU.min).then_inc(nmax_made, 1)
                dve.wait_ge(nmax_made, M + 1)
                dve.wait_ge(shift_in, M + 1)
                dve.tensor_copy(nmax_w[:, :, STACK:ROWS], fp(nmax_new[:]).rearrange("p (t j) -> p t j", t=TT)
                                ).then_inc(nmax_wide, 1)
                dve.wait_ge(scale_made, M + 1)
                dve.tensor_tensor(drop[:], fp(nmax_new[:]), fp(nmax[:, g, :]), ALU.subtract).then_inc(drop_made, 1)
                dve.wait_ge(drop_made, M + 1)
                dve.tensor_copy(nmax[:, g, :], fp(nmax_new[:])).then_inc(nmax_kept, 1)

            def shift_copy(M, g):
                dve.wait_ge(shift_in, M + 2)
                for j in range(1, HG):
                    dve.tensor_copy(qst[STACK:ROWS, g, j], fp(qst[STACK:ROWS, g, 0])).then_inc(shift_in_2, 1)

            def add_out(N, b, g):
                dve.wait_ge(pv_mm, n_pv(N, b, -1))
                dve.wait_ge(scaled, N + 1)
                dve.tensor_tensor(acc_o[:, g, :], ps_o[:, 0, :], acc_o[:, g, :], ALU.add).then_inc(o_added, 1)

            def add_den(N, b, g):
                dve.wait_ge(den_mm, N + b + 1)
                dve.tensor_tensor(acc_d[:, g, :], ps_d[:, 0, :], acc_d[:, g, :], ALU.add).then_inc(d_added, 1)

            k_evac(0, 0, 0)
            k_evac(1, 1, 1)
            k_evac(2, 2, 0)
            with dve.Fori(0, B) as b:
                dve.wait_ge(nmax_kept, b * (STEPS + 2) + 1)
                dve.memset(fp(nmax[:]), BIG).then_inc(nmax_kept, 1)
                maxima(b * (STEPS + 1), 0, 16)
                dve.wait_ge(stored, 16 * b + 16)
                update_max(b * (STEPS + 1), b, 0)
                shift_copy(b * (STEPS + 1), 0)
                with dve.Fori(0, CH // 2) as c2:
                    for u in range(2):
                        for g in range(G):
                            C = b * CH + c2 * 2 + u
                            N = C * G + g
                            M = N + b + 1
                            maxima(M, 0, 5)
                            add_out(N, b, (g + 3) % G)
                            maxima(M, 5, 2)
                            k_evac(N + 3, (g + 3) % G, (g + 1) % 2)
                            for d in range(DT):
                                maxima(M, 7 + 2 * d, 2)
                                if g == 0:
                                    split_lo(C + 1, d)
                            maxima(M, 15, 1)
                            update_max(M, b, (g + 1) % G)
                            add_den(N, b, (g + 3) % G)
                            shift_copy(M, (g + 1) % G)
                N = (b + 1) * STEPS
                for g in range(G):
                    if g < G - 1:
                        dve.wait_ge(d_added, n_added(N, b) - 1)
                        dve.wait_ge(o_added, n_added(N, b) - 1)
                    else:
                        add_out(N, b, g)
                        add_den(N, b, g)
                        dve.wait_ge(d_added, n_added(N, b))
                        dve.wait_ge(o_added, n_added(N, b))
                    dve.reciprocal(acc_d[:, g, :], acc_d[:, g, :]).then_inc(inv_made, 1)
                    dve.wait_ge(inv_made, G * b + g + 1)
                    dve.tensor_tensor(acc_o[:, g, :], acc_o[:, g, :], acc_d[:, g, :], ALU.mult).then_inc(divided, 1)

        @block.gpsimd
        def _(pool):
            pool.memset(scale_t[:], 0.0).then_inc(scale_made, 1)
            pool.memset(acc_o[:], 0.0).then_inc(o_added, 1)
            pool.memset(acc_d[:], 0.0).then_inc(d_added, 1)
            pool.memset(prob[:], 0.0).then_inc(exp_done, 16)
            pool.wait_ge(ready, 3 + G)
            pool.memset(psum4[:], 0.0).then_inc(summed, 3)
            with pool.Fori(0, B) as b:
                with pool.Fori(0, STEPS // G) as c:
                    for g in range(G):
                        N = (b * CH + c) * G + g
                        if g == 0:
                            pool.wait_ge(stored, 16 * b + 16)
                        pool.wait_ge(scale_in, N + 1)
                        pool.wait_ge(d_added, n_added(N, b) - 1)
                        pool.tensor_tensor(acc_o[:, g, :], acc_o[:, g, :], scale_b[:], ALU.mult)
                        pool.tensor_tensor(acc_d[:, g, :], acc_d[:, g, :], scale_b[:], ALU.mult).then_inc(scaled, 1)
                        pool.wait_ge(exp_done, n_exp(N, 1, 3))
                        pool.wait_ge(den_mm, N + b + 1)
                        pool.tensor_tensor(psum4[:], prob[:, 0], prob[:, 1], ALU.add).then_inc(summed, 1)
                        for k in (1, 2):
                            pool.wait_ge(exp_done, n_exp(N, k + 1, 3))
                            pool.wait_ge(summed, n_summed(N, k))
                            pool.tensor_tensor(psum4[:], psum4[:], prob[:, k + 1], ALU.add).then_inc(summed, 1)

        @block.tensor
        def _(pe):
            def project_k(part, g):
                wp, cp = ((wkh, chi), (wkh, clo), (wkl, chi))[part]
                for d in range(DT):
                    mm = pe.matmul(ps_p[:, 0, :], wp[:, d, g * P:(g + 1) * P], cp[:, d, :],
                                   start=(part == 0 and d == 0), stop=(part == 2 and d == DT - 1))
                if part == 2:
                    mm.then_inc(proj_mm, 1)

            def project_v(part, t):
                cp, wp = ((chi, wvh), (chi, wvl), (clo, wvh))[part]
                for d in range(DT):
                    mm = pe.matmul(ps_p[:, 0, :], cp[:, d, t * P:(t + 1) * P], wp[:, d, :],
                                   start=(part == 0 and d == 0), stop=(part == 2 and d == DT - 1))
                if part == 2:
                    mm.then_inc(proj_mm, 1)

            def max_scores(M, g, k):
                j, t = k // TT, k % TT
                pe.wait_ge(max_read, n_max_read(M, k - 2))
                pe.matmul(ps_m[:, k % 2, :], qst[0:STACK, g, j, t * P:(t + 1) * P], kst[0:STACK, g, j, :],
                          start=True, stop=True).then_inc(max_mm, 1)

            def shift_rows(M):
                pe.wait_ge(nmax_wide, M + 1)
                for t in range(TT):
                    mm = pe.matmul(ps_x[:, 0, t * P:(t + 1) * P], nmax_w[:, t, :], idr[:], start=True, stop=True)
                mm.then_inc(shift_mm, 1)

            def scores(N, g, t, j):
                pe.wait_ge(exp_done, n_exp(N, t, j) - 2)
                pe.matmul(ps_s[:, j % 2, :], kst[0:ROWS, g, j, t * P:(t + 1) * P], qst[0:ROWS, g, j, :],
                          start=True, stop=True).then_inc(score_mm, 1)

            def values(N, par, g, t):
                pe.wait_ge(exp_done, n_exp(N, t, 3))
                for j in range(HG):
                    c = (g * HG + j) * HD
                    mm = pe.matmul(ps_o[j * HD:(j + 1) * HD, 0, :], val[:, par, t, c:c + HD], prob[:, t, j, :],
                                   start=(t == 0), stop=(t == KT - 1))
                mm.then_inc(pv_mm, 1)

            def denominators(N, b):
                pe.wait_ge(summed, n_summed(N - 1, 3))
                pe.wait_ge(d_added, n_added(N, b) - 1)
                for j in range(HG):
                    mm = pe.matmul(ps_d[j * HD:(j + 1) * HD, 0, :], ones[:], psum4[:, j, :], start=True, stop=True)
                mm.then_inc(den_mm, 1)

            def scale_rows(N, b):
                pe.wait_ge(scale_made, N + b + 2)
                pe.wait_ge(shift_in, N + b + 2)
                for t in range(TT):
                    mm = pe.transpose(ps_x[:, 0, t * P:(t + 1) * P], scale_t[:, t].rearrange("p j r -> p (j r)"), idn[:])
                mm.then_inc(scale_mm, 1)

            for k in range(3):
                if k:
                    pe.wait_ge(k_lo, k)
                for part in range(3):
                    project_k(part, k)
            for t in range(KT):
                if t == 0:
                    pe.wait_ge(k_lo, 3)
                else:
                    pe.wait_ge(v_copied, t)
                for part in range(3):
                    project_v(part, t)

            pe.wait_ge(ready, 3 + G)
            pe.wait_ge(c_in, 64)
            with pe.Fori(0, B) as b:
                M0 = b * (STEPS + 1)
                pe.wait_ge(qst_in, 192 * b + 192)
                pe.wait_ge(kst_in[0], b * (96 * STEPS) + 384)
                for k in range(16):
                    max_scores(M0, 0, k)
                pe.wait_ge(shift_in, M0 + 1)
                shift_rows(M0)
                pe.wait_ge(o_added, b * (STEPS + 1) + 1)
                pe.wait_ge(exp_done, b * (16 * STEPS) + 16)
                for j in range(HG):
                    c = (3 * HG + j) * HD
                    pe.matmul(ps_o[j * HD:(j + 1) * HD, 0, :], val[:, 0, 0, c:c + HD], prob[:, 3, j, :],
                              start=True, stop=False)
                with pe.Fori(0, CH // 2) as c2:
                    for u in range(2):
                        for g in range(G):
                            C = b * CH + c2 * 2 + u
                            N = C * G + g
                            M = N + b + 1
                            score = lambda t, j: scores(N, g, t, j)
                            peak = lambda k: max_scores(M, (g + 1) % G, k)

                            pe.wait_ge(kst_in[(g + 1) % 2], n_stacked(C, g + 1))
                            peak(0)
                            pe.wait_ge(v_copied, N + 4)
                            project_k(0, (g + 3) % G)
                            peak(1)
                            pe.wait_ge(shift_in, N + b + 2)
                            score(0, 0)
                            pe.wait_ge(shift_in_2, 3 * (N + b) + 2)
                            score(0, 1)
                            peak(2)
                            values(N - 1, u if g else 1 - u, (g + 3) % G, 3)
                            peak(3)
                            pe.wait_ge(shift_in_2, 3 * (N + b) + 3)
                            score(0, 2)
                            project_k(1, (g + 3) % G)
                            peak(4)
                            pe.wait_ge(shift_in_2, 3 * (N + b) + 4)
                            score(0, 3)
                            scale_rows(N, b)
                            peak(5)
                            project_k(2, (g + 3) % G)
                            peak(6)
                            score(1, 0)
                            pe.wait_ge(o_added, n_added(N, b))
                            peak(7)
                            values(N, u, g, 0)
                            peak(8)
                            score(1, 1)
                            score(1, 2)
                            peak(9)
                            denominators(N, b)
                            peak(10)
                            score(1, 3)
                            score(2, 0)
                            peak(11)
                            pe.wait_ge(k_lo, N + 4)
                            if g == 0:
                                pe.wait_ge(ctx_hi, 2 * C + 2)
                            project_v(0, g)
                            peak(12)
                            score(2, 1)
                            peak(13)
                            values(N, u, g, 1)
                            peak(14)
                            score(2, 2)
                            score(2, 3)
                            peak(15)
                            project_v(1, g)
                            score(3, 0)
                            if g == 0:
                                pe.wait_ge(ctx_lo, DT * (C + 1))
                            project_v(2, g)
                            pe.wait_ge(scale_in, N + 1)
                            shift_rows(M)
                            score(3, 1)
                            values(N, u, g, 2)
                            score(3, 2)
                            score(3, 3)
                N = (b + 1) * STEPS
                values(N - 1, 1, G - 1, 3)
                denominators(N, b)


class Merge:

    def __init__(self, nc, ctx, tag):
        sb = lambda name, shape, dt=F32: ctx.enter_context(nc.sbuf_tensor(f"{tag}_{name}", shape, dt))
        sem = lambda name: ctx.enter_context(nc.semaphore(f"{tag}_{name}"))
        self.ps = ctx.enter_context(nc.psum_tensor(f"{tag}_ps_merge", [P, 2, 512], F32))
        self.y, self.bias = sb("y", [P, NT, D]), sb("bias", [P, D])
        self.o, self.oh, self.ol = sb("o", [P, B, G, T]), sb("oh", [P, B, G, T], F32R), sb("ol", [P, B, G, T], F32R)
        self.w, self.wh, self.wl = sb("w", [P, DT, D]), sb("wh", [P, DT, D], F32R), sb("wl", [P, DT, D], F32R)
        self.w_in, self.bias_in = sem("w_in"), sem("bias_in")
        self.o_in, self.y_in = [sem(f"o_in{b}") for b in range(B)], [sem(f"y_in{b}") for b in range(B)]
        self.wh_done, self.wl_done, self.oh_done, self.ol_done = sem("wh_done"), sem("wl_done"), sem("oh_done"), sem("ol_done")
        self.biased, self.mm, self.y_done = sem("biased"), sem("mm"), sem("y_done")

    def sync_1_load(self, sp, x, attended, w, bias):
        sp.dma_start(self.w[:], w).then_inc(self.w_in, 16)
        sp.dma_start(self.bias[:], bias.partition_broadcast(P)).then_inc(self.bias_in, 16)
        for b in range(B):
            sp.dma_start(self.o[:, b], attended[b]).then_inc(self.o_in[b], 16)
            sp.dma_start(self.y[:, TT * b:TT * (b + 1), :], x[b].rearrange("(t p) d -> p t d", p=P)).then_inc(self.y_in[b], 16)

    def scalar_2_hi(self, act):
        act.wait_ge(self.w_in, 16)
        act.activation(self.wh[:], self.w[:], ACT.Copy).then_inc(self.wh_done, 1)
        for b in range(B):
            act.wait_ge(self.o_in[b], 16)
            act.activation(self.oh[:, b], self.o[:, b], ACT.Copy).then_inc(self.oh_done, 1)

    def gpsimd_2_bias(self, pool):
        pool.wait_ge(self.bias_in, 16)
        for b in range(B):
            pool.wait_ge(self.y_in[b], 16)
            for i in range(TT * b, TT * (b + 1)):
                pool.tensor_tensor(self.y[:, i, :], self.y[:, i, :], self.bias[:], ALU.add).then_inc(self.biased, 1)

    def vector_3_lo(self, dve):
        dve.wait_ge(self.wh_done, 1)
        dve.tensor_tensor(self.wl[:], self.w[:], fp(self.wh[:]), ALU.subtract).then_inc(self.wl_done, 1)
        for b in range(B):
            dve.wait_ge(self.oh_done, b + 1)
            dve.tensor_tensor(self.ol[:, b], self.o[:, b], fp(self.oh[:, b]), ALU.subtract).then_inc(self.ol_done, 1)

    def tensor_4_product(self, pe):
        pe.wait_ge(self.wl_done, 1)
        for i in range(NT):
            b, t = i // TT, i % TT
            pe.wait_ge(self.ol_done, b + 1)
            if i >= 2:
                pe.wait_ge(self.y_done, i - 1)
            exact_product(pe, self.ps[:, i % 2, :], lambda part, d: (self.oh, self.ol)[part][:, b, d, t * P:(t + 1) * P],
                          lambda part, d: (self.wh, self.wl)[part][:, d, :]).then_inc(self.mm, 1)

    def vector_5_add(self, dve, i):
        dve.wait_ge(self.mm, i + 1)
        dve.wait_ge(self.biased, i + 1)
        dve.tensor_tensor(self.y[:, i, :], self.ps[:, i % 2, :], self.y[:, i, :], ALU.add).then_inc(self.y_done, 1)
        dve.wait_ge(self.y_done, i + 1)


def project_self(nc, x, attended, wo, bo, w_qkv, cos, sin, ident, x1, qk_split, v_out):
    with ExitStack() as ctx:
        sb = lambda name, shape, dt=F32: ctx.enter_context(nc.sbuf_tensor(name, shape, dt))
        sem = lambda name: ctx.enter_context(nc.semaphore(name))
        idn = sb("c_id", [P, P])
        merge = Merge(nc, ctx, "cm")
        ps_e = ctx.enter_context(nc.psum_tensor("c_ps_pair", [P, 2, 2, 512], F32))
        norm = Norm(nc, ctx, "cn", merge.y, idn)
        table = sb("c_table", [P, 2, 2, T])
        own = sb("c_qh", [P, DT, D], F32R), sb("c_ql", [P, DT, D], F32R)
        parts = own, (merge.wh, merge.wl), own
        prod = sb("c_prod", [P, 4, T])
        part_h, part_l = sb("c_part_h", [P, 2, 2, T], F32R), sb("c_part_l", [P, 2, 2, T], F32R)
        turned_qk = sb("c_turned", [P, 2, T])
        val = sb("c_val", [P, 2, D])
        c_in, w_in = sem("c_c_in"), sem("c_w2_in")
        wh_done, wl_done = sem("c_wh2_done"), sem("c_wl2_done")
        pair_mm, mults, turns, ph_done, pl_done = (sem("c_pair_mm"), sem("c_mults"), sem("c_turns"), sem("c_ph_done"), sem("c_pl_done"))
        v_mm, v_done = sem("c_v_mm"), sem("c_v_done")
        parts_out = [sem("c_parts_out0"), sem("c_parts_out1")]
        v_sent, x1_out = [sem("c_v_sent0"), sem("c_v_sent1")], sem("c_x1_out")
        block = ctx.enter_context(nc.Block())
        PAIRS = 2 * B * 2

        @block.sync
        def _(sp):
            sp.dma_start(idn[:], ident).then_inc(c_in, 16)
            sp.dma_start(table[:, 0], cos).then_inc(c_in, 16)
            sp.dma_start(table[:, 1], sin).then_inc(c_in, 16)
            merge.sync_1_load(sp, x, attended, wo, bo)
            sp.wait_ge(merge.wl_done, 1)
            sp.dma_start(merge.w[:], w_qkv[0]).then_inc(w_in, 16)
            sp.wait_ge(wl_done, 1)
            sp.dma_start(merge.w[:], w_qkv[1]).then_inc(w_in, 16)
            for b in range(B):
                sp.wait_ge(merge.y_done, TT * (b + 1))
                sp.dma_start(x1[b].rearrange("(t p) d -> p t d", p=P), merge.y[:, TT * b:TT * (b + 1), :]).then_inc(x1_out, 16)
            sp.wait_ge(wl_done, 2)
            sp.dma_start(merge.w[:], w_qkv[2]).then_inc(w_in, 16)
            for m in range(PAIRS):
                which, b, e = m // (2 * B), (m // 2) % B, m % 2
                for r in range(2):
                    rows = slice(r * HD // 2, (r + 1) * HD // 2)
                    for part, src, done in ((0, part_h, ph_done), (1, part_l, pl_done)):
                        sp.wait_ge(done, 2 * m + r + 1)
                        dst = qk_split[b, which, part, 2 * e:2 * e + 2, :, rows].rearrange("g j r t -> (g j) r t")
                        sp.dma_start(dst, fp(src[:, m % 2, r, :])).then_inc(parts_out[m % 2], 16)
            for i in range(NT):
                sp.wait_ge(v_done, i + 1)
                sp.dma_start(v_out[i // TT, :, i % TT, :], val[:, i % 2, :]).then_inc(v_sent[i % 2], 16)
            sp.wait_ge(x1_out, 16 * B)
            for out in parts_out:
                sp.wait_ge(out, 32 * PAIRS)
            for sent in v_sent:
                sp.wait_ge(sent, 8 * NT)

        @block.gpsimd
        def _(pool):
            merge.gpsimd_2_bias(pool)
            for m in range(PAIRS):
                pool.wait_ge(mults, 4 * m + 2)
                if m:
                    pool.wait_ge(pl_done, 2 * m - 1)
                pool.tensor_tensor(turned_qk[:, 0], prod[:, 0], prod[:, 1], ALU.subtract).then_inc(turns, 1)
                pool.wait_ge(mults, 4 * m + 4)
                if m:
                    pool.wait_ge(pl_done, 2 * m)
                pool.tensor_tensor(turned_qk[:, 1], prod[:, 2], prod[:, 3], ALU.add).then_inc(turns, 1)

        @block.scalar
        def _(act):
            merge.scalar_2_hi(act)

            def weights(n):
                act.wait_ge(w_in, 16 * (n + 1))
                if n == 1:
                    act.wait_ge(merge.mm, NT)
                if n == 2:
                    act.wait_ge(pair_mm, PAIRS // 2)
                act.activation(parts[n][0][:], merge.w[:], ACT.Copy).then_inc(wh_done, 1)

            weights(0)
            norm.scalar_3_root(act)
            norm.scalar_6_hi(act)
            weights(1)
            for m in range(PAIRS):
                for r in range(2):
                    act.wait_ge(turns, 2 * m + r + 1)
                    if m >= 2:
                        act.wait_ge(parts_out[m % 2], 64 * (m // 2))
                    act.activation(part_h[:, m % 2, r, :], turned_qk[:, r], ACT.Copy).then_inc(ph_done, 1)
                if m == PAIRS // 2:
                    weights(2)
            for i in range(NT):
                act.wait_ge(v_mm, i + 1)
                if i >= 2:
                    act.wait_ge(v_sent[i % 2], 16 * (i // 2))
                act.copy(val[:, i % 2, :], ps_e[:, 0, i % 2, :]).then_inc(v_done, 1)

        @block.vector
        def _(dve):
            merge.vector_3_lo(dve)
            for i in range(NT):
                merge.vector_5_add(dve, i)
                norm.vector_1_stats(dve, i)
            norm.vector_2_variance(dve)

            def weights(n):
                dve.wait_ge(wh_done, n + 1)
                high, low = parts[n]
                dve.tensor_tensor(low[:], merge.w[:], fp(high[:]), ALU.subtract).then_inc(wl_done, 1)

            weights(0)
            norm.vector_4_apply(dve)
            norm.vector_7_lo(dve)
            weights(1)
            dve.wait_ge(c_in, 48)
            for m in range(PAIRS):
                e = m % 2
                dve.wait_ge(pair_mm, m + 1)
                if m:
                    dve.wait_ge(turns, 2 * m)
                for n, (half, tab) in enumerate(((0, 0), (1, 1), (0, 1), (1, 0))):
                    dve.tensor_tensor(prod[:, n], ps_e[:, m % 2, half, :], table[:, tab, e, :], ALU.mult).then_inc(mults, 1)
                for r in range(2):
                    dve.wait_ge(ph_done, 2 * m + r + 1)
                    dve.tensor_tensor(part_l[:, m % 2, r, :], turned_qk[:, r], fp(part_h[:, m % 2, r, :]),
                                      ALU.subtract).then_inc(pl_done, 1)
                if m == PAIRS // 2:
                    weights(2)

        @block.tensor
        def _(pe):
            pe.wait_ge(c_in, 48)
            merge.tensor_4_product(pe)
            norm.tensor_5_turn(pe)
            for m in range(PAIRS):
                b, e = (m // 2) % B, m % 2
                pe.wait_ge(wl_done, 1 + m // (2 * B))
                pe.wait_ge(norm.lo_done, DT * (b + 1))
                if m >= 2:
                    pe.wait_ge(mults, 4 * (m - 1))
                for half in range(2):
                    c = (2 * half + e) * P
                    mm = exact_product(pe, ps_e[:, m % 2, half, :], lambda part, d: parts[m // (2 * B)][part][:, d, c:c + P],
                                       lambda part, d: (norm.hi, norm.lo)[part][:, d, b * T:(b + 1) * T])
                mm.then_inc(pair_mm, 1)
            pe.wait_ge(wl_done, 3)
            for i in range(NT):
                if i < 2:
                    pe.wait_ge(mults, 4 * (PAIRS - 1))
                else:
                    pe.wait_ge(v_done, i - 1)
                exact_product(pe, ps_e[:, 0, i % 2, :], lambda part, d: (norm.hi, norm.lo)[part][:, d, i * P:(i + 1) * P],
                              lambda part, d: parts[2][part][:, d, :]).then_inc(v_mm, 1)


def self_attention(nc, qk_split, v_in, ident, onehot, attended):
    STEPS = B * G
    SLOTS = 3
    with ExitStack() as ctx:
        sb = lambda name, shape, dt=F32: ctx.enter_context(nc.sbuf_tensor(name, shape, dt))
        sem = lambda name: ctx.enter_context(nc.semaphore(name))
        bank = lambda name, n=1: ctx.enter_context(nc.psum_tensor(name, [P, n, 512], F32))
        ps_s, ps_m, ps_o, ps_d, ps_x = (bank("d_ps_score", 2), bank("d_ps_max", 2), bank("d_ps_out", 2),
                                        bank("d_ps_den"), bank("d_ps_turn"))
        idn, idr, ones = sb("d_idn", [P, P]), sb("d_idr", [P, P], F32R), sb("d_ones", [P, HD])
        hot = sb("d_hot", [P, HG, T])
        kst, qst = sb("d_kst", [P, SLOTS, HG, T], F32R), sb("d_qst", [P, SLOTS, HG, T], F32R)
        val = sb("d_val", [P, B, TT, D])
        prob, pair = sb("d_prob", [P, TT, HG, T]), sb("d_pair", [P, 2, HG, T])
        tile_max, nmax_w = sb("d_tile_max", [P, TT, HG]), sb("d_nmax_w", [P, TT, P], F32R)
        inv, out = sb("d_inv", [P, T]), sb("d_out", [P, 2, T])
        c_in, v_in_sem, zeroed, consts = sem("d_c_in"), sem("d_v_in"), sem("d_zeroed"), sem("d_consts")
        stack_in = [sem("d_stack_in0"), sem("d_stack_in1")]
        max_mm, max_read, wide = sem("d_max_mm"), sem("d_max_read"), sem("d_wide")
        shift_mm, shift_in = sem("d_shift_mm"), sem("d_shift_in")
        score_mm, exp_done, pv_mm, summed, den_mm = (sem("d_score_mm"), sem("d_exp_done"), sem("d_pv_mm"),
                                                     sem("d_summed"), sem("d_den_mm"))
        inv_done, out_done, out_sent = sem("d_inv_done"), sem("d_out_done"), [sem("d_out_sent0"), sem("d_out_sent1")]
        block = ctx.enter_context(nc.Block())

        @block.sync
        def _(sp):
            sp.dma_start(idn[:], ident).then_inc(c_in, 16)
            sp.dma_start(hot[STACK:P], onehot).then_inc(c_in, 16)

            def stacks(n):
                b, g = n // G, n % G
                for which, dst, order in ((1, kst, (0, 0, 1)), (0, qst, (0, 1, 0))):
                    for q, part in enumerate(order):
                        sp.dma_start(fp(dst[HD * q:HD * (q + 1), n % SLOTS]), qk_split[b, which, part, g].rearrange(
                            "j r t -> r j t")).then_inc(stack_in[n % 2], 16)

            stacks(0)
            for b in range(B):
                sp.dma_start(val[:, b], v_in[b]).then_inc(v_in_sem, 16)
            stacks(1)
            sp.wait_ge(max_mm, 1)
            stacks(2)
            for n in range(STEPS):
                if n + 3 < STEPS:
                    sp.wait_ge(score_mm, 16 * (n + 1))
                    stacks(n + 3)
                sp.wait_ge(out_done, n + 1)
                sp.dma_start(attended[n // G, :, n % G, :], out[:, n % 2, :]).then_inc(out_sent[n % 2], 16)
            for sent in out_sent:
                sp.wait_ge(sent, 8 * STEPS)

        @block.gpsimd
        def _(pool):
            for n in range(STEPS):
                for k in range(2):
                    pool.wait_ge(exp_done, 16 * n + 8 * k + 8)
                    if n:
                        pool.wait_ge(den_mm, n)
                    pool.tensor_tensor(pair[:, k], prob[:, 2 * k], prob[:, 2 * k + 1], ALU.add).then_inc(summed, 1)

        @block.scalar
        def _(act):
            act.wait_ge(c_in, 32)
            act.activation(idr[:], idn[:], ACT.Copy).then_inc(consts, 1)
            for s in range(SLOTS):
                act.activation(kst[STACK:P, s], hot[STACK:P], ACT.Copy).then_inc(consts, 1)

            def shift_copy(n, j):
                act.wait_ge(shift_mm, n + 1)
                act.activation(qst[STACK:ROWS, n % SLOTS, j], ps_x[STACK:ROWS, 0, :], ACT.Copy).then_inc(shift_in, 1)

            for j in range(HG):
                shift_copy(0, j)
            for n in range(STEPS):
                for t in range(TT):
                    for j in range(HG):
                        if n and j == 0:
                            act.wait_ge(pv_mm, 4 * (n - 1) + t + 1)
                            act.wait_ge(summed, 2 * (n - 1) + t // 2 + 1)
                        act.wait_ge(score_mm, 16 * n + 4 * t + j + 1)
                        act.activation(prob[:, t, j, :], ps_s[:, j % 2, :], ACT.Exp, scale=SCALE).then_inc(exp_done, 1)
                        if t == 3 and n + 1 < STEPS:
                            for head in ((), (0,), (1,), (2, 3))[j]:
                                shift_copy(n + 1, head)

        @block.vector
        def _(dve):
            dve.memset(ones[:], 1.0).then_inc(zeroed, 1)
            dve.memset(fp(nmax_w[:]), 0.0).then_inc(zeroed, 1)

            def maxima(n, first, count):
                for k in range(first, first + count):
                    dve.wait_ge(max_mm, 16 * n + k + 1)
                    dve.tensor_reduce(tile_max[:, k % TT, k // TT:k // TT + 1], ps_m[:, k % 2, :], AX_X, ALU.max,
                                      negate=True).then_inc(max_read, 1)

            def shift(n):
                dve.wait_ge(max_read, 16 * n + 16)
                if n:
                    dve.wait_ge(shift_mm, n)
                else:
                    dve.wait_ge(zeroed, 2)
                dve.tensor_copy(nmax_w[:, :, STACK:ROWS], tile_max[:]).then_inc(wide, 1)

            def inverse(n, q):
                dve.wait_ge(den_mm, n + 1)
                if n:
                    dve.wait_ge(out_done, n)
                tokens = slice(q * P, (q + 1) * P)
                dve.reciprocal(inv[:, tokens], ps_d[:, 0, tokens]).then_inc(inv_done, 1)

            def finish(n):
                dve.wait_ge(inv_done, TT * (n + 1))
                if n >= 2:
                    dve.wait_ge(out_sent[n % 2], 16 * (n // 2))
                dve.wait_ge(pv_mm, 4 * n + 4)
                dve.tensor_tensor(out[:, n % 2, :], ps_o[:, n % 2, :], inv[:], ALU.mult).then_inc(out_done, 1)

            maxima(0, 0, 16)
            shift(0)
            for n in range(STEPS):
                last = n + 1 == STEPS
                if not last:
                    maxima(n + 1, 0, 9)
                if n:
                    for q in range(TT):
                        inverse(n - 1, q)
                        if not last:
                            maxima(n + 1, 9 + q, 1)
                    finish(n - 1)
                elif not last:
                    maxima(n + 1, 9, 4)
                if not last:
                    maxima(n + 1, 13, 3)
                    shift(n + 1)
            for q in range(TT):
                inverse(STEPS - 1, q)
            finish(STEPS - 1)

        @block.tensor
        def _(pe):
            pe.wait_ge(zeroed, 2)
            pe.wait_ge(consts, 1 + SLOTS)

            def max_scores(n, k):
                s, j, t = n % SLOTS, k // TT, k % TT
                if 16 * n + k >= 2:
                    pe.wait_ge(max_read, 16 * n + k - 1)
                pe.matmul(ps_m[:, k % 2, :], qst[0:STACK, s, j, t * P:(t + 1) * P], kst[0:STACK, s, j, :],
                          start=True, stop=True).then_inc(max_mm, 1)

            def shift_rows(n):
                pe.wait_ge(wide, n + 1)
                for t in range(TT):
                    mm = pe.matmul(ps_x[:, 0, t * P:(t + 1) * P], nmax_w[:, t, :], idr[:], start=True, stop=True)
                mm.then_inc(shift_mm, 1)

            def values(n, t):
                pe.wait_ge(exp_done, 16 * n + 4 * t + 4)
                for j in range(HG):
                    c = ((n % G) * HG + j) * HD
                    mm = pe.matmul(ps_o[j * HD:(j + 1) * HD, n % 2, :], val[:, n // G, t, c:c + HD], prob[:, t, j, :],
                                   start=(t == 0), stop=(t == TT - 1))
                mm.then_inc(pv_mm, 1)

            def denominators(n):
                pe.wait_ge(summed, 2 * n + 2)
                if n:
                    pe.wait_ge(inv_done, TT * n)
                for k in range(2):
                    for j in range(HG):
                        mm = pe.matmul(ps_d[j * HD:(j + 1) * HD, 0, :], ones[:], pair[:, k, j, :], start=(k == 0), stop=(k == 1))
                mm.then_inc(den_mm, 1)

            def scores(n, t, j):
                if 16 * n + 4 * t + j >= 2:
                    pe.wait_ge(exp_done, 16 * n + 4 * t + j - 1)
                pe.matmul(ps_s[:, j % 2, :], kst[0:ROWS, n % SLOTS, j, t * P:(t + 1) * P], qst[0:ROWS, n % SLOTS, j, :],
                          start=True, stop=True).then_inc(score_mm, 1)

            pe.wait_ge(stack_in[0], 96)
            for k in range(16):
                max_scores(0, k)
            shift_rows(0)
            pe.wait_ge(v_in_sem, 16 * B)
            for n in range(STEPS):
                last = n + 1 == STEPS
                peak = lambda k: None if last else max_scores(n + 1, k)
                if not last:
                    pe.wait_ge(stack_in[(n + 1) % 2], 96 * ((n + 1) // 2 + 1))
                peak(0)
                peak(1)
                peak(2)
                for j in range(HG):
                    pe.wait_ge(shift_in, HG * n + j + 1)
                    scores(n, 0, j)
                    if n and j == 0:
                        values(n - 1, 3)
                    peak(3 + j)
                scores(n, 1, 0)
                peak(7)
                scores(n, 1, 1)
                if n:
                    denominators(n - 1)
                peak(8)
                scores(n, 1, 2)
                peak(9)
                scores(n, 1, 3)
                if n >= 2:
                    pe.wait_ge(out_done, n - 1)
                values(n, 0)
                peak(10)
                scores(n, 2, 0)
                scores(n, 2, 1)
                peak(11)
                values(n, 1)
                peak(12)
                scores(n, 2, 2)
                peak(13)
                scores(n, 2, 3)
                peak(14)
                scores(n, 3, 0)
                peak(15)
                values(n, 2)
                scores(n, 3, 1)
                if not last:
                    shift_rows(n + 1)
                scores(n, 3, 2)
                scores(n, 3, 3)
            values(STEPS - 1, 3)
            denominators(STEPS - 1)


def experts(nc, x1, attended, wu, bu, ident, router_w, router_b, index, expert_w, expert_b, out):
    with ExitStack() as ctx:
        sb = lambda name, shape, dt=F32: ctx.enter_context(nc.sbuf_tensor(name, shape, dt))
        sem = lambda name: ctx.enter_context(nc.semaphore(name))
        idn = sb("e_id", [P, P])
        ps_y = ctx.enter_context(nc.psum_tensor("e_ps_y", [P, 2, 512], F32))
        ps_r = ctx.enter_context(nc.psum_tensor("e_ps_router", [P, 512], F32))
        ps_c = ctx.enter_context(nc.psum_tensor("e_ps_coef", [P, 512], F32))
        merge = Merge(nc, ctx, "em")
        norm = Norm(nc, ctx, "en", merge.y, idn)
        rw, rwh, rwl = sb("e_rw", [P, DT, E]), sb("e_rwh", [P, DT, E], F32R), sb("e_rwl", [P, DT, E], F32R)
        rb, idx8, eb = sb("e_rb", [P, NT, E]), sb("e_idx", [P, NT, E]), sb("e_eb", [E, D])
        logit, top = sb("e_logit", [P, NT, E]), sb("e_top", [P, NT])
        ex, total, gate = sb("e_ex", [P, NT, E]), sb("e_total", [P, NT]), sb("e_gate", [P, NT])
        pick, first, coef = sb("e_pick", [P, NT, E]), sb("e_first", [P, NT]), sb("e_coef", [P, NT, E])
        coef_t = sb("e_coef_t", [E, B * T])
        raw = sb("e_raw", [P, DT, D])
        wh, wl = sb("e_wh", [P, 2, DT, D], F32R), sb("e_wl", [P, 2, DT, D], F32R)
        c_in, raw_in = sem("e_c_in"), sem("e_raw_in")
        rwh_done, rwl_done, chain, router_mm, ex_done = sem("e_rwh_done"), sem("e_rwl_done"), sem("e_chain"), sem("e_router_mm"), sem("e_ex_done")
        coef_done, coef_mm, coef_in, bias_mm, based = sem("e_coef_done"), sem("e_coef_mm"), sem("e_coef_in"), sem("e_bias_mm"), sem("e_based")
        wh_done, wl_done, y_mm, y_read = sem("e_wh2_done"), sem("e_wl2_done"), sem("e_y_mm"), sem("e_y_read")
        sent = sem("e_sent")
        block = ctx.enter_context(nc.Block())

        @block.sync
        def _(sp):
            sp.dma_start(idn[:], ident).then_inc(c_in, 16)
            sp.dma_start(rw[:], router_w).then_inc(c_in, 16)
            sp.dma_start(rb[:], router_b.partition_broadcast(P)).then_inc(c_in, 16)
            sp.dma_start(idx8[:], index.partition_broadcast(P)).then_inc(c_in, 16)
            sp.dma_start(eb[:], expert_b).then_inc(c_in, 16)
            merge.sync_1_load(sp, x1, attended, wu, bu)
            sp.dma_start(raw[:], expert_w[0]).then_inc(raw_in, 16)
            with sp.Fori(1, E) as e:
                sp.wait_ge(wl_done, e)
                sp.dma_start(raw[:], expert_w[bass.ds(e, 1)].rearrange("o p d n -> (o p) d n")).then_inc(raw_in, 16)
            for b in range(B):
                sp.wait_ge(y_read, NT * (E - 1) + TT * (b + 1))
                sp.dma_start(out[b].rearrange("(t p) d -> p t d", p=P), merge.y[:, TT * b:TT * (b + 1), :]).then_inc(sent, 16)
            sp.wait_ge(sent, 16 * B)

        @block.gpsimd
        def _(pool):
            merge.gpsimd_2_bias(pool)

        @block.scalar
        def _(act):
            act.wait_ge(c_in, 80)
            act.activation(rwh[:], rw[:], ACT.Copy).then_inc(rwh_done, 1)
            merge.scalar_2_hi(act)
            norm.scalar_3_root(act)
            norm.scalar_6_hi(act)

            def weights(e, slot, free=None):
                act.wait_ge(raw_in, 16 * e + 16)
                if free is not None:
                    act.wait_ge(y_mm, free)
                act.activation(wh[:, slot], raw[:], ACT.Copy).then_inc(wh_done, 1)

            weights(0, 0)
            act.wait_ge(chain, 3)
            act.activation(ex[:], pick[:], ACT.Exp).then_inc(ex_done, 1)
            act.wait_ge(coef_mm, 1)
            act.copy(coef_t[:, 0:T], ps_c[0:E, :]).then_inc(coef_in, 1)
            act.wait_ge(coef_mm, 2)
            act.copy(coef_t[:, T:2 * T], ps_c[0:E, :]).then_inc(coef_in, 1)
            weights(1, 1)
            with act.Fori(0, E // 2 - 1) as h:
                for slot in range(2):
                    weights(2 * h + 2 + slot, slot, NT * (2 * h + 1 + slot))

        @block.vector
        def _(dve):
            dve.wait_ge(rwh_done, 1)
            dve.tensor_tensor(rwl[:], rw[:], fp(rwh[:]), ALU.subtract).then_inc(rwl_done, 1)
            merge.vector_3_lo(dve)
            for i in range(NT):
                merge.vector_5_add(dve, i)
                norm.vector_1_stats(dve, i)
            norm.vector_2_variance(dve)
            norm.vector_4_apply(dve)
            norm.vector_7_lo(dve)

            def weights(e, slot):
                dve.wait_ge(wh_done, e + 1)
                dve.tensor_tensor(wl[:, slot], raw[:], fp(wh[:, slot]), ALU.subtract).then_inc(wl_done, 1)

            steps = [0]

            def link(ins):
                steps[0] += 1
                ins.then_inc(chain, 1)
                dve.wait_ge(chain, steps[0])

            weights(0, 0)
            wide = lambda small: small[:].unsqueeze(2).to_broadcast([P, NT, E])
            dve.wait_ge(router_mm, 1)
            link(dve.tensor_tensor(logit[:], ps_r[:, 0:NT * E].rearrange("p (n e) -> p n e", n=NT), rb[:], ALU.add))
            link(dve.tensor_reduce(top[:], logit[:], AX_X, ALU.max))
            link(dve.tensor_tensor(pick[:], logit[:], wide(top), ALU.subtract))
            dve.wait_ge(ex_done, 1)
            link(dve.tensor_reduce(total[:], ex[:], AX_X, ALU.add))
            link(dve.reciprocal(gate[:], total[:]))
            link(dve.tensor_scalar(logit[:], pick[:], 0.0, -float(E), ALU.is_ge, ALU.mult))
            link(dve.tensor_tensor(pick[:], logit[:], idx8[:], ALU.add))
            link(dve.tensor_reduce(first[:], pick[:], AX_X, ALU.min))
            link(dve.tensor_tensor(logit[:], pick[:], wide(first), ALU.is_equal))
            dve.tensor_tensor(coef[:], logit[:], wide(gate), ALU.mult).then_inc(coef_done, 1)
            for i in range(NT):
                dve.wait_ge(bias_mm, i + 1)
                dve.tensor_tensor(merge.y[:, i, :], ps_y[:, i % 2, :], merge.y[:, i, :], ALU.add).then_inc(based, 1)
            weights(1, 1)
            dve.wait_ge(based, NT)

            def add(e, i):
                dve.wait_ge(y_mm, e * NT + i + 1)
                if not isinstance(e, int) or e:
                    dve.wait_ge(y_read, (e - 1) * NT + i + 1)
                dve.scalar_tensor_tensor(merge.y[:, i, :], ps_y[:, i % 2, :], coef[:, i, bass.ds(e, 1)] if not isinstance(e, int)
                                         else coef[:, i, e:e + 1], merge.y[:, i, :], ALU.mult, ALU.add).then_inc(y_read, 1)

            def expert(e, slot):
                add(e, 0)
                weights(e + 1, slot)
                for i in range(1, NT):
                    add(e, i)

            for i in range(NT):
                add(0, i)
            with dve.Fori(0, E // 2 - 1) as h:
                for slot in range(2):
                    expert(2 * h + 1 + slot, slot)
            for i in range(NT):
                add(E - 1, i)

        @block.tensor
        def _(pe):
            pe.wait_ge(c_in, 80)
            merge.tensor_4_product(pe)
            norm.tensor_5_turn(pe)
            pe.wait_ge(rwl_done, 1)
            pe.wait_ge(norm.lo_done, B * DT)
            for i in range(NT):
                mm = exact_product(pe, ps_r[:, i * E:(i + 1) * E], lambda part, d: (norm.hi, norm.lo)[part][:, d, i * P:(i + 1) * P],
                                   lambda part, d: (rwh, rwl)[part][:, d, :])
            mm.then_inc(router_mm, 1)
            pe.wait_ge(coef_done, 1)
            for b in range(B):
                if b:
                    pe.wait_ge(coef_in, b)
                for t in range(TT):
                    mm = pe.transpose(ps_c[0:E, t * P:(t + 1) * P], coef[:, b * TT + t, :], idn[:])
                mm.then_inc(coef_mm, 1)
            pe.wait_ge(coef_in, B)
            for i in range(NT):
                if i >= 2:
                    pe.wait_ge(based, i - 1)
                pe.matmul(ps_y[:, i % 2, :], coef_t[:, i * P:(i + 1) * P], eb[:], start=True, stop=True).then_inc(bias_mm, 1)

            def apply(e, slot, first=False):
                pe.wait_ge(wl_done, e + 1)
                for i in range(NT):
                    if first and i < 2:
                        pe.wait_ge(based, NT)
                    else:
                        pe.wait_ge(y_read, e * NT + i - 1)
                    exact_product(pe, ps_y[:, i % 2, :], lambda part, d: (norm.hi, norm.lo)[part][:, d, i * P:(i + 1) * P],
                                  lambda part, d: (wh, wl)[part][:, slot, d, :]).then_inc(y_mm, 1)

            apply(0, 0, True)
            apply(1, 1)
            with pe.Fori(0, E // 2 - 1) as h:
                for slot in range(2):
                    apply(2 * h + 2 + slot, slot)


def perceiver_block(nc, a, out):
    scratch = lambda name, shape: nc.dram_tensor(name, shape, F32, kind="Internal").ap()
    q_split = scratch("q_split", [B, 2, G, P, T])
    crossed, selfed = scratch("crossed", [B, P, G, T]), scratch("selfed", [B, P, G, T])
    x1, v_self = scratch("x1", [B, T, D]), scratch("v_self", [B, P, TT, D])
    qk_split = scratch("qk_split", [B, 2, 2, G, HG, HD, T])
    with ExitStack() as ctx:
        proj = Projection(nc, ctx)
        project_queries(nc, proj, a["x"], a["x_wq"], a["x_bq"], a["ident"], a["x_wk"], a["x_wv"], a["ctx_t"], q_split)
        cross_attention(nc, proj, a["ctx_t"], a["x_bk"], a["x_bv"], a["ident"], a["onehot"], q_split,
                        crossed, a["ctx_t"].shape[0] // B)
    project_self(nc, a["x"], crossed, a["x_wo"], a["x_bo"], a["w_qkv"], a["cos"], a["sin"], a["ident"], x1, qk_split, v_self)
    self_attention(nc, qk_split, v_self, a["ident"], a["onehot"], selfed)
    experts(nc, x1, selfed, a["s_wu"], a["s_bu"], a["ident"], a["router_w"], a["router_b"], a["index"], a["expert_w"],
            a["expert_b"], out)


def kernel(**inputs):
    import numpy as np
    import concourse.bacc as bacc
    from concourse.bass_utils import run_bass_kernel_spmd

    x = {k: np.asarray(v) for k, v in inputs.items()}
    tiles = lambda w: np.ascontiguousarray(w.reshape(DT, P, -1).transpose(1, 0, 2))
    column = lambda v: np.ascontiguousarray(v.reshape(DT, P).T)
    row = lambda v: np.ascontiguousarray(v.reshape(1, -1))
    halves = lambda w: np.concatenate([w[0::2], w[1::2]])
    ctx = x["ctx_1024"]
    chunks = ctx.shape[1] // KC
    half = D // 2
    theta = np.float32(1.0) / np.float32(10000.0) ** (np.arange(half, dtype=np.float32) / np.float32(half))
    angle = np.arange(T, dtype=np.float32)[:, None] * theta[None, :]
    onehot = np.zeros((P - STACK, HG, T), np.float32)
    for j in range(HG):
        onehot[j, j] = 1.0
    turn = lambda v: np.ascontiguousarray(v.astype(np.float32).T.reshape(2, P, T).transpose(1, 0, 2))
    arrays = {
        "x": x["x"],
        "ctx_t": np.ascontiguousarray(ctx.reshape(B, chunks, KC, DT, P).transpose(0, 1, 4, 3, 2)).reshape(B * chunks, P, DT, KC),
        "x_wq": tiles(x["L0_xattn_Wq"].T), "x_bq": column(x["L0_xattn_bq"]),
        "x_wk": tiles(x["L0_xattn_Wk"].T), "x_bk": column(x["L0_xattn_bk"]),
        "x_wv": tiles(x["L0_xattn_Wv"].T), "x_bv": column(x["L0_xattn_bv"]),
        "x_wo": tiles(x["L0_xattn_Wo"].T), "x_bo": row(x["L0_xattn_bo"]),
        "w_qkv": np.stack([tiles(halves(x["L0_attn_Wq"]).T), tiles(halves(x["L0_attn_Wk"]).T), tiles(x["L0_attn_Wv"].T)]),
        "cos": turn(np.cos(angle)), "sin": turn(np.sin(angle)),
        "s_wu": tiles(x["L0_attn_Wu"].T), "s_bu": row(x["L0_attn_bu"]),
        "router_w": tiles(x["L0_ffn_router_w"]), "router_b": np.ascontiguousarray(np.tile(x["L0_ffn_router_b"], NT)).reshape(1, NT, E),
        "index": (np.arange(NT * E, dtype=np.float32) % E + E).reshape(1, NT, E).astype(np.float32),
        "expert_w": np.ascontiguousarray(x["L0_ffn_expert_w"].reshape(E, DT, P, D).transpose(0, 2, 1, 3)),
        "expert_b": x["L0_ffn_expert_b"],
        "ident": np.eye(P, dtype=np.float32), "onehot": onehot,
    }
    nc = bacc.Bacc("TRN2", target_bir_lowering=False, num_devices=1)
    ins, feed = {}, {}
    for name, a in arrays.items():
        feed[f"in_{name}"] = np.ascontiguousarray(a)
        ins[name] = nc.dram_tensor(f"in_{name}", a.shape, F32, kind="ExternalInput").ap()
    out = nc.dram_tensor("out", (B, T, D), F32, kind="ExternalOutput").ap()
    perceiver_block(nc, ins, out)
    r = run_bass_kernel_spmd(nc, [feed], core_ids=[0])
    return r.results[0]["out"]
```

```python
from contextlib import ExitStack

import concourse.bass as bass
from concourse import mybir

F32 = mybir.dt.float32
F32R = mybir.dt.float32r
ALU = mybir.AluOpType
ACT = mybir.ActivationFunctionType
AX_X = mybir.AxisListType.X

P = 128
B = 2
T = 512
D = 512
DT = D // P
H = 16
HD = D // H
HG = P // HD
G = H // HG
KC = 512
KT = KC // P
TT = T // P
SCALE = float(HD) ** -0.5
EPS = 1e-5
STACK = 3 * HD
NT = B * TT
E = 8
ROWS = STACK + HG
BIG = 1e30


def fp(ap):
    return ap.bitcast(F32)


class Norm:

    def __init__(self, nc, ctx, tag, x, ident):
        sb = lambda name, shape, dt=F32: ctx.enter_context(nc.sbuf_tensor(f"{tag}_{name}", shape, dt))
        sem = lambda name: ctx.enter_context(nc.semaphore(f"{tag}_{name}"))
        self.x, self.ident = x, ident
        self.ps = ctx.enter_context(nc.psum_tensor(f"{tag}_ps_turn", [P, 2, 512], F32))
        self.xn = sb("xn", [P, NT, D])
        self.hi, self.lo = sb("nh", [P, DT, B * T], F32R), sb("nl", [P, DT, B * T], F32R)
        self.stats, self.mv, self.var = sb("stats", [P, NT, 6]), sb("mv", [P, NT, 2]), sb("var", [P, NT])
        self.std, self.rstd, self.work = sb("std", [P, NT]), sb("rstd", [P, NT]), sb("work", [P, NT])
        self.vector_steps, self.std_done, self.xn_done = sem("vector_steps"), sem("std_done"), sem("xn_done")
        self.turned, self.hi_done, self.lo_done = sem("turned"), sem("hi_done"), sem("lo_done")

    def vector_1_stats(self, dve, i):
        dve.bn_stats(self.stats[:, i, :], self.x[:, i, :]).then_inc(self.vector_steps, 1)

    def vector_2_variance(self, dve, b):
        before, tiles = (2 * TT + 6) * b, slice(TT * b, TT * (b + 1))
        for t in range(TT):
            dve.wait_ge(self.vector_steps, before + TT + t)
            dve.bn_aggr(self.mv[:, TT * b + t, :], self.stats[:, TT * b + t, :]).then_inc(self.vector_steps, 1)
        dve.wait_ge(self.vector_steps, before + 2 * TT)
        dve.tensor_scalar(self.var[:, tiles], self.mv[:, tiles, 1], EPS, None, ALU.add).then_inc(self.vector_steps, 1)

    def scalar_3_root(self, act, b):
        tiles = slice(TT * b, TT * (b + 1))
        act.wait_ge(self.vector_steps, (2 * TT + 6) * b + 2 * TT + 1)
        act.activation(self.std[:, tiles], self.var[:, tiles], ACT.Sqrt).then_inc(self.std_done, 1)

    def vector_4_apply(self, dve, b):
        before, tiles = (2 * TT + 6) * b + 2 * TT, slice(TT * b, TT * (b + 1))
        y, w, var, step = self.rstd[:, tiles], self.work[:, tiles], self.var[:, tiles], self.vector_steps
        dve.wait_ge(self.std_done, b + 1)
        dve.reciprocal(y, self.std[:, tiles]).then_inc(step, 1)
        dve.wait_ge(step, before + 2)
        dve.tensor_tensor(w, y, y, ALU.mult).then_inc(step, 1)
        dve.wait_ge(step, before + 3)
        dve.tensor_tensor(w, w, var, ALU.mult).then_inc(step, 1)
        dve.wait_ge(step, before + 4)
        dve.tensor_scalar(w, w, -0.5, 1.5, ALU.mult, ALU.add).then_inc(step, 1)
        dve.wait_ge(step, before + 5)
        dve.tensor_tensor(y, y, w, ALU.mult).then_inc(step, 1)
        dve.wait_ge(step, before + 6)
        for i in range(TT * b, TT * (b + 1)):
            dve.tensor_scalar(self.xn[:, i, :], self.x[:, i, :], self.mv[:, i, 0:1], self.rstd[:, i:i + 1],
                              ALU.subtract, ALU.mult).then_inc(self.xn_done, 1)

    def tensor_5_turn(self, pe, b):
        for k in range(DT * b, DT * (b + 1)):
            d = k % DT
            pe.wait_ge(self.xn_done, TT * (b + 1))
            if k >= 2:
                pe.wait_ge(self.lo_done, k - 1)
            for t in range(TT):
                mm = pe.transpose(self.ps[:, k % 2, t * P:(t + 1) * P],
                                  self.xn[:, b * TT + t, d * P:(d + 1) * P], self.ident[:])
            mm.then_inc(self.turned, 1)

    def _tokens(self, k):
        return slice((k // DT) * T, (k // DT + 1) * T)

    def scalar_6_hi(self, act, b):
        for k in range(DT * b, DT * (b + 1)):
            act.wait_ge(self.turned, k + 1)
            act.activation(self.hi[:, k % DT, self._tokens(k)], self.ps[:, k % 2, :], ACT.Copy).then_inc(self.hi_done, 1)

    def vector_7_lo(self, dve, b):
        for k in range(DT * b, DT * (b + 1)):
            dve.wait_ge(self.hi_done, k + 1)
            s = self._tokens(k)
            dve.tensor_tensor(self.lo[:, k % DT, s], self.ps[:, k % 2, :], fp(self.hi[:, k % DT, s]),
                              ALU.subtract).then_inc(self.lo_done, 1)


def exact_product(pe, out, left, right):
    for n, (lp, rp) in enumerate(((0, 0), (0, 1), (1, 0))):
        for d in range(DT):
            mm = pe.matmul(out, left(lp, d), right(rp, d), start=(n == 0 and d == 0), stop=(n == 2 and d == DT - 1))
    return mm


class Projection:

    def __init__(self, nc, ctx):
        sb = lambda name, shape, dt=F32: ctx.enter_context(nc.sbuf_tensor(name, shape, dt))
        self.wkh, self.wkl = sb("wkh", [P, DT, D], F32R), sb("wkl", [P, DT, D], F32R)
        self.wvh, self.wvl = sb("wvh", [P, DT, D], F32R), sb("wvl", [P, DT, D], F32R)
        self.raw = sb("raw", [P, DT, KC])
        self.chi, self.clo = sb("chi", [P, DT, KC], F32R), sb("clo", [P, DT, KC], F32R)


def project_queries(nc, proj, x, wq, bq, ident, wk, wv, ctx_t, q_split):
    with ExitStack() as ctx:
        sb = lambda name, shape, dt=F32: ctx.enter_context(nc.sbuf_tensor(name, shape, dt))
        sem = lambda name: ctx.enter_context(nc.semaphore(name))
        ps_q = ctx.enter_context(nc.psum_tensor("a_ps_q", [P, 2, 512], F32))
        xs, idn, bias = sb("a_x", [P, NT, D]), sb("a_id", [P, P]), sb("a_b", [P, DT])
        w, wh, wl = sb("a_w", [P, DT, D]), sb("a_wh", [P, DT, D], F32R), sb("a_wl", [P, DT, D], F32R)
        qh, ql = sb("a_qh", [P, 2, T], F32R), sb("a_ql", [P, 2, T], F32R)
        stage = sb("a_stage", [P, 2, DT, D])
        splits = ((stage[:, 0], proj.wkh, proj.wkl), (proj.raw, proj.chi, proj.clo), (stage[:, 1], proj.wvh, proj.wvl))
        norm = Norm(nc, ctx, "a", xs, idn)
        w_in, c_in, later_in, later_hi, later_lo = sem("a_w_in"), sem("a_c_in"), sem("a_later_in"), sem("a_later_hi"), sem("a_later_lo")
        x_in = [sem("a_x_in0"), sem("a_x_in1")]
        wh_done, wl_done = sem("a_wh_done"), sem("a_wl_done")
        q_mm, qh_done, ql_done = sem("a_q_mm"), sem("a_qh_done"), sem("a_ql_done")
        q_stored = [sem("a_q_stored0"), sem("a_q_stored1")]
        block = ctx.enter_context(nc.Block())

        @block.sync
        def _(sp):
            for b in range(B):
                sp.dma_start(xs[:, TT * b:TT * (b + 1), :], x[b].rearrange("(t p) d -> p t d", p=P)).then_inc(x_in[b], 16)
                if b == 0:
                    sp.dma_start(idn[:], ident).then_inc(c_in, 16)
            sp.dma_start(w[:], wq).then_inc(w_in, 16)
            sp.dma_start(bias[:], bq).then_inc(c_in, 16)
            for dst, src in ((stage[:, 0], wk), (proj.raw[:], ctx_t[0]), (stage[:, 1], wv)):
                sp.dma_start(dst, src).then_inc(later_in, 16)
            for m in range(B * G):
                sp.wait_ge(qh_done, m + 1)
                sp.dma_start(q_split[m // G, 0, m % G], fp(qh[:, m % 2, :])).then_inc(q_stored[m % 2], 16)
                sp.wait_ge(ql_done, m + 1)
                sp.dma_start(q_split[m // G, 1, m % G], fp(ql[:, m % 2, :])).then_inc(q_stored[m % 2], 16)
            for stored in q_stored:
                sp.wait_ge(stored, 16 * B * G)

        @block.scalar
        def _(act):
            norm.scalar_3_root(act, 0)
            norm.scalar_3_root(act, 1)
            norm.scalar_6_hi(act, 0)
            act.wait_ge(w_in, 16)
            act.activation(wh[:], w[:], ACT.Copy).then_inc(wh_done, 1)
            norm.scalar_6_hi(act, 1)
            act.wait_ge(c_in, 32)
            for m in range(B * G):
                act.wait_ge(q_mm, m + 1)
                if m >= 2:
                    act.wait_ge(q_stored[m % 2], 32 * (m // 2))
                act.activation(qh[:, m % 2, :], ps_q[:, m % 2, :], ACT.Identity,
                               bias=bias[:, m % G:m % G + 1]).then_inc(qh_done, 1)
                if m % 2 == 1 and m // 2 < len(splits):
                    src, high, low = splits[m // 2]
                    act.wait_ge(later_in, 16 * len(splits))
                    act.activation(high[:], src[:], ACT.Copy).then_inc(later_hi, 1)

        @block.vector
        def _(dve):
            for b in range(B):
                dve.wait_ge(x_in[b], 16)
                for i in range(TT * b, TT * (b + 1)):
                    norm.vector_1_stats(dve, i)
                norm.vector_2_variance(dve, b)
                norm.vector_4_apply(dve, b)
            norm.vector_7_lo(dve, 0)
            dve.wait_ge(wh_done, 1)
            dve.tensor_tensor(wl[:], w[:], fp(wh[:]), ALU.subtract).then_inc(wl_done, 1)
            norm.vector_7_lo(dve, 1)
            for m in range(B * G):
                dve.wait_ge(qh_done, m + 1)
                dve.scalar_tensor_tensor(ql[:, m % 2, :], ps_q[:, m % 2, :], bias[:, m % G:m % G + 1],
                                         fp(qh[:, m % 2, :]), ALU.add, ALU.subtract).then_inc(ql_done, 1)
                if m % 2 == 0 and m:
                    src, high, low = splits[m // 2 - 1]
                    dve.wait_ge(later_hi, m // 2)
                    dve.tensor_tensor(low[:], src[:], fp(high[:]), ALU.subtract).then_inc(later_lo, 1)

        @block.tensor
        def _(pe):
            pe.wait_ge(c_in, 32)
            norm.tensor_5_turn(pe, 0)
            norm.tensor_5_turn(pe, 1)
            pe.wait_ge(wl_done, 1)
            for m in range(B * G):
                b, g = m // G, m % G
                pe.wait_ge(norm.lo_done, DT * (b + 1))
                if m >= 2:
                    pe.wait_ge(ql_done, m - 1)
                exact_product(pe, ps_q[:, m % 2, :], lambda part, d: (wh, wl)[part][:, d, g * P:(g + 1) * P],
                              lambda part, d: (norm.hi, norm.lo)[part][:, d, b * T:(b + 1) * T]).then_inc(q_mm, 1)


def cross_attention(nc, proj, ctx_t, bk, bv, ident, onehot, q_split, attended, CH):
    STEPS = CH * G
    NCH = B * CH
    with ExitStack() as ctx:
        sb = lambda name, shape, dt=F32: ctx.enter_context(nc.sbuf_tensor(name, shape, dt))
        sem = lambda name: ctx.enter_context(nc.semaphore(name))
        bank = lambda name, n=1: ctx.enter_context(nc.psum_tensor(name, [P, n, 512], F32))
        ps_s, ps_m, ps_o, ps_d, ps_p, ps_x = (bank("ps_score", 2), bank("ps_max", 2), bank("ps_out"),
                                              bank("ps_den"), bank("ps_proj"), bank("ps_turn"))
        idn, idr, ones = sb("idn", [P, P]), sb("idr", [P, P], F32R), sb("ones", [P, HD])
        bk_s, bv_s = sb("bk_s", [P, G]), sb("bv_s", [P, G])
        wkh, wkl, wvh, wvl = proj.wkh, proj.wkl, proj.wvh, proj.wvl
        raw, chi, clo = proj.raw, proj.chi, proj.clo
        knh, knl = sb("knh", [P, 2, KC], F32R), sb("knl", [P, 2, KC], F32R)
        kst = sb("kst", [P, G, HG, KC], F32R)
        qst = sb("qst", [P, G, HG, T], F32R)
        val = sb("val", [P, 2, KT, D])
        prob = sb("prob", [P, KT, HG, T])
        psum4 = sb("psum4", [P, HG, T])
        acc_o, acc_d = sb("acc_o", [P, G, T]), sb("acc_d", [P, G, T])
        scale_b = sb("scale_b", [P, T])
        scale_t = sb("scale_t", [P, TT, HG, HD])
        nmax, nmax_new = sb("nmax", [P, G, TT * HG], F32R), sb("nmax_new", [P, TT * HG], F32R)
        tile_max, drop = sb("tile_max", [P, TT, HG]), sb("drop", [P, TT * HG])
        nmax_w = sb("nmax_w", [P, TT, P], F32R)

        c_in, ready = sem("c_in"), sem("b_ready")
        raw_in = sem("raw_in")
        ctx_hi, ctx_lo = sem("ctx_hi"), sem("ctx_lo")
        proj_mm, k_hi, k_lo, v_copied = sem("proj_mm"), sem("k_hi"), sem("k_lo"), sem("v_copied")
        kst_in, qst_in = [sem("kst_in0"), sem("kst_in1")], sem("qst_in")
        max_mm, max_read = sem("max_mm"), sem("max_read")
        nmax_made, nmax_wide, drop_made, nmax_kept = sem("nmax_made"), sem("nmax_wide"), sem("drop_made"), sem("nmax_kept")
        shift_mm, shift_in, shift_in_2 = sem("shift_mm"), sem("shift_in"), sem("shift_in_2")
        scale_made, scale_mm, scale_in, scaled = sem("scale_made"), sem("scale_mm"), sem("scale_in"), sem("scaled")
        score_mm, exp_done, pv_mm, summed = sem("score_mm"), sem("exp_done"), sem("pv_mm"), sem("summed")
        den_mm, o_added, d_added = sem("den_mm"), sem("o_added"), sem("d_added")
        inv_made, divided, biased, stored = sem("inv_made"), sem("divided"), sem("biased"), sem("stored")
        block = ctx.enter_context(nc.Block())

        n_exp = lambda N, t, j: 16 * N + 16 + 4 * t + j + 1
        n_max_read = lambda M, k: 16 * M + 16 + k + 1
        n_pv = lambda N, b, t: 4 * N + b + t + 6
        n_summed = lambda N, k: 3 * N + 3 + k
        n_added = lambda N, b: N + b + 2
        n_stacked = lambda C, g: 384 * C + 192 * (g // 2) + 192
        n_proj = lambda N: 2 * N + 7

        @block.sync
        def _(sp):
            sp.dma_start(bk_s[:], bk).then_inc(c_in, 16)
            sp.dma_start(bv_s[:], bv).then_inc(c_in, 16)
            sp.dma_start(raw[:], ctx_t[1]).then_inc(raw_in, 16)
            sp.dma_start(idn[:], ident).then_inc(c_in, 16)
            sp.dma_start(psum4[STACK:P], onehot).then_inc(c_in, 16)

            def queries(b):
                for g in range(G):
                    for q, part in enumerate((0, 1, 0)):
                        src = q_split[b, part, g].rearrange("o (j r) t -> r (o j) t", j=HG)
                        sp.dma_start(fp(qst[HD * q:HD * (q + 1), g]), src).then_inc(qst_in, 16)

            def stack_k(k, slot, par, free=None):
                sp.wait_ge(k_hi, k + 1)
                if free is not None:
                    sp.wait_ge(score_mm, free)
                for j in range(HG):
                    rows = slice(HD * j, HD * (j + 1))
                    for q in range(2):
                        sp.dma_start(fp(kst[HD * q:HD * (q + 1), slot, j, :]), fp(knh[rows, par, :])).then_inc(kst_in[par], 16)
                sp.wait_ge(k_lo, k + 1)
                for j in range(HG):
                    rows = slice(HD * j, HD * (j + 1))
                    sp.dma_start(fp(kst[2 * HD:STACK, slot, j, :]), fp(knl[rows, par, :])).then_inc(kst_in[par], 16)

            queries(slice(0, 1))
            stack_k(0, 0, 0)
            stack_k(1, 1, 1)
            stack_k(2, 2, 0)
            with sp.Fori(0, B) as b:
                with sp.Fori(0, CH // 2) as c2:
                    for u in range(2):
                        for g in range(G):
                            C = b * CH + c2 * 2 + u
                            N = C * G + g
                            stack_k(N + 3, (g + 3) % G, (g + 1) % 2, 16 * N + 1)
                            if g == 0:
                                sp.wait_ge(ctx_lo, DT * (C + 1))
                                sp.dma_start(raw[:], ctx_t[bass.ds((C + 2) % NCH, 1)].rearrange(
                                    "o p d k -> (o p) d k")).then_inc(raw_in, 16)
                sp.wait_ge(score_mm, (b + 1) * (16 * STEPS))
                queries(bass.ds((b + 1) % B, 1))
                for g in range(G):
                    sp.wait_ge(biased, G * b + g + 1)
                    sp.dma_start(attended[bass.ds(b, 1), :, g].rearrange("o p t -> (o p) t"), acc_o[:, g]).then_inc(stored, 16)
            sp.wait_ge(stored, (16 * G) * B + 16)
            sp.wait_ge(qst_in, 192 * (B + 1))
            sp.wait_ge(kst_in[0], 96 * (B * STEPS + 4))
            sp.wait_ge(kst_in[1], 96 * (B * STEPS + 2))
            sp.wait_ge(raw_in, 16 * (NCH + 1))

        @block.scalar
        def _(act):
            act.wait_ge(c_in, 64)

            def split_hi(C, half):
                act.wait_ge(raw_in, 16 * C)
                s = slice(2 * half, 2 * half + 2)
                act.activation(chi[:, s, :], raw[:, s, :], ACT.Copy).then_inc(ctx_hi, 1)

            def k_evac(k, proj, g, par, loaded=None):
                act.wait_ge(proj_mm, proj)
                if loaded is not None:
                    act.wait_ge(kst_in[par], loaded)
                act.activation(knh[:, par, :], ps_p[:, 0, :], ACT.Identity, bias=bk_s[:, g:g + 1]).then_inc(k_hi, 1)

            def v_evac(t, par, proj, pv=None):
                act.wait_ge(proj_mm, proj)
                if pv is not None:
                    act.wait_ge(pv_mm, pv)
                act.copy(val[:, par, t, :], ps_p[:, 0, :]).then_inc(v_copied, 1)

            def shift_copy(M, g):
                act.wait_ge(shift_mm, M + 1)
                act.activation(qst[STACK:ROWS, g, 0], ps_x[STACK:ROWS, 0, :],
                               ACT.Copy).then_inc(shift_in, 1)

            def scale_exp(M):
                act.wait_ge(drop_made, M + 1)
                act.wait_ge(scale_made, M + 1)
                act.activation(scale_t[:], drop[:].rearrange("p (t j) -> p t j", t=TT).unsqueeze(3).to_broadcast(
                    [P, TT, HG, HD]), ACT.Exp, scale=SCALE).then_inc(scale_made, 1)

            def exps(N, b, t, heads):
                for j in heads:
                    if j == 0:
                        act.wait_ge(pv_mm, n_pv(N, b, -1) if t == 3 else n_pv(N - 1, b, t))
                        act.wait_ge(summed, n_summed(N - 1, max(t, 1)))
                    act.wait_ge(score_mm, 16 * N + 4 * t + j + 1)
                    act.activation(prob[:, t, j, :], ps_s[:, j % 2, :], ACT.Exp, scale=SCALE).then_inc(exp_done, 1)

            for k in range(3):
                k_evac(k, k + 1, k, k % 2, 192 if k == 2 else None)
            act.activation(idr[:], idn[:], ACT.Copy).then_inc(ready, 1)
            for t in range(KT):
                v_evac(t, 0, 4 + t)
            with act.Fori(0, B) as b:
                shift_copy(b * (STEPS + 1), 0)
                scale_exp(b * (STEPS + 1))
                with act.Fori(0, CH // 2) as c2:
                    for u in range(2):
                        for g in range(G):
                            C = b * CH + c2 * 2 + u
                            N = C * G + g
                            exps(N, b, 0, range(4))
                            act.wait_ge(scale_mm, N + 1)
                            act.wait_ge(scaled, N + 1)
                            act.copy(scale_b[:], ps_x[:, 0, :]).then_inc(scale_in, 1)
                            k_evac(N + 3, n_proj(N) + 1, (g + 3) % G, (g + 1) % 2, n_stacked(C, g + 1))
                            if g == 0:
                                exps(N, b, 1, range(1))
                                split_hi(C + 1, 0)
                                exps(N, b, 1, range(1, 3))
                                split_hi(C + 1, 1)
                                exps(N, b, 1, range(3, 4))
                            else:
                                exps(N, b, 1, range(4))
                            exps(N, b, 2, range(4))
                            exps(N, b, 3, range(1))
                            v_evac(g, 1 - u, n_proj(N) + 2, n_pv(N, b, -1))
                            shift_copy(N + b + 1, (g + 1) % G)
                            exps(N, b, 3, range(1, 4))
                            scale_exp(N + b + 1)
                for g in range(G):
                    act.wait_ge(divided, G * b + g + 1)
                    act.activation(acc_o[:, g, :], acc_o[:, g, :], ACT.Identity, bias=bv_s[:, g:g + 1]).then_inc(biased, 1)

        @block.vector
        def _(dve):
            dve.memset(ones[:], 1.0).then_inc(ready, 1)
            dve.memset(val[:, 1, KT - 1], 0.0).then_inc(ready, 1)
            dve.memset(fp(nmax_w[:]), 0.0).then_inc(shift_in, 1)
            dve.memset(drop[:], 0.0).then_inc(stored, 16)
            dve.memset(nmax_new[:].bitcast(F32), BIG).then_inc(shift_in_2, 1)
            dve.memset(ps_o[:], 0.0).then_inc(pv_mm, 4)
            dve.memset(fp(nmax[:]), BIG).then_inc(nmax_kept, 1)
            dve.memset(scale_b[:], 0.0).then_inc(scaled, 1)
            dve.memset(tile_max[:], 0.0).then_inc(max_read, 16)

            def split_lo(C, d):
                dve.wait_ge(ctx_hi, 2 * C - 1 + d // 2)
                dve.tensor_tensor(clo[:, d, :], raw[:, d, :], fp(chi[:, d, :]), ALU.subtract).then_inc(ctx_lo, 1)

            def k_evac(k, g, par):
                dve.wait_ge(k_hi, k + 1)
                dve.scalar_tensor_tensor(knl[:, par, :], ps_p[:, 0, :], bk_s[:, g:g + 1], fp(knh[:, par, :]),
                                         ALU.add, ALU.subtract).then_inc(k_lo, 1)

            def maxima(M, first, n):
                for k in range(first, first + n):
                    j, t = k // TT, k % TT
                    dve.wait_ge(max_mm, 16 * M + k + 1)
                    dve.tensor_reduce(tile_max[:, t, j:j + 1], ps_m[:, k % 2, :], AX_X, ALU.max,
                                      negate=True).then_inc(max_read, 1)

            def update_max(M, b, g):
                dve.wait_ge(max_read, n_max_read(M, 15))
                dve.wait_ge(nmax_kept, M + b + 2)
                dve.tensor_tensor(nmax_new[:], fp(nmax[:, g, :]), tile_max[:].rearrange("p t j -> p (t j)"),
                                  ALU.min).then_inc(nmax_made, 1)
                dve.wait_ge(nmax_made, M + 1)
                dve.wait_ge(shift_in, M + 1)
                dve.tensor_copy(nmax_w[:, :, STACK:ROWS], fp(nmax_new[:]).rearrange("p (t j) -> p t j", t=TT)
                                ).then_inc(nmax_wide, 1)
                dve.wait_ge(scale_made, M + 1)
                dve.tensor_tensor(drop[:], fp(nmax_new[:]), fp(nmax[:, g, :]), ALU.subtract).then_inc(drop_made, 1)
                dve.wait_ge(drop_made, M + 1)
                dve.tensor_copy(nmax[:, g, :], fp(nmax_new[:])).then_inc(nmax_kept, 1)

            def shift_copy(M, g):
                dve.wait_ge(shift_in, M + 2)
                for j in range(1, HG):
                    dve.tensor_copy(qst[STACK:ROWS, g, j], fp(qst[STACK:ROWS, g, 0])).then_inc(shift_in_2, 1)

            def add_out(N, b, g):
                dve.wait_ge(pv_mm, n_pv(N, b, -1))
                dve.wait_ge(scaled, N + 1)
                dve.tensor_tensor(acc_o[:, g, :], ps_o[:, 0, :], acc_o[:, g, :], ALU.add).then_inc(o_added, 1)

            def add_den(N, b, g):
                dve.wait_ge(den_mm, N + b + 1)
                dve.tensor_tensor(acc_d[:, g, :], ps_d[:, 0, :], acc_d[:, g, :], ALU.add).then_inc(d_added, 1)

            k_evac(0, 0, 0)
            k_evac(1, 1, 1)
            k_evac(2, 2, 0)
            for g in range(G):
                dve.tensor_copy(kst[STACK:P, g], psum4[STACK:P]).then_inc(ready, 1)
            with dve.Fori(0, B) as b:
                dve.wait_ge(nmax_kept, b * (STEPS + 2) + 1)
                dve.memset(fp(nmax[:]), BIG).then_inc(nmax_kept, 1)
                maxima(b * (STEPS + 1), 0, 16)
                dve.wait_ge(stored, (16 * G) * b + 16)
                update_max(b * (STEPS + 1), b, 0)
                shift_copy(b * (STEPS + 1), 0)
                with dve.Fori(0, CH // 2) as c2:
                    for u in range(2):
                        for g in range(G):
                            C = b * CH + c2 * 2 + u
                            N = C * G + g
                            M = N + b + 1
                            maxima(M, 0, 5)
                            add_out(N, b, (g + 3) % G)
                            maxima(M, 5, 2)
                            k_evac(N + 3, (g + 3) % G, (g + 1) % 2)
                            for d in range(DT):
                                maxima(M, 7 + 2 * d, 2)
                                if g == 0:
                                    split_lo(C + 1, d)
                            maxima(M, 15, 1)
                            update_max(M, b, (g + 1) % G)
                            add_den(N, b, (g + 3) % G)
                            shift_copy(M, (g + 1) % G)
                N = (b + 1) * STEPS
                for g in range(G):
                    if g < G - 1:
                        dve.wait_ge(d_added, n_added(N, b) - 1)
                        dve.wait_ge(o_added, n_added(N, b) - 1)
                    else:
                        add_out(N, b, g)
                        add_den(N, b, g)
                        dve.wait_ge(d_added, n_added(N, b))
                        dve.wait_ge(o_added, n_added(N, b))
                    dve.reciprocal(acc_d[:, g, :], acc_d[:, g, :]).then_inc(inv_made, 1)
                    dve.wait_ge(inv_made, G * b + g + 1)
                    dve.tensor_tensor(acc_o[:, g, :], acc_o[:, g, :], acc_d[:, g, :], ALU.mult).then_inc(divided, 1)

        @block.gpsimd
        def _(pool):
            pool.memset(scale_t[:], 0.0).then_inc(scale_made, 1)
            pool.memset(acc_o[:], 0.0).then_inc(o_added, 1)
            pool.memset(acc_d[:], 0.0).then_inc(d_added, 1)
            pool.memset(prob[:], 0.0).then_inc(exp_done, 16)
            pool.wait_ge(ready, 3 + G)
            pool.memset(psum4[:], 0.0).then_inc(summed, 3)
            with pool.Fori(0, B) as b:
                with pool.Fori(0, STEPS // G) as c:
                    for g in range(G):
                        N = (b * CH + c) * G + g
                        if g == 0:
                            pool.wait_ge(stored, (16 * G) * b + 16)
                        pool.wait_ge(scale_in, N + 1)
                        pool.wait_ge(d_added, n_added(N, b) - 1)
                        pool.tensor_tensor(acc_o[:, g, :], acc_o[:, g, :], scale_b[:], ALU.mult)
                        pool.tensor_tensor(acc_d[:, g, :], acc_d[:, g, :], scale_b[:], ALU.mult).then_inc(scaled, 1)
                        pool.wait_ge(exp_done, n_exp(N, 1, 3))
                        pool.wait_ge(den_mm, N + b + 1)
                        pool.tensor_tensor(psum4[:], prob[:, 0], prob[:, 1], ALU.add).then_inc(summed, 1)
                        for k in (1, 2):
                            pool.wait_ge(exp_done, n_exp(N, k + 1, 3))
                            pool.wait_ge(summed, n_summed(N, k))
                            pool.tensor_tensor(psum4[:], psum4[:], prob[:, k + 1], ALU.add).then_inc(summed, 1)

        @block.tensor
        def _(pe):
            def project_k(part, g):
                wp, cp = ((wkh, chi), (wkh, clo), (wkl, chi))[part]
                for d in range(DT):
                    mm = pe.matmul(ps_p[:, 0, :], wp[:, d, g * P:(g + 1) * P], cp[:, d, :],
                                   start=(part == 0 and d == 0), stop=(part == 2 and d == DT - 1))
                if part == 2:
                    mm.then_inc(proj_mm, 1)

            def project_v(part, t):
                cp, wp = ((chi, wvh), (chi, wvl), (clo, wvh))[part]
                for d in range(DT):
                    mm = pe.matmul(ps_p[:, 0, :], cp[:, d, t * P:(t + 1) * P], wp[:, d, :],
                                   start=(part == 0 and d == 0), stop=(part == 2 and d == DT - 1))
                if part == 2:
                    mm.then_inc(proj_mm, 1)

            def max_scores(M, g, k):
                j, t = k // TT, k % TT
                pe.wait_ge(max_read, n_max_read(M, k - 2))
                pe.matmul(ps_m[:, k % 2, :], qst[0:STACK, g, j, t * P:(t + 1) * P], kst[0:STACK, g, j, :],
                          start=True, stop=True).then_inc(max_mm, 1)

            def shift_rows(M):
                pe.wait_ge(nmax_wide, M + 1)
                for t in range(TT):
                    mm = pe.matmul(ps_x[:, 0, t * P:(t + 1) * P], nmax_w[:, t, :], idr[:], start=True, stop=True)
                mm.then_inc(shift_mm, 1)

            def scores(N, g, t, j):
                pe.wait_ge(exp_done, n_exp(N, t, j) - 2)
                pe.matmul(ps_s[:, j % 2, :], kst[0:ROWS, g, j, t * P:(t + 1) * P], qst[0:ROWS, g, j, :],
                          start=True, stop=True).then_inc(score_mm, 1)

            def values(N, par, g, t):
                pe.wait_ge(exp_done, n_exp(N, t, 3))
                for j in range(HG):
                    c = (g * HG + j) * HD
                    mm = pe.matmul(ps_o[j * HD:(j + 1) * HD, 0, :], val[:, par, t, c:c + HD], prob[:, t, j, :],
                                   start=(t == 0), stop=(t == KT - 1))
                mm.then_inc(pv_mm, 1)

            def denominators(N, b):
                pe.wait_ge(summed, n_summed(N - 1, 3))
                pe.wait_ge(d_added, n_added(N, b) - 1)
                for j in range(HG):
                    mm = pe.matmul(ps_d[j * HD:(j + 1) * HD, 0, :], ones[:], psum4[:, j, :], start=True, stop=True)
                mm.then_inc(den_mm, 1)

            def scale_rows(N, b):
                pe.wait_ge(scale_made, N + b + 2)
                pe.wait_ge(shift_in, N + b + 2)
                for t in range(TT):
                    mm = pe.transpose(ps_x[:, 0, t * P:(t + 1) * P], scale_t[:, t].rearrange("p j r -> p (j r)"), idn[:])
                mm.then_inc(scale_mm, 1)

            for k in range(3):
                if k:
                    pe.wait_ge(k_lo, k)
                for part in range(3):
                    project_k(part, k)
            for t in range(KT):
                if t == 0:
                    pe.wait_ge(k_lo, 3)
                else:
                    pe.wait_ge(v_copied, t)
                for part in range(3):
                    project_v(part, t)

            pe.wait_ge(ready, 3 + G)
            pe.wait_ge(c_in, 64)
            with pe.Fori(0, B) as b:
                M0 = b * (STEPS + 1)
                pe.wait_ge(qst_in, 192 * b + 192)
                pe.wait_ge(kst_in[0], b * (96 * STEPS) + 384)
                for k in range(16):
                    max_scores(M0, 0, k)
                pe.wait_ge(shift_in, M0 + 1)
                shift_rows(M0)
                pe.wait_ge(o_added, b * (STEPS + 1) + 1)
                pe.wait_ge(exp_done, b * (16 * STEPS) + 16)
                for j in range(HG):
                    c = (3 * HG + j) * HD
                    pe.matmul(ps_o[j * HD:(j + 1) * HD, 0, :], val[:, 0, 0, c:c + HD], prob[:, 3, j, :],
                              start=True, stop=False)
                with pe.Fori(0, CH // 2) as c2:
                    for u in range(2):
                        for g in range(G):
                            C = b * CH + c2 * 2 + u
                            N = C * G + g
                            M = N + b + 1
                            score = lambda t, j: scores(N, g, t, j)
                            peak = lambda k: max_scores(M, (g + 1) % G, k)

                            pe.wait_ge(kst_in[(g + 1) % 2], n_stacked(C, g + 1))
                            peak(0)
                            pe.wait_ge(v_copied, N + 4)
                            project_k(0, (g + 3) % G)
                            peak(1)
                            pe.wait_ge(shift_in, N + b + 2)
                            score(0, 0)
                            pe.wait_ge(shift_in_2, 3 * (N + b) + 2)
                            score(0, 1)
                            peak(2)
                            values(N - 1, u if g else 1 - u, (g + 3) % G, 3)
                            peak(3)
                            pe.wait_ge(shift_in_2, 3 * (N + b) + 3)
                            score(0, 2)
                            project_k(1, (g + 3) % G)
                            peak(4)
                            pe.wait_ge(shift_in_2, 3 * (N + b) + 4)
                            score(0, 3)
                            scale_rows(N, b)
                            peak(5)
                            project_k(2, (g + 3) % G)
                            peak(6)
                            score(1, 0)
                            pe.wait_ge(o_added, n_added(N, b))
                            peak(7)
                            values(N, u, g, 0)
                            peak(8)
                            score(1, 1)
                            score(1, 2)
                            peak(9)
                            denominators(N, b)
                            peak(10)
                            score(1, 3)
                            score(2, 0)
                            peak(11)
                            pe.wait_ge(k_lo, N + 4)
                            if g == 0:
                                pe.wait_ge(ctx_hi, 2 * C + 2)
                            project_v(0, g)
                            peak(12)
                            score(2, 1)
                            peak(13)
                            values(N, u, g, 1)
                            peak(14)
                            score(2, 2)
                            score(2, 3)
                            peak(15)
                            project_v(1, g)
                            score(3, 0)
                            if g == 0:
                                pe.wait_ge(ctx_lo, DT * (C + 1))
                            project_v(2, g)
                            pe.wait_ge(scale_in, N + 1)
                            shift_rows(M)
                            score(3, 1)
                            values(N, u, g, 2)
                            score(3, 2)
                            score(3, 3)
                N = (b + 1) * STEPS
                values(N - 1, 1, G - 1, 3)
                denominators(N, b)


class Merge:

    def __init__(self, nc, ctx, tag):
        sb = lambda name, shape, dt=F32: ctx.enter_context(nc.sbuf_tensor(f"{tag}_{name}", shape, dt))
        sem = lambda name: ctx.enter_context(nc.semaphore(f"{tag}_{name}"))
        self.y, self.bias = sb("y", [P, NT, D]), sb("bias", [P, D])
        self.oh, self.ol = sb("oh", [P, B, G, T], F32R), sb("ol", [P, B, G, T], F32R)
        self.w, self.wh, self.wl = sb("w", [P, DT, D]), sb("wh", [P, DT, D], F32R), sb("wl", [P, DT, D], F32R)
        self.w_in, self.bias_in = sem("w_in"), sem("bias_in")
        self.y_in = [sem(f"y_in{b}") for b in range(B)]
        self.wh_done, self.wl_done, self.oh_done, self.ol_done = sem("wh_done"), sem("wl_done"), sem("oh_done"), sem("ol_done")
        self.biased, self.mm, self.y_done = sem("biased"), sem("mm"), sem("y_done")

    def sync_1_weights(self, sp, w, bias):
        sp.dma_start(self.w[:], w).then_inc(self.w_in, 16)
        sp.dma_start(self.bias[:], bias.partition_broadcast(P)).then_inc(self.bias_in, 16)

    def sync_1_tokens(self, sp, x, b):
        sp.dma_start(self.y[:, TT * b:TT * (b + 1), :], x[b].rearrange("(t p) d -> p t d", p=P)).then_inc(self.y_in[b], 16)

    def scalar_2_hi(self, act):
        act.wait_ge(self.w_in, 16)
        act.activation(self.wh[:], self.w[:], ACT.Copy).then_inc(self.wh_done, 1)

    def gpsimd_2_bias(self, pool, i):
        if i == 0:
            pool.wait_ge(self.bias_in, 16)
        if i % TT == 0:
            pool.wait_ge(self.y_in[i // TT], 16)
        pool.tensor_tensor(self.y[:, i, :], self.y[:, i, :], self.bias[:], ALU.add).then_inc(self.biased, 1)

    def vector_3_lo(self, dve):
        dve.wait_ge(self.wh_done, 1)
        dve.tensor_tensor(self.wl[:], self.w[:], fp(self.wh[:]), ALU.subtract).then_inc(self.wl_done, 1)

    def tensor_4_product(self, pe, ps, tiles):
        pe.wait_ge(self.wl_done, 1)
        for i in tiles:
            b, t = i // TT, i % TT
            pe.wait_ge(self.ol_done, G * (b + 1))
            if i >= 2:
                pe.wait_ge(self.y_done, i - 1)
            exact_product(pe, ps[:, i % 2, :], lambda part, d: (self.oh, self.ol)[part][:, b, d, t * P:(t + 1) * P],
                          lambda part, d: (self.wh, self.wl)[part][:, d, :]).then_inc(self.mm, 1)

    def vector_5_add(self, dve, ps, i):
        dve.wait_ge(self.mm, i + 1)
        dve.wait_ge(self.biased, i + 1)
        dve.tensor_tensor(self.y[:, i, :], ps[:, i % 2, :], self.y[:, i, :], ALU.add).then_inc(self.y_done, 1)
        dve.wait_ge(self.y_done, i + 1)


def project_self(nc, x, attended, wo, bo, w_qkv, cos, sin, ident, x1, qk_split, v_out):
    with ExitStack() as ctx:
        sb = lambda name, shape, dt=F32: ctx.enter_context(nc.sbuf_tensor(name, shape, dt))
        sem = lambda name: ctx.enter_context(nc.semaphore(name))
        idn = sb("c_id", [P, P])
        merge, ps_merge = Merge(nc, ctx, "cm"), ctx.enter_context(nc.psum_tensor("c_ps_merge", [P, 2, 512], F32))
        att = sb("c_att", [P, B, G, T])
        ps_e = ctx.enter_context(nc.psum_tensor("c_ps_pair", [P, 2, 2, 512], F32))
        norm = Norm(nc, ctx, "cn", merge.y, idn)
        table = sb("c_table", [P, 2, 2, T])
        own = sb("c_qh", [P, DT, D], F32R), sb("c_ql", [P, DT, D], F32R)
        parts = own, (merge.wh, merge.wl), own
        prod = sb("c_prod", [P, 4, T])
        part_h, part_l = sb("c_part_h", [P, 2, 2, T], F32R), sb("c_part_l", [P, 2, 2, T], F32R)
        turned_qk = sb("c_turned", [P, 2, T])
        val = sb("c_val", [P, 2, D])
        c_in, w_in, att_in = sem("c_c_in"), sem("c_w2_in"), [sem("c_att_in0"), sem("c_att_in1")]
        wh_done, wl_done = sem("c_wh2_done"), sem("c_wl2_done")
        pair_mm, mults, turns, ph_done, pl_done = (sem("c_pair_mm"), sem("c_mults"), sem("c_turns"), sem("c_ph_done"), sem("c_pl_done"))
        v_mm, v_done = sem("c_v_mm"), sem("c_v_done")
        parts_out = [sem("c_parts_out0"), sem("c_parts_out1")]
        v_sent, x1_out = [sem("c_v_sent0"), sem("c_v_sent1")], sem("c_x1_out")
        block = ctx.enter_context(nc.Block())
        PAIRS = 2 * B * 2

        @block.sync
        def _(sp):
            merge.sync_1_weights(sp, wo, bo)
            for b in range(B):
                sp.dma_start(att[:, b], attended[b]).then_inc(att_in[b], 16)
                merge.sync_1_tokens(sp, x, b)
            sp.dma_start(idn[:], ident).then_inc(c_in, 16)
            sp.dma_start(table[:, 0], cos).then_inc(c_in, 16)
            sp.dma_start(table[:, 1], sin).then_inc(c_in, 16)
            sp.wait_ge(merge.wl_done, 1)
            sp.dma_start(merge.w[:], w_qkv[0]).then_inc(w_in, 16)
            sp.wait_ge(wl_done, 1)
            sp.dma_start(merge.w[:], w_qkv[1]).then_inc(w_in, 16)
            for b in range(B):
                sp.wait_ge(merge.y_done, TT * (b + 1))
                sp.dma_start(x1[b].rearrange("(t p) d -> p t d", p=P), merge.y[:, TT * b:TT * (b + 1), :]).then_inc(x1_out, 16)
            sp.wait_ge(wl_done, 2)
            sp.dma_start(merge.w[:], w_qkv[2]).then_inc(w_in, 16)
            for m in range(PAIRS):
                which, b, e = m // (2 * B), (m // 2) % B, m % 2
                for r in range(2):
                    rows = slice(r * HD // 2, (r + 1) * HD // 2)
                    for part, src, done in ((0, part_h, ph_done), (1, part_l, pl_done)):
                        sp.wait_ge(done, 2 * m + r + 1)
                        dst = qk_split[b, which, part, 2 * e:2 * e + 2, :, rows].rearrange("g j r t -> (g j) r t")
                        sp.dma_start(dst, fp(src[:, m % 2, r, :])).then_inc(parts_out[m % 2], 16)
            for i in range(NT):
                sp.wait_ge(v_done, i + 1)
                sp.dma_start(v_out[i // TT, :, i % TT, :], val[:, i % 2, :]).then_inc(v_sent[i % 2], 16)
            sp.wait_ge(x1_out, 16 * B)
            for out in parts_out:
                sp.wait_ge(out, 32 * PAIRS)
            for sent in v_sent:
                sp.wait_ge(sent, 8 * NT)

        @block.gpsimd
        def _(pool):
            for i in range(NT):
                merge.gpsimd_2_bias(pool, i)
            for m in range(PAIRS):
                pool.wait_ge(mults, 4 * m + 2)
                if m:
                    pool.wait_ge(pl_done, 2 * m - 1)
                pool.tensor_tensor(turned_qk[:, 0], prod[:, 0], prod[:, 1], ALU.subtract).then_inc(turns, 1)
                pool.wait_ge(mults, 4 * m + 4)
                if m:
                    pool.wait_ge(pl_done, 2 * m)
                pool.tensor_tensor(turned_qk[:, 1], prod[:, 2], prod[:, 3], ALU.add).then_inc(turns, 1)

        @block.scalar
        def _(act):
            merge.scalar_2_hi(act)
            for b in range(B):
                act.wait_ge(att_in[b], 16)
                act.activation(merge.oh[:, b], att[:, b], ACT.Copy).then_inc(merge.oh_done, 1)

            def weights(n):
                act.wait_ge(w_in, 16 * (n + 1))
                if n == 1:
                    act.wait_ge(merge.mm, NT)
                if n == 2:
                    act.wait_ge(pair_mm, PAIRS // 2)
                act.activation(parts[n][0][:], merge.w[:], ACT.Copy).then_inc(wh_done, 1)

            weights(0)
            for b in range(B):
                norm.scalar_3_root(act, b)
                norm.scalar_6_hi(act, b)
            weights(1)
            for m in range(PAIRS):
                for r in range(2):
                    act.wait_ge(turns, 2 * m + r + 1)
                    if m >= 2:
                        act.wait_ge(parts_out[m % 2], 64 * (m // 2))
                    act.activation(part_h[:, m % 2, r, :], turned_qk[:, r], ACT.Copy).then_inc(ph_done, 1)
                if m == PAIRS // 2:
                    weights(2)
            for i in range(NT):
                act.wait_ge(v_mm, i + 1)
                if i >= 2:
                    act.wait_ge(v_sent[i % 2], 16 * (i // 2))
                act.copy(val[:, i % 2, :], ps_e[:, 0, i % 2, :]).then_inc(v_done, 1)

        @block.vector
        def _(dve):
            def weights(n):
                dve.wait_ge(wh_done, n + 1)
                high, low = parts[n]
                dve.tensor_tensor(low[:], merge.w[:], fp(high[:]), ALU.subtract).then_inc(wl_done, 1)

            merge.vector_3_lo(dve)
            for b in range(B):
                dve.wait_ge(merge.oh_done, b + 1)
                dve.tensor_tensor(merge.ol[:, b], att[:, b], fp(merge.oh[:, b]), ALU.subtract).then_inc(merge.ol_done, G)
            for i in range(NT):
                merge.vector_5_add(dve, ps_merge, i)
                norm.vector_1_stats(dve, i)
                if i % TT == TT - 1:
                    norm.vector_2_variance(dve, i // TT)
                    norm.vector_4_apply(dve, i // TT)
                if i == TT:
                    weights(0)
                if i == TT + 1:
                    norm.vector_7_lo(dve, 0)
            norm.vector_7_lo(dve, 1)
            weights(1)
            dve.wait_ge(c_in, 48)
            for m in range(PAIRS):
                e = m % 2
                dve.wait_ge(pair_mm, m + 1)
                if m:
                    dve.wait_ge(turns, 2 * m)
                for n, (half, tab) in enumerate(((0, 0), (1, 1), (0, 1), (1, 0))):
                    dve.tensor_tensor(prod[:, n], ps_e[:, m % 2, half, :], table[:, tab, e, :], ALU.mult).then_inc(mults, 1)
                for r in range(2):
                    dve.wait_ge(ph_done, 2 * m + r + 1)
                    dve.tensor_tensor(part_l[:, m % 2, r, :], turned_qk[:, r], fp(part_h[:, m % 2, r, :]),
                                      ALU.subtract).then_inc(pl_done, 1)
                if m == PAIRS // 2:
                    weights(2)

        @block.tensor
        def _(pe):
            merge.tensor_4_product(pe, ps_merge, range(TT + 2))
            pe.wait_ge(c_in, 48)
            norm.tensor_5_turn(pe, 0)
            merge.tensor_4_product(pe, ps_merge, range(TT + 2, NT))
            for m in range(PAIRS):
                b, e = (m // 2) % B, m % 2
                pe.wait_ge(wl_done, 1 + m // (2 * B))
                pe.wait_ge(norm.lo_done, DT * (b + 1))
                if m >= 2:
                    pe.wait_ge(mults, 4 * (m - 1))
                for half in range(2):
                    c = (2 * half + e) * P
                    mm = exact_product(pe, ps_e[:, m % 2, half, :], lambda part, d: parts[m // (2 * B)][part][:, d, c:c + P],
                                       lambda part, d: (norm.hi, norm.lo)[part][:, d, b * T:(b + 1) * T])
                mm.then_inc(pair_mm, 1)
                if m == 0:
                    norm.tensor_5_turn(pe, 1)
            pe.wait_ge(wl_done, 3)
            for i in range(NT):
                if i < 2:
                    pe.wait_ge(mults, 4 * (PAIRS - 1))
                else:
                    pe.wait_ge(v_done, i - 1)
                exact_product(pe, ps_e[:, 0, i % 2, :], lambda part, d: (norm.hi, norm.lo)[part][:, d, i * P:(i + 1) * P],
                              lambda part, d: parts[2][part][:, d, :]).then_inc(v_mm, 1)


def self_attention(nc, merge, x1, wu, bu, qk_split, v_in, ident, onehot):
    STEPS = B * G
    SLOTS = 3
    with ExitStack() as ctx:
        sb = lambda name, shape, dt=F32: ctx.enter_context(nc.sbuf_tensor(name, shape, dt))
        sem = lambda name: ctx.enter_context(nc.semaphore(name))
        bank = lambda name, n=1: ctx.enter_context(nc.psum_tensor(name, [P, n, 512], F32))
        ps_s, ps_m, ps_o, ps_d, ps_x = (bank("d_ps_score", 2), bank("d_ps_max", 2), bank("d_ps_out", 2),
                                        bank("d_ps_den"), bank("d_ps_turn"))
        idn, idr, ones = sb("d_idn", [P, P]), sb("d_idr", [P, P], F32R), sb("d_ones", [P, HD])
        kst, qst = sb("d_kst", [P, SLOTS, HG, T], F32R), sb("d_qst", [P, SLOTS, HG, T], F32R)
        val = sb("d_val", [P, B, TT, D])
        prob, pair = sb("d_prob", [P, TT, HG, T]), sb("d_pair", [P, 2, HG, T])
        tile_max, nmax_w = sb("d_tile_max", [P, TT, HG]), sb("d_nmax_w", [P, TT, P], F32R)
        den, inv_t, inv_w = sb("d_den", [P, T]), sb("d_inv_t", [P, TT, HG]), sb("d_inv_w", [P, TT, HG, HD])
        inv, out = sb("d_inv", [P, T]), sb("d_out", [P, 2, T])
        c_in, v_in_sem, zeroed, consts = sem("d_c_in"), sem("d_v_in"), sem("d_zeroed"), sem("d_consts")
        stack_in = [sem("d_stack_in0"), sem("d_stack_in1")]
        max_mm, max_read, wide = sem("d_max_mm"), sem("d_max_read"), sem("d_wide")
        shift_mm, shift_in = sem("d_shift_mm"), sem("d_shift_in")
        score_mm, exp_done, pv_mm, summed, den_mm = (sem("d_score_mm"), sem("d_exp_done"), sem("d_pv_mm"),
                                                     sem("d_summed"), sem("d_den_mm"))
        den_in, den_turned, inv_done, inv_wide, inv_turned, inv_in = (sem("d_den_in"), sem("d_den_turned"), sem("d_inv_done"),
                                                                      sem("d_inv_wide"), sem("d_inv_turned"), sem("d_inv_in"))
        out_done = sem("d_out_done")
        block = ctx.enter_context(nc.Block())

        @block.sync
        def _(sp):

            def stacks(n):
                b, g = n // G, n % G
                for which, dst, order in ((1, kst, (0, 0, 1)), (0, qst, (0, 1, 0))):
                    for q, part in enumerate(order):
                        sp.dma_start(fp(dst[HD * q:HD * (q + 1), n % SLOTS]), qk_split[b, which, part, g].rearrange(
                            "j r t -> r j t")).then_inc(stack_in[n % 2], 16)

            stacks(0)
            sp.dma_start(idn[:], ident).then_inc(c_in, 16)
            sp.dma_start(pair[STACK:P, 0], onehot).then_inc(c_in, 16)
            for b in range(B):
                sp.dma_start(val[:, b], v_in[b]).then_inc(v_in_sem, 16)
            stacks(1)
            sp.wait_ge(max_mm, 1)
            stacks(2)
            for n in range(STEPS):
                if n + 3 < STEPS:
                    sp.wait_ge(score_mm, 16 * (n + 1))
                    stacks(n + 3)
                if n == 0:
                    merge.sync_1_weights(sp, wu, bu)
                    for b in range(B):
                        merge.sync_1_tokens(sp, x1, b)

        @block.gpsimd
        def _(pool):
            def low(n):
                pool.wait_ge(merge.oh_done, n + 1)
                pool.tensor_tensor(merge.ol[:, n // G, n % G], out[:, n % 2, :], fp(merge.oh[:, n // G, n % G]),
                                   ALU.subtract).then_inc(merge.ol_done, 1)

            pool.wait_ge(consts, 1 + SLOTS)
            for n in range(STEPS):
                for k in range(2):
                    pool.wait_ge(exp_done, 16 * n + 8 * k + 8)
                    if n:
                        pool.wait_ge(den_mm, n)
                    pool.tensor_tensor(pair[:, k], prob[:, 2 * k], prob[:, 2 * k + 1], ALU.add).then_inc(summed, 1)
                if n:
                    low(n - 1)
                    merge.gpsimd_2_bias(pool, n - 1)
            merge.gpsimd_2_bias(pool, NT - 1)
            low(STEPS - 1)

        @block.scalar
        def _(act):
            act.wait_ge(c_in, 32)
            act.activation(idr[:], idn[:], ACT.Copy).then_inc(consts, 1)
            for s in range(SLOTS):
                act.activation(kst[STACK:P, s], pair[STACK:P, 0], ACT.Copy).then_inc(consts, 1)

            def shift_copy(n, j):
                act.wait_ge(shift_mm, n + 1)
                act.activation(qst[STACK:ROWS, n % SLOTS, j], ps_x[STACK:ROWS, 0, :], ACT.Copy).then_inc(shift_in, 1)

            def high(n):
                act.wait_ge(out_done, n + 1)
                act.activation(merge.oh[:, n // G, n % G], out[:, n % 2, :], ACT.Copy).then_inc(merge.oh_done, 1)

            def denominators(n):
                act.wait_ge(den_mm, n + 1)
                if n:
                    act.wait_ge(den_turned, n)
                act.copy(den[:], ps_d[:, 0, :]).then_inc(den_in, 1)

            def widen(n):
                act.wait_ge(inv_done, n + 1)
                if n:
                    act.wait_ge(inv_turned, n)
                act.activation(inv_w[:], inv_t[:].unsqueeze(3).to_broadcast([P, TT, HG, HD]), ACT.Copy).then_inc(inv_wide, 1)

            def inverse(n):
                act.wait_ge(inv_turned, n + 1)
                if n:
                    act.wait_ge(out_done, n)
                act.copy(inv[:], ps_d[:, 0, :]).then_inc(inv_in, 1)

            for j in range(HG):
                shift_copy(0, j)
            for n in range(STEPS):
                for t in range(TT):
                    for j in range(HG):
                        if n and j == 0:
                            act.wait_ge(pv_mm, 4 * (n - 1) + t + 1)
                            act.wait_ge(summed, 2 * (n - 1) + t // 2 + 1)
                        act.wait_ge(score_mm, 16 * n + 4 * t + j + 1)
                        act.activation(prob[:, t, j, :], ps_s[:, j % 2, :], ACT.Exp, scale=SCALE).then_inc(exp_done, 1)
                        if t == 3 and n + 1 < STEPS:
                            for head in ((), (), (0,), (1, 2, 3))[j]:
                                shift_copy(n + 1, head)
                        if n and (t, j) == (1, 2):
                            denominators(n - 1)
                        if n and (t, j) == (2, 1):
                            widen(n - 1)
                        if n and (t, j) == (3, 0):
                            inverse(n - 1)
                if n:
                    high(n - 1)
                if n == 1:
                    merge.scalar_2_hi(act)
            denominators(STEPS - 1)
            widen(STEPS - 1)
            inverse(STEPS - 1)
            high(STEPS - 1)

        @block.vector
        def _(dve):
            dve.memset(ones[:], 1.0).then_inc(zeroed, 1)
            dve.memset(fp(nmax_w[:]), 0.0).then_inc(zeroed, 1)

            def maxima(n, first, count):
                for k in range(first, first + count):
                    dve.wait_ge(max_mm, 16 * n + k + 1)
                    dve.tensor_reduce(tile_max[:, k % TT, k // TT:k // TT + 1], ps_m[:, k % 2, :], AX_X, ALU.max,
                                      negate=True).then_inc(max_read, 1)

            def shift(n):
                dve.wait_ge(max_read, 16 * n + 16)
                if n:
                    dve.wait_ge(shift_mm, n)
                else:
                    dve.wait_ge(zeroed, 2)
                dve.tensor_copy(nmax_w[:, :, STACK:ROWS], tile_max[:]).then_inc(wide, 1)

            def inverse(n):
                dve.wait_ge(den_turned, n + 1)
                if n:
                    dve.wait_ge(inv_wide, n)
                dve.reciprocal(inv_t[:], ps_x[:, 0, :].rearrange("p (t j r) -> p t j r", t=TT, j=HG)[:, :, :, 0]
                               ).then_inc(inv_done, 1)

            def finish(n):
                dve.wait_ge(inv_in, n + 1)
                if n >= 2:
                    dve.wait_ge(merge.ol_done, n - 1)
                dve.wait_ge(pv_mm, 4 * n + 4)
                dve.tensor_tensor(out[:, n % 2, :], ps_o[:, n % 2, :], inv[:], ALU.mult).then_inc(out_done, 1)

            maxima(0, 0, 16)
            shift(0)
            for n in range(STEPS):
                last = n + 1 == STEPS
                if not last:
                    maxima(n + 1, 0, 12)
                if n:
                    inverse(n - 1)
                if not last:
                    maxima(n + 1, 12, 4)
                    shift(n + 1)
                if n:
                    finish(n - 1)
                if n == 2:
                    merge.vector_3_lo(dve)
            inverse(STEPS - 1)
            finish(STEPS - 1)

        @block.tensor
        def _(pe):
            def max_scores(n, k):
                s, j, t = n % SLOTS, k // TT, k % TT
                if 16 * n + k >= 2:
                    pe.wait_ge(max_read, 16 * n + k - 1)
                pe.matmul(ps_m[:, k % 2, :], qst[0:STACK, s, j, t * P:(t + 1) * P], kst[0:STACK, s, j, :],
                          start=True, stop=True).then_inc(max_mm, 1)

            def shift_rows(n):
                pe.wait_ge(wide, n + 1)
                if n >= 2:
                    pe.wait_ge(inv_done, n - 1)
                for t in range(TT):
                    mm = pe.matmul(ps_x[:, 0, t * P:(t + 1) * P], nmax_w[:, t, :], idr[:], start=True, stop=True)
                mm.then_inc(shift_mm, 1)

            def turn_denominators(n):
                pe.wait_ge(den_in, n + 1)
                for t in range(TT):
                    mm = pe.transpose(ps_x[:, 0, t * P:(t + 1) * P], den[:, t * P:(t + 1) * P], idn[:])
                mm.then_inc(den_turned, 1)

            def turn_inverse(n):
                pe.wait_ge(inv_wide, n + 1)
                for t in range(TT):
                    mm = pe.transpose(ps_d[:, 0, t * P:(t + 1) * P], inv_w[:, t].rearrange("p j r -> p (j r)"), idn[:])
                mm.then_inc(inv_turned, 1)

            def values(n, t):
                pe.wait_ge(exp_done, 16 * n + 4 * t + 4)
                for j in range(HG):
                    c = ((n % G) * HG + j) * HD
                    mm = pe.matmul(ps_o[j * HD:(j + 1) * HD, n % 2, :], val[:, n // G, t, c:c + HD], prob[:, t, j, :],
                                   start=(t == 0), stop=(t == TT - 1))
                mm.then_inc(pv_mm, 1)

            def denominators(n):
                pe.wait_ge(summed, 2 * n + 2)
                if n:
                    pe.wait_ge(inv_in, n)
                for k in range(2):
                    for j in range(HG):
                        mm = pe.matmul(ps_d[j * HD:(j + 1) * HD, 0, :], ones[:], pair[:, k, j, :], start=(k == 0), stop=(k == 1))
                mm.then_inc(den_mm, 1)

            def scores(n, t, j):
                if 16 * n + 4 * t + j >= 2:
                    pe.wait_ge(exp_done, 16 * n + 4 * t + j - 1)
                pe.matmul(ps_s[:, j % 2, :], kst[0:ROWS, n % SLOTS, j, t * P:(t + 1) * P], qst[0:ROWS, n % SLOTS, j, :],
                          start=True, stop=True).then_inc(score_mm, 1)

            pe.wait_ge(stack_in[0], 96)
            for k in range(16):
                max_scores(0, k)
            pe.wait_ge(zeroed, 2)
            pe.wait_ge(consts, 1 + SLOTS)
            shift_rows(0)
            pe.wait_ge(v_in_sem, 16 * B)
            for n in range(STEPS):
                last = n + 1 == STEPS
                peak = lambda k: None if last else max_scores(n + 1, k)
                if not last:
                    pe.wait_ge(stack_in[(n + 1) % 2], 96 * ((n + 1) // 2 + 1))
                peak(0)
                peak(1)
                peak(2)
                for j in range(HG):
                    pe.wait_ge(shift_in, HG * n + j + 1)
                    scores(n, 0, j)
                    if n and j == 0:
                        values(n - 1, 3)
                    peak(3 + j)
                scores(n, 1, 0)
                peak(7)
                scores(n, 1, 1)
                if n:
                    denominators(n - 1)
                peak(8)
                scores(n, 1, 2)
                peak(9)
                scores(n, 1, 3)
                if n >= 2:
                    pe.wait_ge(out_done, n - 1)
                values(n, 0)
                if n:
                    turn_denominators(n - 1)
                peak(10)
                scores(n, 2, 0)
                scores(n, 2, 1)
                peak(11)
                values(n, 1)
                peak(12)
                scores(n, 2, 2)
                peak(13)
                scores(n, 2, 3)
                if n:
                    turn_inverse(n - 1)
                peak(14)
                scores(n, 3, 0)
                peak(15)
                scores(n, 3, 1)
                values(n, 2)
                scores(n, 3, 2)
                if not last:
                    shift_rows(n + 1)
                scores(n, 3, 3)
            values(STEPS - 1, 3)
            denominators(STEPS - 1)
            turn_denominators(STEPS - 1)
            turn_inverse(STEPS - 1)


def experts(nc, merge, ident, router_w, router_b, index, expert_w, expert_b, out):
    BANKS = 4
    with ExitStack() as ctx:
        sb = lambda name, shape, dt=F32: ctx.enter_context(nc.sbuf_tensor(name, shape, dt))
        sem = lambda name: ctx.enter_context(nc.semaphore(name))
        idn = sb("e_id", [P, P])
        ps_y = ctx.enter_context(nc.psum_tensor("e_ps_y", [P, BANKS, 512], F32))
        ps_r = ctx.enter_context(nc.psum_tensor("e_ps_router", [P, 512], F32))
        ps_c = ctx.enter_context(nc.psum_tensor("e_ps_coef", [P, 512], F32))
        norm = Norm(nc, ctx, "en", merge.y, idn)
        rw, rwh, rwl = sb("e_rw", [P, DT, E]), sb("e_rwh", [P, DT, E], F32R), sb("e_rwl", [P, DT, E], F32R)
        rb, idx8, eb = sb("e_rb", [P, NT, E]), sb("e_idx", [P, NT, E]), sb("e_eb", [E, D])
        logit, top = sb("e_logit", [P, NT, E]), sb("e_top", [P, NT])
        ex, total, gate = sb("e_ex", [P, NT, E]), sb("e_total", [P, NT]), sb("e_gate", [P, NT])
        pick, first, coef = sb("e_pick", [P, NT, E]), sb("e_first", [P, NT]), sb("e_coef", [P, NT, E])
        coef_t = sb("e_coef_t", [E, B * T])
        raw = sb("e_raw", [P, DT, D])
        wh, wl = sb("e_wh", [P, 2, DT, D], F32R), sb("e_wl", [P, 2, DT, D], F32R)
        c_in, raw_in = sem("e_c_in"), sem("e_raw_in")
        rwh_done, rwl_done, chain, router_mm, ex_done = sem("e_rwh_done"), sem("e_rwl_done"), sem("e_chain"), sem("e_router_mm"), sem("e_ex_done")
        coef_done, coef_mm, coef_in = sem("e_coef_done"), sem("e_coef_mm"), sem("e_coef_in")
        wh_done, wl_done, y_mm, y_read = sem("e_wh2_done"), sem("e_wl2_done"), sem("e_y_mm"), sem("e_y_read")
        sent = sem("e_sent")
        block = ctx.enter_context(nc.Block())

        @block.sync
        def _(sp):
            sp.dma_start(raw[:], expert_w[0]).then_inc(raw_in, 16)
            sp.dma_start(idn[:], ident).then_inc(c_in, 16)
            sp.dma_start(rw[:], router_w).then_inc(c_in, 16)
            sp.dma_start(rb[:], router_b.partition_broadcast(P)).then_inc(c_in, 16)
            sp.dma_start(idx8[:], index.partition_broadcast(P)).then_inc(c_in, 16)
            sp.dma_start(eb[:], expert_b).then_inc(c_in, 16)
            with sp.Fori(1, E) as e:
                sp.wait_ge(wl_done, e)
                sp.dma_start(raw[:], expert_w[bass.ds(e, 1)].rearrange("o p d n -> (o p) d n")).then_inc(raw_in, 16)
            for i in range(NT):
                sp.wait_ge(y_read, NT * E + i + 1)
                sp.dma_start(out[i // TT, (i % TT) * P:(i % TT + 1) * P], merge.y[:, i, :]).then_inc(sent, 16)
            sp.wait_ge(sent, 16 * NT)

        @block.scalar
        def _(act):
            act.wait_ge(c_in, 80)
            act.activation(rwh[:], rw[:], ACT.Copy).then_inc(rwh_done, 1)

            def weights(e, slot, free=None):
                act.wait_ge(raw_in, 16 * e + 16)
                if free is not None:
                    act.wait_ge(y_mm, free)
                act.activation(wh[:, slot], raw[:], ACT.Copy).then_inc(wh_done, 1)

            weights(0, 0)
            for b in range(B):
                norm.scalar_3_root(act, b)
                norm.scalar_6_hi(act, b)
            act.wait_ge(chain, 3)
            act.activation(ex[:], pick[:], ACT.Exp).then_inc(ex_done, 1)
            act.wait_ge(coef_mm, 1)
            act.copy(coef_t[:, 0:T], ps_c[0:E, :]).then_inc(coef_in, 1)
            act.wait_ge(coef_mm, 2)
            act.copy(coef_t[:, T:2 * T], ps_c[0:E, :]).then_inc(coef_in, 1)
            weights(1, 1)
            with act.Fori(0, E // 2 - 1) as h:
                for slot in range(2):
                    weights(2 * h + 2 + slot, slot, NT * (2 * h + 2 + slot))

        @block.vector
        def _(dve):
            dve.wait_ge(rwh_done, 1)
            dve.tensor_tensor(rwl[:], rw[:], fp(rwh[:]), ALU.subtract).then_inc(rwl_done, 1)
            def weights(e, slot):
                dve.wait_ge(wh_done, e + 1)
                dve.tensor_tensor(wl[:, slot], raw[:], fp(wh[:, slot]), ALU.subtract).then_inc(wl_done, 1)

            steps = [0]

            def link(ins):
                steps[0] += 1
                ins.then_inc(chain, 1)
                dve.wait_ge(chain, steps[0])

            for i in range(NT):
                merge.vector_5_add(dve, ps_y, i)
                norm.vector_1_stats(dve, i)
                if i % TT == TT - 1:
                    norm.vector_2_variance(dve, i // TT)
                    norm.vector_4_apply(dve, i // TT)
                if i == 1:
                    weights(0, 0)
                if i == TT + 1:
                    norm.vector_7_lo(dve, 0)
            norm.vector_7_lo(dve, 1)
            wide = lambda small: small[:].unsqueeze(2).to_broadcast([P, NT, E])
            dve.wait_ge(router_mm, 1)
            link(dve.tensor_tensor(logit[:], ps_r[:, 0:NT * E].rearrange("p (n e) -> p n e", n=NT), rb[:], ALU.add))
            link(dve.tensor_reduce(top[:], logit[:], AX_X, ALU.max))
            link(dve.tensor_tensor(pick[:], logit[:], wide(top), ALU.subtract))
            dve.wait_ge(ex_done, 1)
            link(dve.tensor_reduce(total[:], ex[:], AX_X, ALU.add))
            link(dve.reciprocal(gate[:], total[:]))
            link(dve.tensor_scalar(logit[:], pick[:], 0.0, -float(E), ALU.is_ge, ALU.mult))
            link(dve.tensor_tensor(pick[:], logit[:], idx8[:], ALU.add))
            link(dve.tensor_reduce(first[:], pick[:], AX_X, ALU.min))
            link(dve.tensor_tensor(logit[:], pick[:], wide(first), ALU.is_equal))
            dve.tensor_tensor(coef[:], logit[:], wide(gate), ALU.mult).then_inc(coef_done, 1)

            def add(e, i):
                dve.wait_ge(y_mm, (e + 1) * NT + i + 1)
                dve.wait_ge(y_read, e * NT + i + 1)
                dve.scalar_tensor_tensor(merge.y[:, i, :], ps_y[:, i % BANKS, :], coef[:, i, bass.ds(e, 1)], merge.y[:, i, :],
                                         ALU.mult, ALU.add).then_inc(y_read, 1)

            dve.wait_ge(coef_done, 1)
            for i in range(NT):
                dve.wait_ge(y_mm, i + 1)
                dve.scalar_tensor_tensor(merge.y[:, i, :], ps_y[:, i % BANKS, :], coef[:, i, 0:1], merge.y[:, i, :],
                                         ALU.mult, ALU.add).then_inc(y_read, 1)
            for i in range(NT):
                dve.wait_ge(y_mm, NT + i + 1)
                dve.wait_ge(y_read, i + 1)
                dve.tensor_tensor(merge.y[:, i, :], ps_y[:, i % BANKS, :], merge.y[:, i, :], ALU.add).then_inc(y_read, 1)
                if i == 0:
                    weights(1, 1)
            with dve.Fori(0, E // 2 - 1) as h:
                for slot in range(2):
                    e = 2 * h + 1 + slot
                    add(e, 0)
                    weights(e + 1, slot)
                    for i in range(1, NT):
                        add(e, i)
            for i in range(NT):
                add(E - 1, i)

        @block.tensor
        def _(pe):
            merge.tensor_4_product(pe, ps_y, range(TT + 2))
            pe.wait_ge(c_in, 80)
            norm.tensor_5_turn(pe, 0)
            merge.tensor_4_product(pe, ps_y, range(TT + 2, NT))

            def route(b):
                pe.wait_ge(rwl_done, 1)
                pe.wait_ge(norm.lo_done, DT * (b + 1))
                for i in range(TT * b, TT * (b + 1)):
                    mm = exact_product(pe, ps_r[:, i * E:(i + 1) * E], lambda part, d: (norm.hi, norm.lo)[part][:, d, i * P:(i + 1) * P],
                                       lambda part, d: (rwh, rwl)[part][:, d, :])
                return mm

            def apply(slot, i):
                exact_product(pe, ps_y[:, i % BANKS, :], lambda part, d: (norm.hi, norm.lo)[part][:, d, i * P:(i + 1) * P],
                              lambda part, d: (wh, wl)[part][:, slot, d, :]).then_inc(y_mm, 1)

            route(0)
            pe.wait_ge(wl_done, 1)
            pe.wait_ge(merge.y_done, NT)
            apply(0, 0)
            apply(0, 1)
            norm.tensor_5_turn(pe, 1)
            route(1).then_inc(router_mm, 1)
            apply(0, 2)
            apply(0, 3)
            pe.wait_ge(coef_done, 1)
            for b in range(B):
                if b:
                    pe.wait_ge(coef_in, b)
                for t in range(TT):
                    mm = pe.transpose(ps_c[0:E, t * P:(t + 1) * P], coef[:, b * TT + t, :], idn[:])
                mm.then_inc(coef_mm, 1)
            for i in range(BANKS, NT):
                pe.wait_ge(y_read, i - BANKS + 1)
                apply(0, i)
            pe.wait_ge(coef_in, B)
            for i in range(NT):
                pe.wait_ge(y_read, NT + i - BANKS + 1)
                pe.matmul(ps_y[:, i % BANKS, :], coef_t[:, i * P:(i + 1) * P], eb[:], start=True, stop=True).then_inc(y_mm, 1)

            def expert(e, slot):
                pe.wait_ge(wl_done, e + 1)
                for i in range(NT):
                    pe.wait_ge(y_read, e * NT + (NT + i - BANKS + 1))
                    apply(slot, i)

            expert(1, 1)
            with pe.Fori(0, E // 2 - 1) as h:
                for slot in range(2):
                    expert(2 * h + 2 + slot, slot)


def perceiver_block(nc, a, out):
    scratch = lambda name, shape: nc.dram_tensor(name, shape, F32, kind="Internal").ap()
    q_split = scratch("q_split", [B, 2, G, P, T])
    crossed = scratch("crossed", [B, P, G, T])
    x1, v_self = scratch("x1", [B, T, D]), scratch("v_self", [B, P, TT, D])
    qk_split = scratch("qk_split", [B, 2, 2, G, HG, HD, T])
    with ExitStack() as ctx:
        proj = Projection(nc, ctx)
        project_queries(nc, proj, a["x"], a["x_wq"], a["x_bq"], a["ident"], a["x_wk"], a["x_wv"], a["ctx_t"], q_split)
        cross_attention(nc, proj, a["ctx_t"], a["x_bk"], a["x_bv"], a["ident"], a["onehot"], q_split,
                        crossed, a["ctx_t"].shape[0] // B)
    project_self(nc, a["x"], crossed, a["x_wo"], a["x_bo"], a["w_qkv"], a["cos"], a["sin"], a["ident"], x1, qk_split, v_self)
    with ExitStack() as ctx:
        merge = Merge(nc, ctx, "em")
        self_attention(nc, merge, x1, a["s_wu"], a["s_bu"], qk_split, v_self, a["ident"], a["onehot"])
        experts(nc, merge, a["ident"], a["router_w"], a["router_b"], a["index"], a["expert_w"], a["expert_b"], out)


def kernel(**inputs):
    import numpy as np
    import concourse.bacc as bacc
    from concourse.bass_utils import run_bass_kernel_spmd

    x = {k: np.asarray(v) for k, v in inputs.items()}
    tiles = lambda w: np.ascontiguousarray(w.reshape(DT, P, -1).transpose(1, 0, 2))
    column = lambda v: np.ascontiguousarray(v.reshape(DT, P).T)
    row = lambda v: np.ascontiguousarray(v.reshape(1, -1))
    halves = lambda w: np.concatenate([w[0::2], w[1::2]])
    ctx = x["ctx_1024"]
    chunks = ctx.shape[1] // KC
    half = D // 2
    theta = np.float32(1.0) / np.float32(10000.0) ** (np.arange(half, dtype=np.float32) / np.float32(half))
    angle = np.arange(T, dtype=np.float32)[:, None] * theta[None, :]
    onehot = np.zeros((P - STACK, HG, T), np.float32)
    for j in range(HG):
        onehot[j, j] = 1.0
    turn = lambda v: np.ascontiguousarray(v.astype(np.float32).T.reshape(2, P, T).transpose(1, 0, 2))
    arrays = {
        "x": x["x"],
        "ctx_t": np.ascontiguousarray(ctx.reshape(B, chunks, KC, DT, P).transpose(0, 1, 4, 3, 2)).reshape(B * chunks, P, DT, KC),
        "x_wq": tiles(x["L0_xattn_Wq"].T), "x_bq": column(x["L0_xattn_bq"]),
        "x_wk": tiles(x["L0_xattn_Wk"].T), "x_bk": column(x["L0_xattn_bk"]),
        "x_wv": tiles(x["L0_xattn_Wv"].T), "x_bv": column(x["L0_xattn_bv"]),
        "x_wo": tiles(x["L0_xattn_Wo"].T), "x_bo": row(x["L0_xattn_bo"]),
        "w_qkv": np.stack([tiles(halves(x["L0_attn_Wq"]).T), tiles(halves(x["L0_attn_Wk"]).T), tiles(x["L0_attn_Wv"].T)]),
        "cos": turn(np.cos(angle)), "sin": turn(np.sin(angle)),
        "s_wu": tiles(x["L0_attn_Wu"].T), "s_bu": row(x["L0_attn_bu"]),
        "router_w": tiles(x["L0_ffn_router_w"]), "router_b": np.ascontiguousarray(np.tile(x["L0_ffn_router_b"], NT)).reshape(1, NT, E),
        "index": (np.arange(NT * E, dtype=np.float32) % E + E).reshape(1, NT, E).astype(np.float32),
        "expert_w": np.ascontiguousarray(x["L0_ffn_expert_w"].reshape(E, DT, P, D).transpose(0, 2, 1, 3)),
        "expert_b": x["L0_ffn_expert_b"],
        "ident": np.eye(P, dtype=np.float32), "onehot": onehot,
    }
    nc = bacc.Bacc("TRN2", target_bir_lowering=False, num_devices=1)
    ins, feed = {}, {}
    for name, a in arrays.items():
        feed[f"in_{name}"] = np.ascontiguousarray(a)
        ins[name] = nc.dram_tensor(f"in_{name}", a.shape, F32, kind="ExternalInput").ap()
    out = nc.dram_tensor("out", (B, T, D), F32, kind="ExternalOutput").ap()
    perceiver_block(nc, ins, out)
    r = run_bass_kernel_spmd(nc, [feed], core_ids=[0])
    return r.results[0]["out"]
```
